# Optimizing a Trainium2 kernel written in Bass

```python
import numpy as np
import jax
import jax.numpy as jnp

def _softmax(x, axis=-1):
    return jax.nn.softmax(x, axis=axis)

def _gelu(x):
    return jax.nn.gelu(x, approximate=True)

def _silu(x):
    return jax.nn.silu(x)

def _sigmoid(x):
    return jax.nn.sigmoid(x)

def _layernorm(x, axis=-1, eps=1e-05):
    m = jnp.mean(x, axis=axis, keepdims=True)
    v = jnp.var(x, axis=axis, keepdims=True)
    return (x - m) / jnp.sqrt(v + eps)

def _scatter_add(tgt, idx, src, axis=0):
    return tgt.at[idx].add(src)

def _segment_sum(src, seg, n):
    return jax.ops.segment_sum(src, seg, n)
kernel_name = 'mk_vit_tower_d1_tok_img1024_r4_24adf9'

def setup_inputs(seed: int=0):
    np.random.seed(seed)
    _w = jnp.asarray

    def _rec_inputs():
        import jax
        import jax.numpy as jnp
        _rk = jax.random.key(seed)
        x = -0.00016672 + 0.999947 * jax.random.normal(jax.random.fold_in(_rk, 1), (64, 3, 96, 96), jnp.float32)
        return x
    x = _rec_inputs()

    def _L0_tok_setup():
        import jax, jax.numpy as jnp
        import numpy as np
        DIM = 256
        IMG = 96
        P = 16
        C = 3
        TEMP = 10000.0
        EPS = 1e-05
        PATCH_DIM = C * P * P
        HP = IMG // P

        def layernorm(x, gamma, beta):
            mu = jnp.mean(x, axis=-1, keepdims=True)
            var = jnp.var(x, axis=-1, keepdims=True)
            return (x - mu) * jax.lax.rsqrt(var + EPS) * gamma + beta

        def posemb_sincos_2d(h, w, dim, dtype):
            y, x = jnp.meshgrid(jnp.arange(h), jnp.arange(w), indexing='ij')
            omega = jnp.arange(dim // 4, dtype=jnp.float32) / (dim // 4 - 1)
            omega = 1.0 / TEMP ** omega
            y = y.reshape(-1)[:, None] * omega[None, :]
            x = x.reshape(-1)[:, None] * omega[None, :]
            pe = jnp.concatenate((jnp.sin(x), jnp.cos(x), jnp.sin(y), jnp.cos(y)), axis=1)
            return pe.astype(dtype)
        key = jax.random.key(seed)
        ks = jax.random.split(key, 8)
        B = 64
        img = jax.random.normal(ks[0], (B, C, IMG, IMG), dtype=jnp.float32)
        cls_token = jax.random.normal(ks[1], (1, 1, DIM), dtype=jnp.float32)
        cls_pos_embedding = jax.random.normal(ks[2], (1, 1, DIM), dtype=jnp.float32)
        ln1_g = jnp.ones((PATCH_DIM,), jnp.float32)
        ln1_b = jnp.zeros((PATCH_DIM,), jnp.float32)
        W = jax.random.normal(ks[3], (PATCH_DIM, DIM), dtype=jnp.float32) / np.sqrt(PATCH_DIM)
        bias = jnp.zeros((DIM,), jnp.float32)
        ln2_g = jnp.ones((DIM,), jnp.float32)
        ln2_b = jnp.zeros((DIM,), jnp.float32)
        return {'img': img, 'cls_token': cls_token, 'cls_pos_embedding': cls_pos_embedding, 'ln1_g': ln1_g, 'ln1_b': ln1_b, 'W': W, 'bias': bias, 'ln2_g': ln2_g, 'ln2_b': ln2_b}
    _L0_tok_all = _L0_tok_setup()
    _L0_tok_in = {k: v for k, v in _L0_tok_all.items() if k in ('cls_token', 'cls_pos_embedding', 'ln1_g', 'ln1_b', 'W', 'bias', 'ln2_g', 'ln2_b')}
    del _L0_tok_all

    def _L0_attn_setup():
        import jax, jax.numpy as jnp
        import numpy as np
        DIM = 256
        HEADS = 16
        DIM_HEAD = 64
        DIM_INNER = HEADS * DIM_HEAD

        def rms_norm(x, gamma):
            eps = 1e-12
            norm = jnp.maximum(jnp.linalg.norm(x, axis=-1, keepdims=True), eps)
            return x / norm * x.shape[-1] ** 0.5 * (gamma + 1.0)
        key = jax.random.key(seed)
        k1, k2, k3 = jax.random.split(key, 3)
        x = jax.random.normal(k1, (2, 512, DIM), dtype=jnp.float32)
        gamma = jnp.zeros((DIM,), dtype=jnp.float32)
        w_qkv = jax.random.normal(k2, (DIM, DIM_INNER * 3), dtype=jnp.float32) * DIM ** (-0.5)
        w_out = jax.random.normal(k3, (DIM_INNER, DIM), dtype=jnp.float32) * DIM_INNER ** (-0.5)
        return {'x': x, 'gamma': gamma, 'w_qkv': w_qkv, 'w_out': w_out}
    _L0_attn_all = _L0_attn_setup()
    _L0_attn_in = {k: v for k, v in _L0_attn_all.items() if k in ('gamma', 'w_qkv', 'w_out')}
    del _L0_attn_all

    def _L0_ffn_setup():
        import jax, jax.numpy as jnp
        import numpy as np
        DIM = 256
        E = 16
        TOPK = 2
        G = 4
        TOPK_G = 2
        INTER = 128
        N_SHARED = 2
        ROUTE_SCALE = 1.0

        def _gate(xf, gate_w, gate_b):
            scores = xf @ gate_w.T
            scores = jax.nn.softmax(scores.astype(jnp.float32), axis=-1)
            orig = scores
            scores = scores + gate_b
            T = xf.shape[0]
            sg = scores.reshape(T, G, E // G)
            group_scores = jax.lax.top_k(sg, 2)[0].sum(-1)
            _, gidx = jax.lax.top_k(group_scores, TOPK_G)
            keep = jax.nn.one_hot(gidx, G).sum(axis=1) > 0
            sg = jnp.where(keep[:, :, None], sg, -jnp.inf)
            scores = sg.reshape(T, E)
            _, idx = jax.lax.top_k(scores, TOPK)
            weights = jnp.take_along_axis(orig, idx, axis=1)
            weights = (weights * ROUTE_SCALE).astype(xf.dtype)
            return (weights, idx)
        key = jax.random.key(seed)
        ks = jax.random.split(key, 16)
        s = lambda fan_in: 1.0 / np.sqrt(fan_in)
        inp = {'x': jax.random.normal(ks[0], (4, 256, DIM), dtype=jnp.float32), 'gate_w': jax.random.normal(ks[1], (E, DIM), dtype=jnp.float32) * s(DIM), 'gate_b': jnp.zeros((E,), dtype=jnp.float32), 'We1': jax.random.normal(ks[2], (E, DIM, INTER), dtype=jnp.float32) * s(DIM), 'be1': jnp.zeros((E, INTER), dtype=jnp.float32), 'We2': jax.random.normal(ks[3], (E, INTER, DIM), dtype=jnp.float32) * s(INTER), 'be2': jnp.zeros((E, DIM), dtype=jnp.float32), 'We3': jax.random.normal(ks[4], (E, DIM, INTER), dtype=jnp.float32) * s(DIM), 'be3': jnp.zeros((E, INTER), dtype=jnp.float32), 'ws1': jax.random.normal(ks[5], (DIM, N_SHARED * INTER), dtype=jnp.float32) * s(DIM), 'bs1': jnp.zeros((N_SHARED * INTER,), dtype=jnp.float32), 'ws2': jax.random.normal(ks[6], (N_SHARED * INTER, DIM), dtype=jnp.float32) * s(N_SHARED * INTER), 'bs2': jnp.zeros((DIM,), dtype=jnp.float32), 'ws3': jax.random.normal(ks[7], (DIM, N_SHARED * INTER), dtype=jnp.float32) * s(DIM), 'bs3': jnp.zeros((N_SHARED * INTER,), dtype=jnp.float32)}
        return inp
    _L0_ffn_all = _L0_ffn_setup()
    _L0_ffn_in = {k: v for k, v in _L0_ffn_all.items() if k in ('gate_w', 'gate_b', 'We1', 'be1', 'We2', 'be2', 'We3', 'be3', 'ws1', 'bs1', 'ws2', 'bs2', 'ws3', 'bs3')}
    del _L0_ffn_all
    return {'x': x, 'L0_tok_cls_token': _L0_tok_in['cls_token'], 'L0_tok_cls_pos_embedding': _L0_tok_in['cls_pos_embedding'], 'L0_tok_ln1_g': _L0_tok_in['ln1_g'], 'L0_tok_ln1_b': _L0_tok_in['ln1_b'], 'L0_tok_W': _L0_tok_in['W'], 'L0_tok_bias': _L0_tok_in['bias'], 'L0_tok_ln2_g': _L0_tok_in['ln2_g'], 'L0_tok_ln2_b': _L0_tok_in['ln2_b'], 'L0_attn_gamma': _L0_attn_in['gamma'], 'L0_attn_w_qkv': _L0_attn_in['w_qkv'], 'L0_attn_w_out': _L0_attn_in['w_out'], 'L0_ffn_gate_w': _L0_ffn_in['gate_w'], 'L0_ffn_gate_b': _L0_ffn_in['gate_b'], 'L0_ffn_We1': _L0_ffn_in['We1'], 'L0_ffn_be1': _L0_ffn_in['be1'], 'L0_ffn_We2': _L0_ffn_in['We2'], 'L0_ffn_be2': _L0_ffn_in['be2'], 'L0_ffn_We3': _L0_ffn_in['We3'], 'L0_ffn_be3': _L0_ffn_in['be3'], 'L0_ffn_ws1': _L0_ffn_in['ws1'], 'L0_ffn_bs1': _L0_ffn_in['bs1'], 'L0_ffn_ws2': _L0_ffn_in['ws2'], 'L0_ffn_bs2': _L0_ffn_in['bs2'], 'L0_ffn_ws3': _L0_ffn_in['ws3'], 'L0_ffn_bs3': _L0_ffn_in['bs3']}

def reference(x, L0_tok_cls_token, L0_tok_cls_pos_embedding, L0_tok_ln1_g, L0_tok_ln1_b, L0_tok_W, L0_tok_bias, L0_tok_ln2_g, L0_tok_ln2_b, L0_attn_gamma, L0_attn_w_qkv, L0_attn_w_out, L0_ffn_gate_w, L0_ffn_gate_b, L0_ffn_We1, L0_ffn_be1, L0_ffn_We2, L0_ffn_be2, L0_ffn_We3, L0_ffn_be3, L0_ffn_ws1, L0_ffn_bs1, L0_ffn_ws2, L0_ffn_bs2, L0_ffn_ws3, L0_ffn_bs3):
    import jax
    import jax.numpy as jnp

    def _L0_tok_ref(img, cls_token, cls_pos_embedding, ln1_g, ln1_b, W, bias, ln2_g, ln2_b):
        import jax, jax.numpy as jnp
        import numpy as np
        DIM = 256
        IMG = 96
        P = 16
        C = 3
        TEMP = 10000.0
        EPS = 1e-05
        PATCH_DIM = C * P * P
        HP = IMG // P

        def layernorm(x, gamma, beta):
            mu = jnp.mean(x, axis=-1, keepdims=True)
            var = jnp.var(x, axis=-1, keepdims=True)
            return (x - mu) * jax.lax.rsqrt(var + EPS) * gamma + beta

        def posemb_sincos_2d(h, w, dim, dtype):
            y, x = jnp.meshgrid(jnp.arange(h), jnp.arange(w), indexing='ij')
            omega = jnp.arange(dim // 4, dtype=jnp.float32) / (dim // 4 - 1)
            omega = 1.0 / TEMP ** omega
            y = y.reshape(-1)[:, None] * omega[None, :]
            x = x.reshape(-1)[:, None] * omega[None, :]
            pe = jnp.concatenate((jnp.sin(x), jnp.cos(x), jnp.sin(y), jnp.cos(y)), axis=1)
            return pe.astype(dtype)
        b = img.shape[0]
        x = img.reshape(b, C, HP, P, HP, P)
        x = jnp.transpose(x, (0, 2, 4, 3, 5, 1))
        x = x.reshape(b, HP, HP, PATCH_DIM)
        x = layernorm(x, ln1_g, ln1_b)
        x = jnp.einsum('bhwp,pd->bhwd', x, W) + bias
        x = layernorm(x, ln2_g, ln2_b)
        pe = posemb_sincos_2d(HP, HP, DIM, x.dtype)
        x = x.reshape(b, HP * HP, DIM) + pe[None]
        cls_tokens = jnp.broadcast_to(cls_token + cls_pos_embedding, (b, 1, DIM))
        return jnp.concatenate((cls_tokens, x), axis=1)

    def _L0_attn_ref(x, gamma, w_qkv, w_out):
        import jax, jax.numpy as jnp
        import numpy as np
        DIM = 256
        HEADS = 16
        DIM_HEAD = 64
        DIM_INNER = HEADS * DIM_HEAD

        def rms_norm(x, gamma):
            eps = 1e-12
            norm = jnp.maximum(jnp.linalg.norm(x, axis=-1, keepdims=True), eps)
            return x / norm * x.shape[-1] ** 0.5 * (gamma + 1.0)
        b, n, _ = x.shape
        scale = DIM_HEAD ** (-0.5)
        xn = rms_norm(x, gamma)
        qkv = xn @ w_qkv
        qkv = qkv.reshape(b, n, 3, HEADS, DIM_HEAD)
        qkv = jnp.transpose(qkv, (2, 0, 3, 1, 4))
        q, k, v = (qkv[0], qkv[1], qkv[2])
        q = q * scale
        sim = jnp.einsum('bhid,bhjd->bhij', q, k)
        attn = jax.nn.softmax(sim, axis=-1)
        out = jnp.einsum('bhij,bhjd->bhid', attn, v)
        out = jnp.transpose(out, (0, 2, 1, 3)).reshape(b, n, DIM_INNER)
        return out @ w_out

    def _L0_ffn_ref(x, gate_w, gate_b, We1, be1, We2, be2, We3, be3, ws1, bs1, ws2, bs2, ws3, bs3):
        import jax, jax.numpy as jnp
        import numpy as np
        DIM = 256
        E = 16
        TOPK = 2
        G = 4
        TOPK_G = 2
        INTER = 128
        N_SHARED = 2
        ROUTE_SCALE = 1.0

        def _gate(xf, gate_w, gate_b):
            scores = xf @ gate_w.T
            scores = jax.nn.softmax(scores.astype(jnp.float32), axis=-1)
            orig = scores
            scores = scores + gate_b
            T = xf.shape[0]
            sg = scores.reshape(T, G, E // G)
            group_scores = jax.lax.top_k(sg, 2)[0].sum(-1)
            _, gidx = jax.lax.top_k(group_scores, TOPK_G)
            keep = jax.nn.one_hot(gidx, G).sum(axis=1) > 0
            sg = jnp.where(keep[:, :, None], sg, -jnp.inf)
            scores = sg.reshape(T, E)
            _, idx = jax.lax.top_k(scores, TOPK)
            weights = jnp.take_along_axis(orig, idx, axis=1)
            weights = (weights * ROUTE_SCALE).astype(xf.dtype)
            return (weights, idx)
        shape = x.shape
        xf = x.reshape(-1, DIM)
        weights, idx = _gate(xf, gate_w, gate_b)
        combine = (jax.nn.one_hot(idx, E, dtype=xf.dtype) * weights[..., None]).sum(1)
        h1 = jnp.einsum('td,edi->tei', xf, We1) + be1
        h3 = jnp.einsum('td,edi->tei', xf, We3) + be3
        h = jax.nn.silu(h1) * h3
        yo = jnp.einsum('tei,eid->ted', h, We2) + be2
        y = jnp.einsum('te,ted->td', combine, yo)
        z = jax.nn.silu(xf @ ws1 + bs1) * (xf @ ws3 + bs3) @ ws2 + bs2
        return (y + z).reshape(shape)
    h = _L0_tok_ref(x, L0_tok_cls_token, L0_tok_cls_pos_embedding, L0_tok_ln1_g, L0_tok_ln1_b, L0_tok_W, L0_tok_bias, L0_tok_ln2_g, L0_tok_ln2_b)
    h = h + _L0_attn_ref(_layernorm(h, axis=-1), L0_attn_gamma, L0_attn_w_qkv, L0_attn_w_out)
    h = h + _L0_ffn_ref(_layernorm(h, axis=-1), L0_ffn_gate_w, L0_ffn_gate_b, L0_ffn_We1, L0_ffn_be1, L0_ffn_We2, L0_ffn_be2, L0_ffn_We3, L0_ffn_be3, L0_ffn_ws1, L0_ffn_bs1, L0_ffn_ws2, L0_ffn_bs2, L0_ffn_ws3, L0_ffn_bs3)
    return h

_drawn_inputs = setup_inputs


def setup_inputs(seed=0):
    import zlib

    import numpy as np

    out = dict(_drawn_inputs(seed))
    spreads = {'L0_tok_ln1_g': (1.0, 0.2),
     'L0_tok_ln1_b': (0.0, 0.1),
     'L0_tok_bias': (0.0, 0.1),
     'L0_tok_ln2_g': (1.0, 0.2),
     'L0_tok_ln2_b': (0.0, 0.1),
     'L0_attn_gamma': (0.0, 0.1),
     'L0_ffn_gate_b': (0.0, 0.1),
     'L0_ffn_be1': (0.0, 0.634),
     'L0_ffn_be2': (0.0, 0.389),
     'L0_ffn_be3': (0.0, 0.668),
     'L0_ffn_bs1': (0.0, 0.1),
     'L0_ffn_bs2': (0.0, 0.1),
     'L0_ffn_bs3': (0.0, 0.1)}
    factors = {}
    for name, (base, spread) in spreads.items():
        noise = np.random.default_rng([zlib.crc32(name.encode()), seed]).standard_normal(out[name].shape)
        drawn = base * np.exp(spread * noise) if base else spread * noise
        out[name] = jnp.asarray(drawn.astype(out[name].dtype))
    for name, factor in factors.items():
        out[name] = (out[name] * factor).astype(out[name].dtype)
    return out
```

```python
from contextlib import ExitStack

import numpy as np

import concourse.bass as bass
from concourse import mybir

F32 = mybir.dt.float32
F16 = mybir.dt.float16
ALU = mybir.AluOpType
ACT = mybir.ActivationFunctionType
AX = mybir.AxisListType

B, C, IMG, PATCH = 64, 3, 96, 16
HP = IMG // PATCH
NPATCH = HP * HP
SEQ = NPATCH + 1
D = 256
PD = C * PATCH * PATCH
HEADS, DH = 16, 64
DI = HEADS * DH
E, INTER = 16, 128
NE = E + 2
P = 128
KD = D // P
KP = PD // P
KI = DI // P
GI = 3
PR = GI * NPATCH
R = GI * SEQ
TILES = -(-B // GI)
LAST_B0 = B - GI
G = TILES // 2
N2 = 2 * R
UNITS = 8
HU = HEADS // 4
assert TILES == 2 * G and 3 * (TILES - 1) > LAST_B0

EPS = 1e-5
WS = 64.0
PS = 256.0
EXP_SCALE = DH ** -0.5 / (WS * WS)
OUT = 1e30
ROUTE_STEPS = 38
BIG = 32768.0


def constants():
    om = np.arange(D // 4, dtype=np.float32) / np.float32(D // 4 - 1)
    om = (np.float32(1.0) / np.power(np.float32(10000.0), om)).astype(np.float32)
    y, x = np.meshgrid(np.arange(HP), np.arange(HP), indexing="ij")
    y = (y.reshape(-1)[:, None] * om[None, :]).astype(np.float32)
    x = (x.reshape(-1)[:, None] * om[None, :]).astype(np.float32)
    pe = np.concatenate((np.sin(x), np.cos(x), np.sin(y), np.cos(y)), axis=1).astype(np.float32)
    rows = np.zeros((P, D), np.float32)
    rows[:PR] = np.tile(pe, (GI, 1))
    img = np.array([r // NPATCH if r < PR else r - PR for r in range(R)])
    own = (img[None, :] == np.arange(GI)[:, None]).astype(np.float32)
    ml = np.zeros((P, R), np.float16)
    mr = np.zeros((P, HU * R), np.float16)
    for base in (0, 64):
        ml[base:base + GI] = own * BIG
        mr[base:base + GI] = np.tile(-(1 - own) * BIG, (1, HU))
    small = np.zeros((P, 24), np.float32)
    small[:, 0] = np.arange(P) < PR
    small[:, 1:17] = np.arange(E) + E
    small[:, 17:21] = np.arange(3, -1, -1)
    return {"c_pe": rows, "c_ident": np.eye(P, dtype=np.float32), "c_maskl": ml, "c_maskr": mr, "c_small": small}


def lay_out(name, v):
    if name == "x":
        v = v.reshape(B, C, HP, PATCH, HP, PATCH).transpose(0, 2, 4, 3, 5, 1).reshape(B * NPATCH, PD)
    elif name in ("L0_tok_ln1_g", "L0_tok_ln1_b", "L0_attn_gamma", "L0_ffn_bs1", "L0_ffn_bs3"):
        v = v.reshape(-1, P).T
    elif name in ("L0_ffn_gate_w", "L0_ffn_be1", "L0_ffn_be3"):
        v = v.T
    return np.ascontiguousarray(v)


def done(per, g, k):
    return per * g + (k + 1)


def build(nc, a, out):
    x = a["x"]
    ctx = ExitStack()
    with ctx:
        def sb(name, shape, dt=F32):
            return ctx.enter_context(nc.sbuf_tensor(name, shape, dt))

        def bank(name, shape, dt=F32):
            return ctx.enter_context(nc.psum_tensor(name, shape, dt))

        def sem(name):
            return ctx.enter_context(nc.semaphore(name))

        wtok = sb("wtok", [P, 2, KP, D], F16)
        wqkv = sb("wqkv", [P, 2, KD, 3 * DI], F16)
        wout = sb("wout", [P, 2, KI, D], F16)
        w13 = sb("w13", [P, 2, NE, KD, 2 * INTER], F16)
        w2 = sb("w2", [P, 2, NE, D], F16)
        wgate = sb("wgate", [P, 2, KD, E], F16)

        ident = sb("ident", [P, P])
        maskl = sb("maskl", [P, R], F16)
        maskr = sb("maskr", [P, HU * R], F16)
        small = sb("small", [P, 24])
        addrow = sb("addrow", [P, D])
        g2row = sb("g2row", [P, D])
        biasrow = sb("biasrow", [P, D])
        g1col = sb("g1col", [P, KP])
        b1col = sb("b1col", [P, KP])
        gamcol = sb("gamcol", [P, KD])
        gatest = sb("gatest", [P, KD, E])
        gbrow = sb("gbrow", [P, E])
        b13col = sb("b13col", [P, 2, NE])
        be2row = sb("be2row", [NE, D])
        power = sb("power", [P, 5])
        scrap = sb("scrap", [P, 2])

        hrows = sb("hrows", [P, TILES, D])
        xft = sb("xft", [P, 2, KD, TILES * R], F16)
        logits = sb("logits", [P, TILES, E])
        stage = hrows[:, :, :].rearrange("p t d -> p (t d)")

        xin = sb("xin", [P, 2, PD])
        xt = sb("xt", [P, 2, 2, KP, R], F16)
        ytok = sb("ytok", [P, 2, D])
        xn = sb("xn", [P, 2, D])
        xf = sb("xf", [P, 2, D])
        xnt = sb("xnt", [P, 2, KD, N2], F16)
        qk = sb("qk", [P, 2, 2 * KI, N2], F16)
        vv = sb("vv", [P, 2, 2, DI], F16)
        probs = sb("probs", [P, 3, HU, R])
        pt = sb("pt", [P, 2, 2, HU, R], F16)
        ot = sb("ot", [P, 2, KI, N2], F16)
        early = ot[:, :, :, :].rearrange("p a k n -> p (a k n)").bitcast(F32)
        addrow2, addrow3 = early[:, 0:D], early[:, D:2 * D]
        brow, onerow = early[0:1, 2 * D:3 * D], early[0:1, 3 * D:3 * D + R]
        b1wide = early[:, 4 * D:4 * D + KP * R].rearrange("p (k r) -> p k r", k=KP)
        negmax = sb("negmax", [P, UNITS, HU])
        ebias = sb("ebias", [P, UNITS, HU])
        rowsum = sb("rowsum", [P, UNITS, HU])
        rinv = sb("rinv", [P, UNITS, HU])
        xst = sb("xst", [P, 2, 2, 6])
        xmv = sb("xmv", [P, 2, 2])
        yst = sb("yst", [P, 2, 6])
        ymv = sb("ymv", [P, 2, 2])
        hst = sb("hst", [P, 2, 6])
        hmv = sb("hmv", [P, 2, 2])
        fst = sb("fst", [P, 2, 6])
        fmv = sb("fmv", [P, 2, 2])
        xrs = sb("xrs", [P, 2, 2])
        yrs = sb("yrs", [P, 2, 3])
        hrs = sb("hrs", [P, 2, 8])
        frs = sb("frs", [P, 2, 2])

        qkf = qk[:, :, :, :].rearrange("p a c n -> p (a c n)").bitcast(F32)
        TE = TILES * E
        def rt(k):
            return qkf[0:R, k * TE:(k + 1) * TE].rearrange("p (t e) -> p t e", t=TILES)
        def rg(k):
            return qkf[0:R, 8 * TE + k * TILES * 4:8 * TE + (k + 1) * TILES * 4].rearrange("p (t g) -> p t g", t=TILES)
        comb = sb("comb", [P, TILES, NE])
        comb12 = sb("comb12", [P, TILES, NE])
        combt = sb("combt", [NE, N2])
        comb_now = sb("comb_now", [P, 2, NE])
        sc8 = sb("sc8", [P, 8, TILES])
        vf = vv[:, :, :, :].rearrange("p a t n -> p (a t n)").bitcast(F32)
        silu = vf[:, 0:2 * N2].rearrange("p (s n) -> p s n", s=2)
        gated = vf[:, 2 * N2:5 * N2].rearrange("p (s n) -> p s n", s=3)
        gp = pt[:, :, :, :, :].rearrange("p s a h r -> p (s a h r)")[:, 0:6 * N2].rearrange("p (s a n) -> p s a n", s=3, a=2)

        proj_ps = [bank(f"proj{k}", [P, 512]) for k in range(2)]
        front_ps = bank("front", [P, 512])
        back_ps = bank("back", [P, 512])
        score_ps = [bank(f"score{k}", [P, 512]) for k in range(2)]
        pt_ps = bank("ptps", [P, 512])
        o_ps = bank("ops", [P, 512])

        const_in = sem("const_in")
        stage_in = [sem(f"stage_in{k}") for k in range(3)]
        w_hi, w_lo = sem("w_hi"), sem("w_lo")
        prep = sem("prep")
        bias_mm = sem("bias_mm")
        x_in = [sem(f"x_in{k}") for k in range(2)]
        proj_ready, proj_hi, proj_lo = sem("proj_ready"), sem("proj_hi"), sem("proj_lo")
        front_ready, front_hi, front_out = sem("front_ready"), sem("front_hi"), sem("front_out")
        back_ready, back_hi, back_out = sem("back_ready"), sem("back_hi"), sem("back_out")
        scores_ready, max_done, bias_done, exp_done = sem("scores_ready"), sem("max_done"), sem("bias_done"), sem("exp_done")
        rinv_done, probs_ready = sem("rinv_done"), sem("probs_ready")
        pt_ready, pt_hi, pt_lo = sem("pt_ready"), sem("pt_hi"), sem("pt_lo")
        pv_ready, ot_hi, ot_lo = sem("pv_ready"), sem("ot_hi"), sem("ot_lo")
        x_stats, x_moments, x_rstd, xhat_done = sem("x_stats"), sem("x_moments"), sem("x_rstd"), sem("xhat_done")
        y_stats, y_moments, y_rstd = sem("y_stats"), sem("y_moments"), sem("y_rstd")
        y_norm, y_gain, h_done = sem("y_norm"), sem("y_gain"), sem("h_done")
        h_stats, h_moments, h_scale, xn_done = sem("h_stats"), sem("h_moments"), sem("h_scale"), sem("xn_done")
        f_stats, f_moments, f_rstd, xf_done = sem("f_stats"), sem("f_moments"), sem("f_rstd"), sem("xf_done")
        px, py, ph, pf = sem("px_step"), sem("py_step"), sem("ph_step"), sem("pf_step")
        route, route_exp_in, route_exp = sem("route"), sem("route_exp_in"), sem("route_exp")
        comb_now_in = sem("comb_now_in")
        combt_ready, combt_out, be2_ready, be2_added = sem("combt_ready"), sem("combt_out"), sem("be2_ready"), sem("be2_added")
        ff_ready, silu_done, gated_done, g_hi, g_lo = sem("ff_ready"), sem("silu_done"), sem("gated_done"), sem("g_hi"), sem("g_lo")
        y_ready, y_added = sem("y_ready"), sem("y_added")
        rows_final = sem("rows_final")
        stored = sem("stored")

        def stage_at(slot, *shape):
            n = int(np.prod(shape))
            v = stage[:, slot * 1536:slot * 1536 + n]
            names = "abc"[:len(shape)]
            return v.rearrange(f"p ({' '.join(names)}) -> p {' '.join(names)}", **dict(zip(names, shape)))

        pieces = []

        def piece(loads, parts):
            pieces.append((loads, parts))

        def slot():
            return len(pieces) % 3

        v = stage_at(slot(), KP, D)
        piece([(v, a["L0_tok_W"].rearrange("(k p) d -> p k d", p=P))],
              [(v[:, k, :], wtok[:, 0, k, :], wtok[:, 1, k, :], ("g1", k)) for k in range(KP)])
        for k in range(KD):
            for half in range(2):
                v = stage_at(slot(), 1536)
                sl = slice(half * 1536, (half + 1) * 1536)
                piece([(v, a["L0_attn_w_qkv"][k * P:(k + 1) * P, sl])],
                      [(v, wqkv[:, 0, k, sl], wqkv[:, 1, k, sl], ("gam", k))])
        for half in range(2):
            v = stage_at(slot(), 4, D)
            sl = slice(4 * half, 4 * half + 4)
            piece([(v, a["L0_attn_w_out"].rearrange("(c p) d -> p c d", p=P)[:, sl, :])],
                  [(v, wout[:, 0, sl, :], wout[:, 1, sl, :], None)])
        for e in range(0, NE, 2):
            v = stage_at(slot(), 2, KD, 2 * INTER)
            loads = []
            for j in range(2):
                for n, (routed, shared) in enumerate((("We1", "ws1"), ("We3", "ws3"))):
                    src = (a["L0_ffn_" + routed][e + j] if e < E
                           else a["L0_ffn_" + shared][:, j * INTER:(j + 1) * INTER])
                    loads.append((v[:, j, :, n * INTER:(n + 1) * INTER], src.rearrange("(c p) i -> p c i", p=P)))
            piece(loads, [(v, w13[:, 0, e:e + 2], w13[:, 1, e:e + 2], None)])
        for e in range(0, NE, 4):
            n = min(4, NE - e)
            v = stage_at(slot(), n, D)
            src = (a["L0_ffn_We2"][e:e + n].rearrange("e i d -> i e d") if e < E
                   else a["L0_ffn_ws2"].rearrange("(m i) d -> i m d", m=2))
            piece([(v, src)], [(v, w2[:, 0, e:e + n, :], w2[:, 1, e:e + n, :], None)])

        def landed(k):
            return stage_in[k % 3], 16 * sum(len(pieces[j][0]) for j in range(k % 3, k + 1, 3))

        block = ctx.enter_context(nc.Block())

        NCONST = 21

        @block.sync
        def _(sp):
            n = [0]

            def const(dst, src):
                n[0] += 1
                sp.dma_start(dst, src, allow_slow_non_contiguous=True).then_inc(const_in, 16)

            const(g1col[:, :], a["L0_tok_ln1_g"])
            const(b1col[:, :], a["L0_tok_ln1_b"])
            const(gamcol[:, :], a["L0_attn_gamma"])
            for k, (loads, _parts) in enumerate(pieces[:3]):
                for dst, src in loads:
                    sp.dma_start(dst, src).then_inc(stage_in[k % 3], 16)
            sp.wait_ge(prep, 1)
            const(ident[:, :], a["c_ident"])
            const(maskl[:, :], a["c_maskl"])
            const(maskr[:, :], a["c_maskr"])
            const(small[:, :], a["c_small"])
            const(addrow[:, :], a["c_pe"])
            const(addrow2[0:PR, :], a["L0_tok_ln2_b"].rearrange("(o d) -> o d", o=1).to_broadcast([PR, D]))
            const(addrow2[PR:R, :], a["L0_tok_cls_token"].rearrange("a b d -> (a b) d").to_broadcast([GI, D]))
            const(addrow3[PR:R, :], a["L0_tok_cls_pos_embedding"].rearrange("a b d -> (a b) d").to_broadcast([GI, D]))
            const(g2row[0:R, :], a["L0_tok_ln2_g"].rearrange("(o d) -> o d", o=1).to_broadcast([R, D]))
            const(brow[:, :], a["L0_tok_bias"].rearrange("(o d) -> o d", o=1))
            const(gatest[:, :, :], a["L0_ffn_gate_w"].rearrange("(k p) e -> p k e", p=P))
            const(gbrow[0:R, :], a["L0_ffn_gate_b"].rearrange("(o e) -> o e", o=1).to_broadcast([R, E]))
            const(b13col[:, 0, 0:E], a["L0_ffn_be1"])
            const(b13col[:, 1, 0:E], a["L0_ffn_be3"])
            const(b13col[:, 0, E:NE], a["L0_ffn_bs1"])
            const(b13col[:, 1, E:NE], a["L0_ffn_bs3"])
            const(be2row[0:E, :], a["L0_ffn_be2"])
            const(be2row[E:E + 1, :], a["L0_ffn_bs2"].rearrange("(o d) -> o d", o=1))

            def load_x(b0, t):
                sp.dma_start(xin[0:PR, t, :], x[bass.ds(b0 * NPATCH, PR), :]).then_inc(x_in[t], 16)

            load_x(0, 0)
            load_x(GI, 1)
            for k in range(3, len(pieces)):
                sp.wait_ge(w_lo, k - 2)
                sp.wait_ge(w_hi, k - 2)
                for dst, src in pieces[k][0]:
                    sp.dma_start(dst, src).then_inc(stage_in[k % 3], 16)

            with sp.Fori(4, 4 + 7 * (G - 2), 7) as turned:
                sp.wait_ge(const_in, 16)
                sp.wait_ge(front_ready, turned)
                g = (turned - 4) // 7 + 1
                load_x(2 * GI * g, 0)
                load_x(2 * GI * g + GI, 1)
            sp.wait_ge(front_ready, done(7, G - 2, 3))
            load_x(2 * GI * (G - 1), 0)
            load_x(LAST_B0, 1)

            flat = out.rearrange("b s d -> (b s) d")
            cls = out[:, 0, :]

            def store(tile, b0, first=0):
                for im in range(first, GI):
                    sp.dma_start(flat[bass.ds((b0 + im) * SEQ + 1, NPATCH), :],
                                 hrows[im * NPATCH:(im + 1) * NPATCH, tile, :]).then_inc(stored, 16)
                sp.dma_start(cls[bass.ds(b0 + first, GI - first), :], hrows[PR + first:R, tile, :]).then_inc(stored, 16)

            with sp.Fori(1, G) as ready:
                sp.wait_ge(const_in, 16)
                sp.wait_ge(rows_final, ready)
                g = ready - 1
                store(2 * g, 2 * GI * g)
                store(2 * g + 1, 2 * GI * g + GI)
            sp.wait_ge(rows_final, G)
            store(TILES - 2, 2 * GI * (G - 1))
            store(TILES - 1, LAST_B0, first=GI * (TILES - 1) - LAST_B0)
            sp.wait_ge(stored, 16 * ((1 + GI) * TILES - (GI * (TILES - 1) - LAST_B0)))
            assert n[0] == NCONST, n[0]

        @block.tensor
        def _(pe):
            def mm3(dst, lh, rh, first, last, **kw):
                pe.matmul(dst, lh[0], rh[0], start=first, stop=False, **kw)
                pe.matmul(dst, lh[0], rh[1], start=False, stop=False, **kw)
                return pe.matmul(dst, lh[1], rh[0], start=False, stop=last, **kw)

            pe.wait_ge(prep, 4)
            pe.wait_ge(*landed(0))
            v0 = stage_at(0, KP, D)
            for k in range(KP):
                pe.matmul(back_ps[0:R, 0:D], b1wide[:, k, :], v0[:, k, :], start=k == 0, stop=False)
            pe.matmul(back_ps[0:R, 0:D], onerow[:, :], brow[:, :], start=False, stop=True).then_inc(bias_mm, 1)

            def project(g, s):
                if s == 0:
                    pe.wait_ge(front_out, done(7, g, 6))
                if not (isinstance(g, int) and g == 0 and s < 2):
                    pe.wait_ge(proj_lo, done(12, g, s - 2))
                bk = proj_ps[s % 2]
                if s < 8:
                    for j in range(2):
                        cs = slice((2 * s + j) * P, (2 * s + j + 1) * P)
                        for k in range(KD):
                            ins = mm3(bk[:, j * N2:(j + 1) * N2], (wqkv[:, 0, k, cs], wqkv[:, 1, k, cs]),
                                      (xnt[:, 0, k, :], xnt[:, 1, k, :]), k == 0, k == KD - 1)
                else:
                    t, half = (s - 8) // 2, s % 2
                    cs = slice(2 * DI + half * 512, 2 * DI + (half + 1) * 512)
                    ts = slice(t * R, (t + 1) * R)
                    for k in range(KD):
                        ins = mm3(bk[0:R, :], (xnt[:, 0, k, ts], xnt[:, 1, k, ts]),
                                  (wqkv[:, 0, k, cs], wqkv[:, 1, k, cs]), k == 0, k == KD - 1)
                ins.then_inc(proj_ready, 1)

            def scores(g, u):
                t, half, par = u // 4, u // 2 % 2, u % 2
                if u == 0:
                    pe.wait_ge(proj_lo, done(12, g, 7))
                if not (isinstance(g, int) and g == 0 and u < 2):
                    pe.wait_ge(exp_done, done(8, g, u - 2))
                bk = score_ps[u % 2]
                rows = slice(64 * par, 64 * par + 64)
                pe.matmul(bk[0:R, 0:HU * R], maskl[rows, :], maskr[rows, :], start=True, stop=False)
                for j in range(HU):
                    ch = 4 * half + j
                    ts = slice(t * R, (t + 1) * R)
                    ins = mm3(bk[0:R, j * R:(j + 1) * R],
                              (qk[rows, 0, ch, ts], qk[rows, 1, ch, ts]),
                              (qk[rows, 0, KI + ch, ts], qk[rows, 1, KI + ch, ts]), False, j == HU - 1)
                ins.then_inc(scores_ready, 1)

            def turn_probs(g, u):
                pe.wait_ge(probs_ready, done(8, g, u))
                if not (isinstance(g, int) and g == 0 and u == 0):
                    pe.wait_ge(pt_lo, done(8, g, u - 1))
                for j in range(HU):
                    ins = pe.transpose(pt_ps[0:R, j * R:(j + 1) * R], probs[0:R, u % 3, j, :], ident[0:R, 0:R])
                ins.then_inc(pt_ready, 1)

            def attend(g, u):
                t, half, par = u // 4, u // 2 % 2, u % 2
                if u == 0:
                    pe.wait_ge(proj_lo, done(12, g, 11))
                pe.wait_ge(pt_lo, done(8, g, u))
                if par == 0 and not (isinstance(g, int) and g == 0 and u == 0):
                    pe.wait_ge(ot_lo, done(4, g, u // 2 - 1))
                for j in range(HU):
                    h = 2 * (4 * half + j) + par
                    hs = slice(h * DH, (h + 1) * DH)
                    ins = mm3(o_ps[64 * par:64 * par + 64, j * R:(j + 1) * R],
                              (vv[0:R, 0, t, hs], vv[0:R, 1, t, hs]),
                              (pt[0:R, u % 2, 0, j, :], pt[0:R, u % 2, 1, j, :]), True, True)
                ins.then_inc(pv_ready, 1)

            def turn_pixels(g, t, part):
                pe.wait_ge(xhat_done, done(2, g, t))
                if not (isinstance(g, int) and g == 0 and t == 0 and part == 0):
                    pe.wait_ge(front_out, done(7, g, 2 * t + part - 1))
                for j in range(3):
                    k = 3 * part + j
                    ins = pe.transpose(front_ps[:, j * PR:(j + 1) * PR], xin[0:PR, t, k * P:(k + 1) * P], ident[0:PR, 0:PR])
                ins.then_inc(front_ready, 1)

            def embed(g, t):
                pe.wait_ge(front_out, done(7, g, 3 + t))
                for k in range(KP):
                    ins = mm3(front_ps[0:R, 0:D], (xt[:, t, 0, k, :], xt[:, t, 1, k, :]),
                              (wtok[:, 0, k, :], wtok[:, 1, k, :]), k == 0, k == KP - 1)
                ins.then_inc(front_ready, 1)

            def turn_rows(g):
                pe.wait_ge(xn_done, done(2, g, 1))
                pe.wait_ge(front_out, done(7, g, 5))
                for k in range(KD):
                    for t in range(2):
                        ins = pe.transpose(front_ps[:, k * N2 + t * R:k * N2 + (t + 1) * R],
                                           xn[0:R, t, k * P:(k + 1) * P], ident[0:R, 0:R])
                ins.then_inc(front_ready, 1)

            def out_proj(g, t):
                pe.wait_ge(ot_lo, done(4, g, 2 * t + 1))
                if not (isinstance(g, int) and g == 0 and t == 0):
                    pe.wait_ge(back_out, done(4, g, t - 1))
                ts = slice(t * R, (t + 1) * R)
                for k in range(KI):
                    ins = mm3(back_ps[0:R, 0:D], (ot[:, 0, k, ts], ot[:, 1, k, ts]),
                              (wout[:, 0, k, :], wout[:, 1, k, :]), k == 0, k == KI - 1)
                ins.then_inc(back_ready, 1)

            def turn_xf(g):
                pe.wait_ge(xf_done, done(2, g, 1))
                pe.wait_ge(back_out, done(4, g, 1))
                for k in range(KD):
                    for t in range(2):
                        ins = pe.transpose(back_ps[:, k * N2 + t * R:k * N2 + (t + 1) * R],
                                           xf[0:R, t, k * P:(k + 1) * P], ident[0:R, 0:R])
                ins.then_inc(back_ready, 1)

            def gate(g):
                pe.wait_ge(back_out, done(4, g, 2))
                for t in range(2):
                    for k in range(KD):
                        cs = bass.ds(g * N2 + t * R, R)
                        ins = mm3(back_ps[0:R, t * E:(t + 1) * E], (xft[:, 0, k, cs], xft[:, 1, k, cs]),
                                  (wgate[:, 0, k, :], wgate[:, 1, k, :]), k == 0, k == KD - 1)
                ins.then_inc(back_ready, 1)

            def front(g):
                for t in range(2):
                    turn_pixels(g, t, 0)
                    turn_pixels(g, t, 1)
                embed(g, 0)
                embed(g, 1)
                turn_rows(g)

            def tail(g):
                pass

            def body(g, first, last):
                if not first:
                    turn_probs(g - 1, 6)
                    attend(g - 1, 5)
                project(g, 0)
                if not first:
                    turn_probs(g - 1, 7)
                    attend(g - 1, 6)
                project(g, 1)
                project(g, 2)
                if not first:
                    attend(g - 1, 7)
                for s in range(3, 6):
                    project(g, s)
                if not first:
                    out_proj(g - 1, 0)
                project(g, 6)
                if not first:
                    out_proj(g - 1, 1)
                project(g, 7)
                project(g, 8)
                project(g, 9)
                scores(g, 0)
                project(g, 10)
                if not first:
                    turn_xf(g - 1)
                scores(g, 1)
                project(g, 11)
                if not last:
                    turn_pixels(g + 1, 0, 0)
                if not first:
                    gate(g - 1)
                for s in range(2, UNITS):
                    scores(g, s)
                    if not last:
                        if s == 2:
                            turn_pixels(g + 1, 0, 1)
                        if s == 3:
                            turn_pixels(g + 1, 1, 0)
                        if s == 4:
                            embed(g + 1, 0)
                        if s == 5:
                            embed(g + 1, 1)
                    turn_probs(g, s - 2)
                    if s >= 3:
                        attend(g, s - 3)
                    if s == 3 and not last:
                        turn_pixels(g + 1, 1, 1)
                if not last:
                    turn_rows(g + 1)

            pe.wait_ge(prep, 5)
            pe.wait_ge(w_lo, len(pieces))
            pe.wait_ge(prep, 9)
            front(0)
            body(0, True, False)
            with pe.Fori(1, G - 1) as g:
                body(g, False, False)
            body(G - 1, False, True)
            turn_probs(G - 1, 6)
            attend(G - 1, 5)
            turn_probs(G - 1, 7)
            attend(G - 1, 6)
            attend(G - 1, 7)
            out_proj(G - 1, 0)
            out_proj(G - 1, 1)
            turn_xf(G - 1)
            gate(G - 1)

            def hidden(g, e):
                if not (isinstance(g, int) and g == 0 and e < 2):
                    pe.wait_ge(gated_done, done(NE, g, e - 2))
                cs = bass.ds(g * N2, N2)
                bk = proj_ps[e % 2]
                for j in range(2):
                    ws = slice(j * INTER, (j + 1) * INTER)
                    for k in range(KD):
                        ins = mm3(bk[:, j * N2:(j + 1) * N2], (w13[:, 0, e, k, ws], w13[:, 1, e, k, ws]),
                                  (xft[:, 0, k, cs], xft[:, 1, k, cs]), k == 0, k == KD - 1)
                ins.then_inc(ff_ready, 1)

            def down(g, e):
                pe.wait_ge(g_lo, done(NE, g, e))
                if not (isinstance(g, int) and g == 0 and e < 2):
                    pe.wait_ge(y_added, done(NE, g, e - 2))
                for t in range(2):
                    ts = slice(t * R, (t + 1) * R)
                    ins = mm3(score_ps[e % 2][0:R, t * D:(t + 1) * D], (gp[:, e % 3, 0, ts], gp[:, e % 3, 1, ts]),
                              (w2[:, 0, e, :], w2[:, 1, e, :]), True, True)
                ins.then_inc(y_ready, 1)

            def experts(g, first):
                if not first:
                    pe.wait_ge(be2_added, g)
                pe.wait_ge(comb_now_in, g + 1)
                for t in range(2):
                    ins = pe.transpose(pt_ps[0:NE, t * R:(t + 1) * R], comb_now[0:R, t, :], ident[0:R, 0:R])
                ins.then_inc(combt_ready, 1)
                for e in range(NE):
                    hidden(g, e)
                    if e >= 2:
                        down(g, e - 2)
                    elif not first:
                        down(g - 1, NE - 2 + e)
                    if e == 1:
                        pe.wait_ge(combt_out, g + 1)
                        for t in range(2):
                            ins = pe.matmul(o_ps[0:R, t * D:(t + 1) * D], combt[:, t * R:(t + 1) * R], be2row[:, :],
                                            start=True, stop=True)
                        ins.then_inc(be2_ready, 1)

            pe.wait_ge(route, ROUTE_STEPS)
            experts(0, True)
            with pe.Fori(1, G) as g:
                experts(g, False)
            down(G - 1, NE - 2)
            down(G - 1, NE - 1)

        @block.scalar
        def _(act):
            for k, (_loads, parts) in enumerate(pieces):
                act.wait_ge(*landed(k))
                if k == 0:
                    act.wait_ge(prep, 3)
                for n, (st, hi, _lo, scale) in enumerate(parts):
                    s = WS if scale is None else {"g1": g1col, "gam": gamcol}[scale[0]][:, scale[1]:scale[1] + 1]
                    ins = nc.scalar.activation(hi, st, ACT.Copy, scale=s)
                ins.then_inc(w_hi, 1)
            act.wait_ge(prep, 5)
            nc.scalar.activation(wgate[:, 0], gatest[:, :, :], ACT.Copy, scale=WS).then_inc(w_hi, 1)

            def project_hi(g, s):
                act.wait_ge(proj_ready, done(12, g, s))
                if s < 8:
                    nc.scalar.activation(qk[:, 0, 2 * s:2 * s + 2, :],
                                         proj_ps[s % 2][:, 0:2 * N2].rearrange("p (a n) -> p a n", a=2),
                                         ACT.Copy).then_inc(proj_hi, 1)
                else:
                    t, half = (s - 8) // 2, s % 2
                    nc.scalar.activation(vv[0:R, 0, t, half * 512:(half + 1) * 512], proj_ps[s % 2][0:R, :],
                                         ACT.Copy).then_inc(proj_hi, 1)

            def exps(g, u):
                act.wait_ge(bias_done, done(8, g, u))
                for j in range(HU):
                    ins = nc.scalar.activation(probs[0:R, u % 3, j, :], score_ps[u % 2][0:R, j * R:(j + 1) * R], ACT.Exp,
                                               bias=ebias[0:R, u, j:j + 1], scale=EXP_SCALE,
                                               accum_out=rowsum[0:R, u, j:j + 1])
                ins.then_inc(exp_done, 1)

            def probs_hi(g, u):
                act.wait_ge(pt_ready, done(8, g, u))
                nc.scalar.activation(pt[0:R, u % 2, 0], pt_ps[0:R, 0:HU * R].rearrange("p (h r) -> p h r", h=HU),
                                     ACT.Copy, scale=PS).then_inc(pt_hi, 1)

            def attend_hi(g, w):
                t, half = w // 2, w % 2
                act.wait_ge(pv_ready, done(8, g, 2 * w + 1))
                nc.scalar.activation(ot[:, 0, 4 * half:4 * half + 4, t * R:(t + 1) * R],
                                     o_ps[:, 0:HU * R].rearrange("p (h r) -> p h r", h=HU),
                                     ACT.Copy, scale=1.0 / PS).then_inc(ot_hi, 1)

            def pixels_hi(g, t, part):
                act.wait_ge(front_ready, done(7, g, 2 * t + part))
                nc.scalar.activation(xt[:, t, 0, 3 * part:3 * part + 3, 0:PR],
                                     front_ps[:, 0:3 * PR].rearrange("p (k r) -> p k r", k=3),
                                     ACT.Copy).then_inc(front_hi, 1)

            def rows_hi(g):
                act.wait_ge(front_ready, done(7, g, 6))
                nc.scalar.activation(xnt[:, 0], front_ps[:, 0:KD * N2].rearrange("p (k n) -> p k n", k=KD),
                                     ACT.Copy).then_inc(front_hi, 1)

            def xf_hi(g):
                act.wait_ge(back_ready, done(4, g, 2))
                nc.scalar.activation(xft[:, 0, :, bass.ds(g * N2, N2)],
                                     back_ps[:, 0:KD * N2].rearrange("p (k n) -> p k n", k=KD),
                                     ACT.Copy).then_inc(back_hi, 1)

            def body(g, first, last):
                if not first:
                    probs_hi(g - 1, 6)
                    attend_hi(g - 1, 2)
                project_hi(g, 0)
                if not first:
                    probs_hi(g - 1, 7)
                project_hi(g, 1)
                project_hi(g, 2)
                if not first:
                    attend_hi(g - 1, 3)
                for s in range(3, 10):
                    project_hi(g, s)
                exps(g, 0)
                project_hi(g, 10)
                if not first:
                    xf_hi(g - 1)
                exps(g, 1)
                project_hi(g, 11)
                if not last:
                    pixels_hi(g + 1, 0, 0)
                for s in range(2, UNITS):
                    if not last:
                        if s == 2:
                            pixels_hi(g + 1, 0, 1)
                        if s == 3:
                            pixels_hi(g + 1, 1, 0)
                    probs_hi(g, s - 2)
                    exps(g, s)
                    if s in (4, 6):
                        attend_hi(g, s // 2 - 2)
                    if s == 3 and not last:
                        pixels_hi(g + 1, 1, 1)
                if not last:
                    rows_hi(g + 1)

            for t in range(2):
                for part in range(2):
                    pixels_hi(0, t, part)
            rows_hi(0)
            body(0, True, False)
            with act.Fori(1, G - 1) as g:
                body(g, False, False)
            body(G - 1, False, True)
            probs_hi(G - 1, 6)
            attend_hi(G - 1, 2)
            probs_hi(G - 1, 7)
            attend_hi(G - 1, 3)
            xf_hi(G - 1)

            act.wait_ge(route_exp_in, 1)
            nc.scalar.activation(rt(1), rt(0), ACT.Exp).then_inc(route_exp, 1)

            def gated_hi(g, e):
                act.wait_ge(gated_done, done(NE, g, e))
                if not (isinstance(g, int) and g == 0 and e < 3):
                    act.wait_ge(y_ready, done(NE, g, e - 3))
                nc.scalar.activation(gp[:, e % 3, 0, :], gated[:, e % 3, :], ACT.Copy).then_inc(g_hi, 1)

            def experts(g, first):
                act.wait_ge(combt_ready, g + 1)
                nc.scalar.activation(combt[:, :], pt_ps[0:NE, 0:N2], ACT.Copy).then_inc(combt_out, 1)
                for e in range(NE):
                    act.wait_ge(ff_ready, done(NE, g, e))
                    nc.scalar.activation(silu[:, e % 2, :], proj_ps[e % 2][:, 0:N2], ACT.Silu,
                                         bias=b13col[:, 0, e:e + 1], scale=1.0 / WS).then_inc(silu_done, 1)
                    if e > 0:
                        gated_hi(g, e - 1)
                    elif not first:
                        gated_hi(g - 1, NE - 1)

            experts(0, True)
            with act.Fori(1, G) as g:
                experts(g, False)
            gated_hi(G - 1, NE - 1)

        @block.vector
        def _(dve):
            V = nc.vector
            V.memset(xt[:, :, :, :, PR:R], 0.0)
            V.memset(onerow[:, :], 1.0)
            V.memset(addrow3[:, :], 0.0)
            V.memset(power[:, 0:1], -0.5)
            V.memset(power[:, 1:2], 0.5)
            V.memset(power[:, 2:3], -1.0)
            V.memset(power[:, 3:4], EPS)
            V.memset(power[:, 4:5], float(D) ** 0.5)
            V.memset(be2row[:, :], 0.0).then_inc(prep, 1)
            dve.wait_ge(const_in, 16 * NCONST)
            V.tensor_scalar(gamcol[:, :], gamcol[:, :], 1.0, WS, ALU.add, ALU.mult).then_inc(prep, 1)
            V.tensor_scalar(g1col[:, :], g1col[:, :], WS, None, ALU.mult).then_inc(prep, 1)
            V.tensor_copy(b1wide[:, :, :], b1col[:, :].unsqueeze(2).to_broadcast([P, KP, R])).then_inc(prep, 1)
            V.tensor_scalar(b13col[:, 1, :], b13col[:, 1, :], WS, None, ALU.mult).then_inc(prep, 1)
            V.tensor_tensor(addrow[0:R, :], addrow[0:R, :], addrow2[0:R, :], ALU.add).then_inc(prep, 1)
            dve.wait_ge(prep, 6)
            V.tensor_tensor(addrow[0:R, :], addrow[0:R, :], addrow3[0:R, :], ALU.add).then_inc(prep, 1)
            dve.wait_ge(bias_mm, 1)
            V.tensor_copy(biasrow[0:R, :], back_ps[0:R, 0:D]).then_inc(prep, 1)
            for k, (_loads, parts) in enumerate(pieces):
                dve.wait_ge(w_hi, k + 1)
                for st, hi, lo, scale in parts:
                    s = WS if scale is None else {"g1": g1col, "gam": gamcol}[scale[0]][:, scale[1]:scale[1] + 1]
                    if len(st.shape) > 3:
                        merge = "p a b c -> p (a b c)"
                        st, hi, lo = st.rearrange(merge), hi.rearrange(merge), lo.rearrange(merge)
                    ins = V.scalar_tensor_tensor(lo, st, s, hi, ALU.mult, ALU.subtract)
                ins.then_inc(w_lo, 1)
            dve.wait_ge(w_hi, len(pieces) + 1)
            V.scalar_tensor_tensor(wgate[:, 1], gatest[:, :, :], WS, wgate[:, 0], ALU.mult, ALU.subtract).then_inc(prep, 1)

            def project_lo(g, s):
                dve.wait_ge(proj_hi, done(12, g, s))
                if s < 8:
                    dst = lambda n: qk[:, n, 2 * s:2 * s + 2, :]
                    V.tensor_tensor(dst(1), proj_ps[s % 2][:, 0:2 * N2].rearrange("p (a n) -> p a n", a=2), dst(0),
                                    ALU.subtract).then_inc(proj_lo, 1)
                else:
                    t, half = (s - 8) // 2, s % 2
                    cs = slice(half * 512, (half + 1) * 512)
                    V.tensor_tensor(vv[0:R, 1, t, cs], proj_ps[s % 2][0:R, :], vv[0:R, 0, t, cs],
                                    ALU.subtract).then_inc(proj_lo, 1)

            def row_max(g, u):
                dve.wait_ge(scores_ready, done(8, g, u))
                V.tensor_reduce(negmax[0:R, u, :], score_ps[u % 2][0:R, 0:HU * R].rearrange("p (h r) -> p h r", h=HU),
                                AX.X, ALU.max, negate=True).then_inc(max_done, 1)
                dve.wait_ge(max_done, done(8, g, u))
                V.tensor_scalar(ebias[0:R, u, :], negmax[0:R, u, :], EXP_SCALE, None, ALU.mult).then_inc(bias_done, 1)

            def row_inv(g, u):
                dve.wait_ge(exp_done, done(8, g, u))
                V.reciprocal(rinv[0:R, u, :], rowsum[0:R, u, :]).then_inc(rinv_done, 1)

            def probs_lo(g, u):
                dve.wait_ge(pt_hi, done(8, g, u))
                V.scalar_tensor_tensor(pt[0:R, u % 2, 1], pt_ps[0:R, 0:HU * R].rearrange("p (h r) -> p h r", h=HU), PS,
                                       pt[0:R, u % 2, 0], ALU.mult, ALU.subtract).then_inc(pt_lo, 1)

            def attend_lo(g, w):
                t, half = w // 2, w % 2
                dst = lambda n: ot[:, n, 4 * half:4 * half + 4, t * R:(t + 1) * R]
                dve.wait_ge(ot_hi, done(4, g, w))
                V.scalar_tensor_tensor(dst(1), o_ps[:, 0:HU * R].rearrange("p (h r) -> p h r", h=HU), 1.0 / PS,
                                       dst(0), ALU.mult, ALU.subtract).then_inc(ot_lo, 1)

            def pixel_stats(g, t):
                dve.wait_ge(x_in[t], 16 * g + 16)
                V.bn_stats(xst[0:PR, t, 0, :], xin[0:PR, t, 0:PD // 2])
                V.bn_stats(xst[0:PR, t, 1, :], xin[0:PR, t, PD // 2:PD]).then_inc(x_stats, 1)
                dve.wait_ge(x_stats, done(2, g, t))
                V.memset(scrap[:, 0:1], 0.0)
                V.bn_aggr(xmv[0:PR, t, :], xst[0:PR, t, :, :].rearrange("p a b -> p (a b)")).then_inc(x_moments, 1)

            def pixel_norm(g, t):
                dve.wait_ge(x_rstd, done(2, g, t))
                V.tensor_scalar(xin[0:PR, t, :], xin[0:PR, t, :], xmv[0:PR, t, 0:1], xrs[0:PR, t, 1:2],
                                ALU.subtract, ALU.mult).then_inc(xhat_done, 1)

            def pixels_lo(g, t, part):
                dve.wait_ge(front_hi, done(5, g, 2 * t + part))
                dst = lambda n: xt[:, t, n, 3 * part:3 * part + 3, 0:PR]
                V.tensor_tensor(dst(1), front_ps[:, 0:3 * PR].rearrange("p (k r) -> p k r", k=3), dst(0),
                                ALU.subtract).then_inc(front_out, 1)

            def embed_out(g, t):
                dve.wait_ge(front_ready, done(7, g, 4 + t))
                V.scalar_tensor_tensor(ytok[0:R, t, :], front_ps[0:R, 0:D], 1.0 / WS, biasrow[0:R, :],
                                       ALU.mult, ALU.add).then_inc(front_out, 1)
                dve.wait_ge(front_out, done(7, g, 4 + t))
                V.memset(scrap[:, 0:1], 0.0)
                V.bn_stats(yst[0:R, t, :], ytok[0:R, t, :]).then_inc(y_stats, 1)
                dve.wait_ge(y_stats, done(2, g, t))
                V.memset(scrap[:, 0:1], 0.0)
                V.bn_aggr(ymv[0:R, t, :], yst[0:R, t, :]).then_inc(y_moments, 1)

            def token_rows(g, t):
                h = hrows[0:R, 2 * g + t, :]
                dve.wait_ge(y_rstd, done(2, g, t))
                V.tensor_scalar(ytok[0:R, t, :], ytok[0:R, t, :], ymv[0:R, t, 0:1], yrs[0:R, t, 2:3],
                                ALU.subtract, ALU.mult).then_inc(y_norm, 1)
                dve.wait_ge(y_norm, done(2, g, t))
                V.tensor_tensor(ytok[0:R, t, :], ytok[0:R, t, :], g2row[0:R, :], ALU.mult).then_inc(y_gain, 1)
                dve.wait_ge(y_gain, done(2, g, t))
                V.tensor_tensor(h, ytok[0:R, t, :], addrow[0:R, :], ALU.add).then_inc(h_done, 1)
                dve.wait_ge(h_done, done(2, g, t))
                V.memset(scrap[:, 0:1], 0.0)
                V.bn_stats(hst[0:R, t, :], h).then_inc(h_stats, 1)
                dve.wait_ge(h_stats, done(2, g, t))
                V.memset(scrap[:, 0:1], 0.0)
                V.bn_aggr(hmv[0:R, t, :], hst[0:R, t, :]).then_inc(h_moments, 1)

            def norm_rows(g, t):
                dve.wait_ge(h_scale, done(2, g, t))
                V.tensor_scalar(xn[0:R, t, :], hrows[0:R, 2 * g + t, :], hmv[0:R, t, 0:1], hrs[0:R, t, 7:8],
                                ALU.subtract, ALU.mult).then_inc(xn_done, 1)

            def rows_lo(g):
                dve.wait_ge(front_hi, done(5, g, 4))
                V.tensor_tensor(xnt[:, 1], front_ps[:, 0:KD * N2].rearrange("p (k n) -> p k n", k=KD), xnt[:, 0],
                                ALU.subtract).then_inc(front_out, 1)

            def residual(g, t):
                h = hrows[0:R, 2 * g + t, :]
                dve.wait_ge(back_ready, done(4, g, t))
                V.scalar_tensor_tensor(h, back_ps[0:R, 0:D], 1.0 / (WS * WS), h, ALU.mult, ALU.add).then_inc(back_out, 1)
                dve.wait_ge(back_out, done(4, g, t))
                V.memset(scrap[:, 0:1], 0.0)
                V.bn_stats(fst[0:R, t, :], h).then_inc(f_stats, 1)
                dve.wait_ge(f_stats, done(2, g, t))
                V.memset(scrap[:, 0:1], 0.0)
                V.bn_aggr(fmv[0:R, t, :], fst[0:R, t, :]).then_inc(f_moments, 1)

            def norm_xf(g, t):
                dve.wait_ge(f_rstd, done(2, g, t))
                V.tensor_scalar(xf[0:R, t, :], hrows[0:R, 2 * g + t, :], fmv[0:R, t, 0:1], frs[0:R, t, 1:2],
                                ALU.subtract, ALU.mult).then_inc(xf_done, 1)

            def xf_lo(g):
                dve.wait_ge(back_hi, g + 1)
                cs = bass.ds(g * N2, N2)
                V.tensor_tensor(xft[:, 1, :, cs], back_ps[:, 0:KD * N2].rearrange("p (k n) -> p k n", k=KD),
                                xft[:, 0, :, cs], ALU.subtract).then_inc(back_out, 1)

            def gate_out(g):
                dve.wait_ge(back_ready, done(4, g, 3))
                V.tensor_scalar(logits[0:R, bass.ds(2 * g, 2), :], back_ps[0:R, 0:2 * E].rearrange("p (t e) -> p t e", t=2),
                                1.0 / WS, None, ALU.mult).then_inc(back_out, 1)

            def body(g, first, last):
                if not first:
                    row_inv(g - 1, 7)
                    probs_lo(g - 1, 6)
                    attend_lo(g - 1, 2)
                project_lo(g, 0)
                if not first:
                    probs_lo(g - 1, 7)
                project_lo(g, 1)
                project_lo(g, 2)
                if not first:
                    attend_lo(g - 1, 3)
                for s in range(3, 6):
                    project_lo(g, s)
                if not first:
                    residual(g - 1, 0)
                project_lo(g, 6)
                if not first:
                    residual(g - 1, 1)
                project_lo(g, 7)
                if not first:
                    norm_xf(g - 1, 0)
                if not last:
                    pixel_stats(g + 1, 0)
                project_lo(g, 8)
                if not first:
                    norm_xf(g - 1, 1)
                if not last:
                    pixel_stats(g + 1, 1)
                project_lo(g, 9)
                row_max(g, 0)
                if not last:
                    pixel_norm(g + 1, 0)
                project_lo(g, 10)
                if not first:
                    xf_lo(g - 1)
                row_inv(g, 0)
                row_max(g, 1)
                if not last:
                    pixel_norm(g + 1, 1)
                project_lo(g, 11)
                if not last:
                    pixels_lo(g + 1, 0, 0)
                if not first:
                    gate_out(g - 1)
                for s in range(2, UNITS):
                    row_inv(g, s - 1)
                    row_max(g, s)
                    if not last:
                        if s == 2:
                            pixels_lo(g + 1, 0, 1)
                        if s == 3:
                            pixels_lo(g + 1, 1, 0)
                        if s == 4:
                            embed_out(g + 1, 0)
                        if s == 5:
                            token_rows(g + 1, 0)
                            embed_out(g + 1, 1)
                        if s == 6:
                            norm_rows(g + 1, 0)
                            token_rows(g + 1, 1)
                        if s == 7:
                            norm_rows(g + 1, 1)
                    probs_lo(g, s - 2)
                    if s in (4, 6):
                        attend_lo(g, s // 2 - 2)
                    if s == 3 and not last:
                        pixels_lo(g + 1, 1, 1)
                if not last:
                    rows_lo(g + 1)

            for t in range(2):
                pixel_stats(0, t)
                pixel_norm(0, t)
            for t in range(2):
                for part in range(2):
                    pixels_lo(0, t, part)
            for t in range(2):
                embed_out(0, t)
            for t in range(2):
                token_rows(0, t)
            for t in range(2):
                norm_rows(0, t)
            rows_lo(0)
            body(0, True, False)
            with dve.Fori(1, G - 1) as g:
                body(g, False, False)
            body(G - 1, False, True)
            row_inv(G - 1, 7)
            probs_lo(G - 1, 6)
            attend_lo(G - 1, 2)
            probs_lo(G - 1, 7)
            attend_lo(G - 1, 3)
            for t in range(2):
                residual(G - 1, t)
            for t in range(2):
                norm_xf(G - 1, t)
            xf_lo(G - 1)
            gate_out(G - 1)

            step = [0]

            def then(ins):
                step[0] += 1
                ins.then_inc(route, 1)
                dve.wait_ge(route, step[0])

            def wide(v, n=E):
                return v.unsqueeze(2).to_broadcast([R, TILES, n])

            lg = logits[0:R, :, :]
            mx, tot, inv, m1, i1, m2, i2 = (sc8[0:R, k, :] for k in range(7))
            dve.wait_ge(back_out, 4 * G)
            dve.wait_ge(scores_ready, 8 * G)
            then(V.tensor_reduce(mx, lg, AX.X, ALU.max))
            V.tensor_tensor(rt(0), lg, wide(mx), ALU.subtract).then_inc(route_exp_in, 1)
            dve.wait_ge(route_exp, 1)
            then(V.tensor_reduce(tot, rt(1), AX.X, ALU.add))
            then(V.reciprocal(inv, tot))
            then(V.tensor_tensor(rt(1), rt(1), wide(inv), ALU.mult))
            gb = gbrow[0:R, :].unsqueeze(1).to_broadcast([R, TILES, E])
            then(V.tensor_tensor(rt(2), rt(1), gb, ALU.add))
            sg = rt(2).rearrange("p t (g e) -> p t g e", g=4)
            V.tensor_tensor(rg(0), sg[:, :, :, 0], sg[:, :, :, 1], ALU.max)
            V.tensor_tensor(rg(1), sg[:, :, :, 0], sg[:, :, :, 1], ALU.min)
            V.tensor_tensor(rg(2), sg[:, :, :, 2], sg[:, :, :, 3], ALU.max)
            then(V.tensor_tensor(rg(3), sg[:, :, :, 2], sg[:, :, :, 3], ALU.min))
            V.tensor_tensor(rg(4), rg(0), rg(2), ALU.max)
            V.tensor_tensor(rg(5), rg(0), rg(2), ALU.min)
            then(V.tensor_tensor(rg(6), rg(1), rg(3), ALU.max))
            then(V.tensor_tensor(rg(5), rg(5), rg(6), ALU.max))
            then(V.tensor_tensor(rg(0), rg(4), rg(5), ALU.add))
            then(V.tensor_copy(rg(1), small[0:R, 17:21].unsqueeze(1).to_broadcast([R, TILES, 4])))
            for d in range(1, 4):
                won = rg(2)[:, :, 0:4 - d]
                then(V.tensor_tensor(won, rg(0)[:, :, 0:4 - d], rg(0)[:, :, d:4], ALU.is_ge))
                then(V.tensor_tensor(rg(1)[:, :, d:4], rg(1)[:, :, d:4], won, ALU.add))
                then(V.tensor_tensor(rg(1)[:, :, 0:4 - d], rg(1)[:, :, 0:4 - d], won, ALU.subtract))
            then(V.tensor_scalar(rg(3), rg(1), 2.0, None, ALU.is_lt))
            then(V.tensor_scalar(rg(4), rg(3), 1.0, OUT, ALU.subtract, ALU.mult))
            keep, pen = (rg(k).unsqueeze(3).to_broadcast([R, TILES, 4, 4]) for k in (3, 4))
            s3 = rt(3).rearrange("p t (g e) -> p t g e", g=4)
            then(V.tensor_tensor(s3, sg, keep, ALU.mult))
            then(V.tensor_tensor(s3, s3, pen, ALU.add))
            iota = small[0:R, 1:17].unsqueeze(1).to_broadcast([R, TILES, E])
            for m, i, pick in ((m1, i1, rt(6)), (m2, i2, rt(7))):
                then(V.tensor_reduce(m, rt(3), AX.X, ALU.max))
                then(V.tensor_tensor(rt(4), rt(3), wide(m), ALU.is_equal))
                then(V.scalar_tensor_tensor(rt(5), rt(4), -float(E), iota, ALU.mult, ALU.add))
                then(V.tensor_reduce(i, rt(5), AX.X, ALU.min))
                then(V.tensor_tensor(pick, rt(5), wide(i), ALU.is_equal))
                then(V.scalar_tensor_tensor(rt(3), pick, -3.0 * OUT, rt(3), ALU.mult, ALU.add))
            then(V.tensor_tensor(rt(4), rt(6), rt(7), ALU.add))
            V.memset(comb[:, :, E:NE], 1.0)
            then(V.tensor_tensor(comb[0:R, :, 0:E], rt(4), rt(1), ALU.mult))
            then(V.tensor_scalar(comb12[0:R, :, :], comb[0:R, :, :], 1.0 / (WS * WS), None, ALU.mult))
            assert step[0] == ROUTE_STEPS, step[0]

            def gate_up(g, e):
                dve.wait_ge(silu_done, done(NE, g, e))
                V.scalar_tensor_tensor(gated[:, e % 3, :], proj_ps[e % 2][:, N2:2 * N2], b13col[:, 1, e:e + 1],
                                       silu[:, e % 2, :], ALU.add, ALU.mult).then_inc(gated_done, 1)

            def gated_lo(g, e):
                dve.wait_ge(g_hi, done(NE, g, e))
                V.tensor_tensor(gp[:, e % 3, 1, :], gated[:, e % 3, :], gp[:, e % 3, 0, :],
                                ALU.subtract).then_inc(g_lo, 1)

            def add_expert(g, e):
                dve.wait_ge(y_ready, done(NE, g, e))
                if e == 0:
                    dve.wait_ge(be2_added, g + 1)
                else:
                    dve.wait_ge(y_added, done(NE, g, e - 1))
                for t in range(2):
                    h = hrows[0:R, 2 * g + t, :]
                    ins = V.scalar_tensor_tensor(h, score_ps[e % 2][0:R, t * D:(t + 1) * D],
                                                 comb12[0:R, 2 * g + t, e:e + 1], h, ALU.mult, ALU.add)
                ins.then_inc(y_added, 1)

            def experts(g, first):
                V.tensor_copy(comb_now[0:R, :, :], comb[0:R, bass.ds(2 * g, 2), :]).then_inc(comb_now_in, 1)
                for e in range(NE):
                    gate_up(g, e)
                    if e > 0:
                        gated_lo(g, e - 1)
                    elif not first:
                        gated_lo(g - 1, NE - 1)
                    if e >= 2:
                        add_expert(g, e - 2)
                    elif not first:
                        add_expert(g - 1, NE - 2 + e)
                    if e == 1:
                        if not first:
                            finish(g - 1)
                        dve.wait_ge(be2_ready, g + 1)
                        rows = hrows[0:R, bass.ds(2 * g, 2), :]
                        V.tensor_tensor(rows, o_ps[0:R, 0:2 * D].rearrange("p (t d) -> p t d", t=2), rows,
                                        ALU.add).then_inc(be2_added, 1)

            def finish(g):
                dve.wait_ge(y_added, done(NE, g, NE - 1))
                V.memset(scrap[:, 1:2], 0.0).then_inc(rows_final, 1)

            experts(0, True)
            with dve.Fori(1, G) as g:
                experts(g, False)
            gated_lo(G - 1, NE - 1)
            add_expert(G - 1, NE - 2)
            add_expert(G - 1, NE - 1)
            finish(G - 1)

        @block.gpsimd
        def _(pool):
            Q = nc.gpsimd

            def normalise(g, u):
                pool.wait_ge(rinv_done, done(8, g, u))
                Q.tensor_tensor(probs[0:R, u % 3], probs[0:R, u % 3], rinv[0:R, u, :].unsqueeze(2).to_broadcast([R, HU, R]),
                                ALU.mult).then_inc(probs_ready, 1)

            def pw(n, k):
                return power[0:n, k:k + 1]

            def pixel_rstd(g, t):
                pool.wait_ge(x_moments, done(2, g, t))
                Q.tensor_tensor(xrs[0:PR, t, 0:1], xmv[0:PR, t, 1:2], pw(PR, 3), ALU.add).then_inc(px, 1)
                pool.wait_ge(px, done(2, g, t))
                Q.tensor_tensor(xrs[0:PR, t, 1:2], xrs[0:PR, t, 0:1], pw(PR, 0), ALU.pow).then_inc(x_rstd, 1)

            def token_rstd(g, t):
                pool.wait_ge(y_moments, done(2, g, t))
                Q.tensor_tensor(yrs[0:R, t, 0:1], ymv[0:R, t, 1:2], pw(R, 3), ALU.add).then_inc(py, 1)
                pool.wait_ge(py, 2 * done(2, g, t) - 1)
                Q.tensor_tensor(yrs[0:R, t, 1:2], yrs[0:R, t, 0:1], pw(R, 0), ALU.pow).then_inc(py, 1)
                pool.wait_ge(py, 2 * done(2, g, t))
                Q.tensor_tensor(yrs[0:R, t, 2:3], yrs[0:R, t, 1:2], small[0:R, 0:1], ALU.mult).then_inc(y_rstd, 1)

            def row_scale(g, t):
                pool.wait_ge(h_moments, done(2, g, t))
                s = [hrs[0:R, t, k:k + 1] for k in range(8)]
                var = hmv[0:R, t, 1:2]
                base = 5 * (done(2, g, t) - 1)
                Q.tensor_tensor(s[0], var, pw(R, 3), ALU.add)
                Q.tensor_tensor(s[2], var, pw(R, 1), ALU.pow).then_inc(ph, 1)
                pool.wait_ge(ph, base + 1)
                Q.tensor_tensor(s[1], s[0], pw(R, 0), ALU.pow).then_inc(ph, 1)
                pool.wait_ge(ph, base + 2)
                Q.tensor_tensor(s[3], s[2], s[1], ALU.mult).then_inc(ph, 1)
                pool.wait_ge(ph, base + 3)
                Q.tensor_tensor(s[6], s[1], pw(R, 4), ALU.mult)
                Q.tensor_scalar(s[4], s[3], float(D) ** 0.5, 1e-12, ALU.mult, ALU.max).then_inc(ph, 1)
                pool.wait_ge(ph, base + 4)
                Q.tensor_tensor(s[5], s[4], pw(R, 2), ALU.pow).then_inc(ph, 1)
                pool.wait_ge(ph, base + 5)
                Q.tensor_tensor(s[7], s[6], s[5], ALU.mult).then_inc(h_scale, 1)

            def last_rstd(g, t):
                pool.wait_ge(f_moments, done(2, g, t))
                Q.tensor_tensor(frs[0:R, t, 0:1], fmv[0:R, t, 1:2], pw(R, 3), ALU.add).then_inc(pf, 1)
                pool.wait_ge(pf, done(2, g, t))
                Q.tensor_tensor(frs[0:R, t, 1:2], frs[0:R, t, 0:1], pw(R, 0), ALU.pow).then_inc(f_rstd, 1)

            def body(g, first, last):
                if not first:
                    normalise(g - 1, 7)
                    last_rstd(g - 1, 0)
                    last_rstd(g - 1, 1)
                if not last:
                    pixel_rstd(g + 1, 0)
                    pixel_rstd(g + 1, 1)
                for u in range(UNITS - 1):
                    normalise(g, u)
                    if not last:
                        if u == 3:
                            token_rstd(g + 1, 0)
                        if u == 4:
                            row_scale(g + 1, 0)
                            token_rstd(g + 1, 1)
                        if u == 5:
                            row_scale(g + 1, 1)

            pool.wait_ge(prep, 7)
            for t in range(2):
                pixel_rstd(0, t)
            for t in range(2):
                token_rstd(0, t)
            for t in range(2):
                row_scale(0, t)
            body(0, True, False)
            with pool.Fori(1, G - 1) as g:
                body(g, False, False)
            body(G - 1, False, True)
            normalise(G - 1, 7)
            for t in range(2):
                last_rstd(G - 1, t)


_INS = ['x', 'L0_tok_cls_token', 'L0_tok_cls_pos_embedding', 'L0_tok_ln1_g', 'L0_tok_ln1_b', 'L0_tok_W', 'L0_tok_bias',
        'L0_tok_ln2_g', 'L0_tok_ln2_b', 'L0_attn_gamma', 'L0_attn_w_qkv', 'L0_attn_w_out', 'L0_ffn_gate_w', 'L0_ffn_gate_b',
        'L0_ffn_We1', 'L0_ffn_be1', 'L0_ffn_We2', 'L0_ffn_be2', 'L0_ffn_We3', 'L0_ffn_be3', 'L0_ffn_ws1', 'L0_ffn_bs1',
        'L0_ffn_ws2', 'L0_ffn_bs2', 'L0_ffn_ws3', 'L0_ffn_bs3']


def kernel(**inputs):
    import numpy as _np
    import concourse.bacc as _bacc
    from concourse import mybir as _mybir
    from concourse.bass_utils import run_bass_kernel_spmd as _run

    nc = _bacc.Bacc("TRN2", target_bir_lowering=False, num_devices=1)
    arrays, args = {}, {}
    for name, value in [(n, inputs[n]) for n in _INS] + list(constants().items()):
        v = lay_out(name, _np.asarray(value))
        arrays[f"in_{name}_dram"] = v
        args[name] = nc.dram_tensor(f"in_{name}_dram", v.shape, _mybir.dt.from_np(v.dtype), kind="ExternalInput").ap()
    out = nc.dram_tensor("out_0_dram", (B, SEQ, D), _mybir.dt.float32, kind="ExternalOutput").ap()
    build(nc, args, out)
    r = _run(nc, [arrays], core_ids=[0])
    return r.results[0]["out_0_dram"]
```

```python
from contextlib import ExitStack

import numpy as np

import concourse.bass as bass
from concourse import mybir

F32 = mybir.dt.float32
F16 = mybir.dt.float16
ALU = mybir.AluOpType
ACT = mybir.ActivationFunctionType
AX = mybir.AxisListType

B, C, IMG, PATCH = 64, 3, 96, 16
HP = IMG // PATCH
NPATCH = HP * HP
SEQ = NPATCH + 1
D = 256
PD = C * PATCH * PATCH
HEADS, DH = 16, 64
DI = HEADS * DH
E, INTER = 16, 128
NE = E + 2
P = 128
KD = D // P
KP = PD // P
KI = DI // P
GI = 3
PR = GI * NPATCH
R = GI * SEQ
TILES = -(-B // GI)
LAST_B0 = B - GI
G = TILES // 2
N2 = 2 * R
UNITS = 8
HU = HEADS // 4
assert TILES == 2 * G and 3 * (TILES - 1) > LAST_B0

EPS = 1e-5
WS = 64.0
PS = 256.0
QS, KS = 2.0 ** -7, 2.0 ** -8
assert QS * KS * WS * WS == DH ** -0.5
OUT = 1e30
MOST = TILES * R
NB = (2 * MOST + E * (P - 1)) // P
STEPS = 6
KMAX = -(-MOST // P)
MID = MOST // 2
assert NB % STEPS == 0 and MID < 2048
BIG = 32768.0


def constants():
    om = np.arange(D // 4, dtype=np.float32) / np.float32(D // 4 - 1)
    om = (np.float32(1.0) / np.power(np.float32(10000.0), om)).astype(np.float32)
    y, x = np.meshgrid(np.arange(HP), np.arange(HP), indexing="ij")
    y = (y.reshape(-1)[:, None] * om[None, :]).astype(np.float32)
    x = (x.reshape(-1)[:, None] * om[None, :]).astype(np.float32)
    pe = np.concatenate((np.sin(x), np.cos(x), np.sin(y), np.cos(y)), axis=1).astype(np.float32)
    rows = np.zeros((P, D), np.float32)
    rows[:PR] = np.tile(pe, (GI, 1))
    img = np.array([r // NPATCH if r < PR else r - PR for r in range(R)])
    own = (img[None, :] == np.arange(GI)[:, None]).astype(np.float32)
    ml = np.zeros((P, R), np.float16)
    mr = np.zeros((P, HU * R), np.float16)
    for base in (0, 64):
        ml[base:base + GI] = own * BIG
        mr[base:base + GI] = np.tile(-(1 - own) * BIG, (1, HU))
    small = np.zeros((P, 24), np.float32)
    small[:, 0] = np.arange(P) < PR
    small[:, 1:17] = np.arange(E) + E
    small[:, 17:21] = np.arange(3, -1, -1)
    route = np.zeros((P, 256 + KMAX + NB + P + TILES), np.float32)
    e = np.arange(E)
    route[:, 0:256] = (e[None, :] < e[:, None]).astype(np.float32).reshape(1, -1)
    route[:, 256:256 + KMAX] = np.arange(KMAX) * P
    route[:, 256 + KMAX:256 + KMAX + NB] = np.arange(NB)
    route[:, 256 + KMAX + NB:256 + KMAX + NB + P] = np.arange(P)
    route[:, 256 + KMAX + NB + P:] = np.arange(TILES)[None, :] * R + np.arange(P)[:, None] - MID
    tri = np.zeros((P, 2, R), np.float16)
    tri[:, 0] = np.arange(P)[:, None] < np.arange(R)[None, :]
    tri[:, 1] = 1
    return {"c_route": route, "c_tri": tri, "c_pe": rows, "c_ident": np.eye(P, dtype=np.float32), "c_maskl": ml, "c_maskr": mr, "c_small": small}


def lay_out(name, v):
    if name == "x":
        v = v.reshape(B, C, HP, PATCH, HP, PATCH).transpose(0, 2, 4, 3, 5, 1).reshape(B * NPATCH, PD)
    elif name in ("L0_tok_ln1_g", "L0_tok_ln1_b", "L0_attn_gamma", "L0_ffn_bs1", "L0_ffn_bs3"):
        v = v.reshape(-1, P).T
    elif name in ("L0_ffn_gate_w", "L0_ffn_be1", "L0_ffn_be3"):
        v = v.T
    return np.ascontiguousarray(v)


def done(per, g, k):
    return per * g + (k + 1)


def build(nc, a, out):
    x = a["x"]
    ctx = ExitStack()
    with ctx:
        def sb(name, shape, dt=F32):
            return ctx.enter_context(nc.sbuf_tensor(name, shape, dt))

        def bank(name, shape, dt=F32):
            return ctx.enter_context(nc.psum_tensor(name, shape, dt))

        def sem(name):
            return ctx.enter_context(nc.semaphore(name))

        wtok = sb("wtok", [P, 2, KP, D], F16)
        wqkv = sb("wqkv", [P, 2, KD, 3 * DI], F16)
        wout = sb("wout", [P, 2, KI, D], F16)
        w13 = sb("w13", [P, 2, NE, KD, 2 * INTER], F16)
        w2 = sb("w2", [P, 2, NE, D], F16)
        wgate = sb("wgate", [P, 2, KD, E], F16)

        ident = sb("ident", [P, P])
        maskl = sb("maskl", [P, R], F16)
        maskr = sb("maskr", [P, HU * R], F16)
        small = sb("small", [P, 24])
        addrow = sb("addrow", [P, D])
        g2row = sb("g2row", [P, D])
        biasrow = sb("biasrow", [P, D])
        g1col = sb("g1col", [P, KP])
        b1col = sb("b1col", [P, KP])
        gamcol = sb("gamcol", [P, KD])
        gatest = sb("gatest", [P, KD, E])
        gbrow = sb("gbrow", [P, E])
        b13col = sb("b13col", [P, 2, NE])
        be2row = sb("be2row", [NE, D])
        shcol = sb("shcol", [P, 2, 2])
        rtab = sb("rtab", [P, 256 + KMAX + NB + P + TILES])
        before = rtab[0:R, 0:256].rearrange("p (a b) -> p a b", a=E)
        full = rtab[0:R, 256:256 + KMAX]
        iota_b = rtab[0:R, 256 + KMAX:256 + KMAX + NB]
        iota_s = rtab[0:R, 256 + KMAX + NB:256 + KMAX + NB + P]
        rowid = rtab[0:R, 256 + KMAX + NB + P:256 + KMAX + NB + P + TILES]
        tri = sb("tri", [P, 2, R], F16)
        power = sb("power", [P, 5])
        scrap = sb("scrap", [P, 15])

        hrows = sb("hrows", [P, TILES, D])
        xft = sb("xft", [P, 2, KD, N2], F16)
        logits = sb("logits", [P, TILES, E])
        stage = hrows[:, 4:TILES, :].rearrange("p t d -> p (t d)")
        pair = sb("pair", [P, 1536])
        pair13 = pair[:, 0:1024].rearrange("p (e c n) -> p e c n", e=2, c=KD)
        pair2 = pair[:, 1024:1536].rearrange("p (e d) -> p e d", e=2)

        xin = sb("xin", [P, 2, PD])
        xt = sb("xt", [P, 2, 2, KP, R], F16)
        ytok = sb("ytok", [P, 2, D])
        xn = sb("xn", [P, 2, D])
        xf = sb("xf", [P, 2, D])
        xnt = sb("xnt", [P, 2, KD, N2], F16)
        qk = sb("qk", [P, 2, 2 * KI, N2], F16)
        arena = sb("arena", [P, 4 * DI + 6 * HU * R + 4 * HU * R + 2 * KI * N2], F16)
        a0, a1, a2, a3 = 4 * DI, 4 * DI + 6 * HU * R, 4 * DI + 10 * HU * R, 4 * DI + 10 * HU * R + 2 * KI * N2
        vv = arena[:, 0:a0].rearrange("p (a t n) -> p a t n", a=2, t=2)
        probs = arena[:, a0:a1].bitcast(F32).rearrange("p (s h r) -> p s h r", s=3, h=HU)
        pt = arena[:, a1:a2].rearrange("p (s a h r) -> p s a h r", s=2, a=2, h=HU)
        ot = arena[:, a2:a3].rearrange("p (a k n) -> p a k n", a=2, k=KI)
        sh_silu = sb("sh_silu", [P, 2, N2])
        sh_gated = sb("sh_gated", [P, 2, N2])
        sh_gp = sb("sh_gp", [P, 2, 2, N2], F16)
        early = arena[:, a2:a3].bitcast(F32)
        addrow2, addrow3 = early[:, 0:D], early[:, D:2 * D]
        brow, onerow = early[0:1, 2 * D:3 * D], early[0:1, 3 * D:3 * D + R]
        b1wide = early[:, 4 * D:4 * D + KP * R].rearrange("p (k r) -> p k r", k=KP)
        negmax = sb("negmax", [P, UNITS, HU])
        rowsum = sb("rowsum", [P, UNITS, HU])
        rinv = sb("rinv", [P, UNITS, HU])
        xst = sb("xst", [P, 2, 2, 6])
        xmv = sb("xmv", [P, 2, 2])
        yst = sb("yst", [P, 2, 6])
        ymv = sb("ymv", [P, 2, 2])
        hst = sb("hst", [P, 2, 6])
        hmv = sb("hmv", [P, 2, 2])
        fst = sb("fst", [P, 2, 6])
        fmv = sb("fmv", [P, 2, 2])
        xrs = sb("xrs", [P, 2, 2])
        yrs = sb("yrs", [P, 2, 3])
        hrs = sb("hrs", [P, 2, 8])
        frs = sb("frs", [P, 2, 2])

        qkf = qk[:, :, :, :].rearrange("p a c n -> p (a c n)").bitcast(F32)
        TE = TILES * E
        def rt(k):
            return qkf[0:R, k * TE:(k + 1) * TE].rearrange("p (t e) -> p t e", t=TILES)
        def rg(k):
            return qkf[0:R, 8 * TE + k * TILES * 4:8 * TE + (k + 1) * TILES * 4].rearrange("p (t g) -> p t g", t=TILES)
        comb = sb("comb", [P, TILES, NE])
        combt = sb("combt", [NE, N2])
        comb_now = sb("comb_now", [P, 2, NE])
        sc8 = sb("sc8", [P, 8, TILES])
        T2 = 2 * TILES
        picks = qkf[0:R, 6 * TE:8 * TE].rearrange("p (j e) -> p j e", j=T2)
        weights = sb("weights", [P, 2, TILES])
        slots = sb("slots", [P, TILES, 2], mybir.dt.int32)
        ids = sb("ids", [P, NB], mybir.dt.int32)
        blk_expert = sb("blk_expert", [1, 3 + NB], mybir.dt.int32)
        ids_now = sb("ids_now", [P, 2 * STEPS], mybir.dt.int32)
        slots_now = sb("slots_now", [P, 8], mybir.dt.int32)
        hot_b = arena[0:R, 0:T2 * NB].rearrange("p (j b) -> p j b", j=T2)
        hot_s = arena[0:R, T2 * NB:T2 * (NB + P)].rearrange("p (j s) -> p j s", j=T2)
        free = arena[0:R, T2 * (NB + P):].bitcast(F32)
        prod = free[:, 0:2 * TE].rearrange("p (j e) -> p j e", j=T2)
        past = free[:, 2 * TE:2 * TE + T2 * (KMAX - 1)].rearrange("p (j k) -> p j k", j=T2)
        held = sb("held", [P, 3 + STEPS])
        chosen = sb("chosen", [P, TE], F16)
        per_e = sb("per_e", [P, 3, E])
        place = sb("place", [P, 6, T2])
        xrow = xin[:, :, :].rearrange("p t n -> p (t n)").rearrange("p (s d) -> p s d", s=STEPS)
        yrow = qkf[:, 0:STEPS * D].rearrange("p (s d) -> p s d", s=STEPS)
        bsilu = qkf[:, 1536:1792].rearrange("p (s n) -> p s n", s=2)
        bgated = qkf[:, 1792:2176].rearrange("p (s n) -> p s n", s=3)
        bgp = qkf[:, 2176:2560].bitcast(F16).rearrange("p (s a n) -> p s a n", s=3, a=2)
        xrt = qkf[:, 2560:3072].bitcast(F16).rearrange("p (s a n) -> p s a n", s=2, a=2)
        ypick = arena[:, 0:16 * D].bitcast(F32).rearrange("p (s d) -> p s d", s=8)

        xf_dram = nc.dram_tensor("xf_rows", (MOST, D), F32, kind="Internal").ap()
        y_dram = nc.dram_tensor("y_rows", (NB * P, D), F32, kind="Internal").ap()

        proj_ps = [bank(f"proj{k}", [P, 512]) for k in range(2)]
        front_ps = bank("front", [P, 512])
        back_ps = bank("back", [P, 512])
        score_ps = [bank(f"score{k}", [P, 512]) for k in range(2)]
        pt_ps = bank("ptps", [P, 512])
        o_ps = bank("ops", [P, 512])

        const_in = sem("const_in")
        stage_in = [sem(f"stage_in{k}") for k in range(3)]
        w_hi, w_lo = sem("w_hi"), sem("w_lo")
        prep = sem("prep")
        bias_mm = sem("bias_mm")
        x_in = [sem(f"x_in{k}") for k in range(2)]
        proj_ready, proj_hi, proj_lo = sem("proj_ready"), sem("proj_hi"), sem("proj_lo")
        front_ready, front_hi, front_out = sem("front_ready"), sem("front_hi"), sem("front_out")
        back_ready, back_hi, back_out = sem("back_ready"), sem("back_hi"), sem("back_out")
        scores_ready, max_done, exp_done = sem("scores_ready"), sem("max_done"), sem("exp_done")
        rinv_done, probs_ready = sem("rinv_done"), sem("probs_ready")
        pt_ready, pt_hi, pt_lo = sem("pt_ready"), sem("pt_hi"), sem("pt_lo")
        pv_ready, ot_hi, ot_lo = sem("pv_ready"), sem("ot_hi"), sem("ot_lo")
        x_stats, x_moments, x_rstd, xhat_done = sem("x_stats"), sem("x_moments"), sem("x_rstd"), sem("xhat_done")
        y_stats, y_moments, y_rstd = sem("y_stats"), sem("y_moments"), sem("y_rstd")
        y_gain, h_done = sem("y_gain"), sem("h_done")
        h_stats, h_moments, h_scale, xn_done = sem("h_stats"), sem("h_moments"), sem("h_scale"), sem("xn_done")
        f_stats, f_moments, f_rstd, xf_done = sem("f_stats"), sem("f_moments"), sem("f_rstd"), sem("xf_done")
        px, py, ph, pf = sem("px_step"), sem("py_step"), sem("ph_step"), sem("pf_step")
        route, route_exp_in, route_exp = sem("route"), sem("route_exp_in"), sem("route_exp")
        comb_now_in = sem("comb_now_in")
        combt_ready, combt_out, be2_ready, be2_added = sem("combt_ready"), sem("combt_out"), sem("be2_ready"), sem("be2_added")
        pair_in, pair_hi, pair_lo = sem("pair_in"), sem("pair_hi"), sem("pair_lo")
        sh_ready, sh_tanh, sh_step, sh_gate_done, sh_hi, sh_lo = (sem("sh_" + n) for n in ("ready", "tanh", "step", "gate", "hi", "lo"))
        xf_stored = sem("xf_stored")
        rank_ready, ids_ready = sem("rank_ready"), sem("ids_ready")
        ids_copied, slots_copied = sem("ids_copied"), sem("slots_copied")
        row_in = [sem(f"row_in{k}") for k in range(STEPS)]
        row_turned, row_hi, row_lo = sem("row_turned"), sem("row_hi"), sem("row_lo")
        hid_ready, silu_done, gated_done, g_hi, g_lo = (sem(n) for n in ("hid_ready", "silu_done", "gated_done", "g_hi", "g_lo"))
        y_ready, y_out = sem("y_ready"), sem("y_out")
        y_stored = [sem(f"y_stored{k}") for k in range(STEPS)]
        pick_in = [sem(f"pick_in{k}") for k in range(8)]
        picked, summed = sem("picked"), sem("summed")
        rows_final = sem("rows_final")
        stored = sem("stored")

        def stage_at(slot, *shape):
            n = int(np.prod(shape))
            v = stage[:, slot * 1536:slot * 1536 + n]
            names = "abc"[:len(shape)]
            return v.rearrange(f"p ({' '.join(names)}) -> p {' '.join(names)}", **dict(zip(names, shape)))

        pieces = []

        def piece(loads, parts):
            pieces.append((loads, parts))

        def slot():
            return len(pieces) % 3

        v = stage_at(slot(), KP, D)
        piece([(v, a["L0_tok_W"].rearrange("(k p) d -> p k d", p=P))],
              [(v[:, k, :], wtok[:, 0, k, :], wtok[:, 1, k, :], ("g1", k)) for k in range(KP)])
        for k in range(KD):
            for half in range(2):
                v = stage_at(slot(), 1536)
                sl = slice(half * 1536, (half + 1) * 1536)
                piece([(v, a["L0_attn_w_qkv"][k * P:(k + 1) * P, sl])],
                      [(v, wqkv[:, 0, k, sl], wqkv[:, 1, k, sl], ("gam", k))])
        for half in range(2):
            v = stage_at(slot(), 4, D)
            sl = slice(4 * half, 4 * half + 4)
            piece([(v, a["L0_attn_w_out"].rearrange("(c p) d -> p c d", p=P)[:, sl, :])],
                  [(v, wout[:, 0, sl, :], wout[:, 1, sl, :], None)])
        v = stage_at(slot(), 1536)
        v13 = v[:, 0:1024].rearrange("p (e c n) -> p e c n", e=2, c=KD)
        v2 = v[:, 1024:1536].rearrange("p (e d) -> p e d", e=2)
        loads = [(v2, a["L0_ffn_ws2"].rearrange("(m i) d -> i m d", m=2))]
        for j in range(2):
            for n, name in enumerate(("ws1", "ws3")):
                loads.append((v13[:, j, :, n * INTER:(n + 1) * INTER],
                              a["L0_ffn_" + name][:, j * INTER:(j + 1) * INTER].rearrange("(c p) i -> p c i", p=P)))
        piece(loads, [(v13, w13[:, 0, E:NE], w13[:, 1, E:NE], None), (v2, w2[:, 0, E:NE, :], w2[:, 1, E:NE, :], None)])

        def landed(k):
            return stage_in[k % 3], 16 * sum(len(pieces[j][0]) for j in range(k % 3, k + 1, 3))

        block = ctx.enter_context(nc.Block())

        def experts_of(turn, engine, first, n):
            _, regs = nc.values_load_multi_w_load_instructions(
                blk_expert[0:1, bass.ds(STEPS * turn + first, n)], engines=[engine], min_val=0, max_val=E - 1,
                skip_runtime_bounds_check_because="the routing takes the minimum with E - 1")
            return regs

        def behind(turn, i, back):
            return (turn, i - back) if i >= back else (turn - 1, STEPS + i - back)

        CHOSEN, PLACED, ROUTED = 38, 55, 59
        PREP = 9

        NCONST = 23

        @block.sync
        def _(sp):
            n = [0]

            def const(dst, src):
                n[0] += 1
                sp.dma_start(dst, src, allow_slow_non_contiguous=True).then_inc(const_in, 16)

            const(g1col[:, :], a["L0_tok_ln1_g"])
            const(b1col[:, :], a["L0_tok_ln1_b"])
            const(gamcol[:, :], a["L0_attn_gamma"])
            def load_x(b0, t):
                sp.dma_start(xin[0:PR, t, :], x[bass.ds(b0 * NPATCH, PR), :]).then_inc(x_in[t], 16)

            load_x(0, 0)
            load_x(GI, 1)
            for dst, src in pieces[0][0]:
                sp.dma_start(dst, src).then_inc(stage_in[0], 16)
            sp.wait_ge(prep, 1)
            const(ident[:, :], a["c_ident"])
            const(maskl[:, :], a["c_maskl"])
            const(maskr[:, :], a["c_maskr"])
            const(small[:, :], a["c_small"])
            const(rtab[:, :], a["c_route"])
            const(tri[:, :, :], a["c_tri"])
            const(addrow[:, :], a["c_pe"])
            const(addrow2[0:PR, :], a["L0_tok_ln2_b"].rearrange("(o d) -> o d", o=1).to_broadcast([PR, D]))
            const(addrow2[PR:R, :], a["L0_tok_cls_token"].rearrange("a b d -> (a b) d").to_broadcast([GI, D]))
            const(addrow3[PR:R, :], a["L0_tok_cls_pos_embedding"].rearrange("a b d -> (a b) d").to_broadcast([GI, D]))
            const(g2row[0:R, :], a["L0_tok_ln2_g"].rearrange("(o d) -> o d", o=1).to_broadcast([R, D]))
            const(brow[:, :], a["L0_tok_bias"].rearrange("(o d) -> o d", o=1))
            const(gatest[:, :, :], a["L0_ffn_gate_w"].rearrange("(k p) e -> p k e", p=P))
            const(gbrow[0:R, :], a["L0_ffn_gate_b"].rearrange("(o e) -> o e", o=1).to_broadcast([R, E]))
            const(b13col[:, 0, 0:E], a["L0_ffn_be1"])
            const(b13col[:, 1, 0:E], a["L0_ffn_be3"])
            const(b13col[:, 0, E:NE], a["L0_ffn_bs1"])
            const(b13col[:, 1, E:NE], a["L0_ffn_bs3"])
            const(be2row[0:E, :], a["L0_ffn_be2"])
            const(be2row[E:E + 1, :], a["L0_ffn_bs2"].rearrange("(o d) -> o d", o=1))

            for k in (1, 2):
                for dst, src in pieces[k][0]:
                    sp.dma_start(dst, src).then_inc(stage_in[k], 16)
            for k in range(3, len(pieces)):
                sp.wait_ge(w_lo, k - 2)
                sp.wait_ge(w_hi, k - 2)
                for dst, src in pieces[k][0]:
                    sp.dma_start(dst, src).then_inc(stage_in[k % 3], 16)

            with sp.Fori(4, 4 + 7 * (G - 2), 7) as turned:
                sp.wait_ge(const_in, 16)
                sp.wait_ge(front_ready, turned)
                g = (turned - 4) // 7 + 1
                load_x(2 * GI * g, 0)
                load_x(2 * GI * g + GI, 1)
            sp.wait_ge(front_ready, done(7, G - 2, 3))
            load_x(2 * GI * (G - 1), 0)
            load_x(LAST_B0, 1)

            flat = out.rearrange("b s d -> (b s) d")
            cls = out[:, 0, :]

            def store(tile, b0, first=0):
                for im in range(first, GI):
                    sp.dma_start(flat[bass.ds((b0 + im) * SEQ + 1, NPATCH), :],
                                 hrows[im * NPATCH:(im + 1) * NPATCH, tile, :]).then_inc(stored, 16)
                sp.dma_start(cls[bass.ds(b0 + first, GI - first), :], hrows[PR + first:R, tile, :]).then_inc(stored, 16)

            with sp.Fori(1, G) as ready:
                sp.wait_ge(const_in, 16)
                sp.wait_ge(rows_final, ready)
                g = ready - 1
                store(2 * g, 2 * GI * g)
                store(2 * g + 1, 2 * GI * g + GI)
            sp.wait_ge(rows_final, G)
            store(TILES - 2, 2 * GI * (G - 1))
            store(TILES - 1, LAST_B0, first=GI * (TILES - 1) - LAST_B0)
            sp.wait_ge(stored, 16 * ((1 + GI) * TILES - (GI * (TILES - 1) - LAST_B0)))
            assert n[0] == NCONST, n[0]

        @block.tensor
        def _(pe):
            def mm3(dst, lh, rh, first, last, **kw):
                pe.matmul(dst, lh[0], rh[0], start=first, stop=False, **kw)
                pe.matmul(dst, lh[0], rh[1], start=False, stop=False, **kw)
                return pe.matmul(dst, lh[1], rh[0], start=False, stop=last, **kw)

            pe.wait_ge(prep, 4)
            pe.wait_ge(*landed(0))
            v0 = stage_at(0, KP, D)
            for k in range(KP):
                pe.matmul(back_ps[0:R, 0:D], b1wide[:, k, :], v0[:, k, :], start=k == 0, stop=False)
            pe.matmul(back_ps[0:R, 0:D], onerow[:, :], brow[:, :], start=False, stop=True).then_inc(bias_mm, 1)

            def project(g, s):
                if s == 0:
                    pe.wait_ge(front_out, done(7, g, 6))
                if not (isinstance(g, int) and g == 0 and s < 2):
                    pe.wait_ge(proj_lo, done(12, g, s - 2))
                if s >= 10 and not (isinstance(g, int) and g == 0):
                    pe.wait_ge(sh_gate_done, done(2, g - 1, s - 10))
                bk = proj_ps[s % 2]
                if s < 8:
                    for j in range(2):
                        cs = slice((2 * s + j) * P, (2 * s + j + 1) * P)
                        for k in range(KD):
                            ins = mm3(bk[:, j * N2:(j + 1) * N2], (wqkv[:, 0, k, cs], wqkv[:, 1, k, cs]),
                                      (xnt[:, 0, k, :], xnt[:, 1, k, :]), k == 0, k == KD - 1)
                else:
                    t, half = (s - 8) // 2, s % 2
                    cs = slice(2 * DI + half * 512, 2 * DI + (half + 1) * 512)
                    ts = slice(t * R, (t + 1) * R)
                    for k in range(KD):
                        ins = mm3(bk[0:R, :], (xnt[:, 0, k, ts], xnt[:, 1, k, ts]),
                                  (wqkv[:, 0, k, cs], wqkv[:, 1, k, cs]), k == 0, k == KD - 1)
                ins.then_inc(proj_ready, 1)

            def scores(g, u):
                t, half, par = u // 4, u // 2 % 2, u % 2
                if u == 0:
                    pe.wait_ge(proj_lo, done(12, g, 7))
                if not (isinstance(g, int) and g == 0 and u < 2):
                    pe.wait_ge(exp_done, done(8, g, u - 2))
                bk = score_ps[u % 2]
                rows = slice(64 * par, 64 * par + 64)
                pe.matmul(bk[0:R, 0:HU * R], maskl[rows, :], maskr[rows, :], start=True, stop=False)
                for j in range(HU):
                    ch = 4 * half + j
                    ts = slice(t * R, (t + 1) * R)
                    ins = mm3(bk[0:R, j * R:(j + 1) * R],
                              (qk[rows, 0, ch, ts], qk[rows, 1, ch, ts]),
                              (qk[rows, 0, KI + ch, ts], qk[rows, 1, KI + ch, ts]), False, j == HU - 1)
                ins.then_inc(scores_ready, 1)

            def turn_probs(g, u):
                pe.wait_ge(probs_ready, done(8, g, u))
                if not (isinstance(g, int) and g == 0 and u == 0):
                    pe.wait_ge(pt_lo, done(8, g, u - 1))
                for j in range(HU):
                    ins = pe.transpose(pt_ps[0:R, j * R:(j + 1) * R], probs[0:R, u % 3, j, :], ident[0:R, 0:R])
                ins.then_inc(pt_ready, 1)

            def attend(g, u):
                t, half, par = u // 4, u // 2 % 2, u % 2
                if u in (0, 4):
                    pe.wait_ge(proj_lo, done(12, g, 9 + u // 2))
                pe.wait_ge(pt_lo, done(8, g, u))
                if par == 0 and not (isinstance(g, int) and g == 0 and u == 0):
                    pe.wait_ge(ot_lo, done(4, g, u // 2 - 1))
                for j in range(HU):
                    h = 2 * (4 * half + j) + par
                    hs = slice(h * DH, (h + 1) * DH)
                    ins = mm3(o_ps[64 * par:64 * par + 64, j * R:(j + 1) * R],
                              (vv[0:R, 0, t, hs], vv[0:R, 1, t, hs]),
                              (pt[0:R, u % 2, 0, j, :], pt[0:R, u % 2, 1, j, :]), True, True)
                ins.then_inc(pv_ready, 1)

            def turn_pixels(g, t, part):
                pe.wait_ge(xhat_done, done(2, g, t))
                if not (isinstance(g, int) and g == 0 and t == 0 and part == 0):
                    pe.wait_ge(front_out, done(7, g, 2 * t + part - 1))
                for j in range(3):
                    k = 3 * part + j
                    ins = pe.transpose(front_ps[:, j * PR:(j + 1) * PR], xin[0:PR, t, k * P:(k + 1) * P], ident[0:PR, 0:PR])
                ins.then_inc(front_ready, 1)

            def embed(g, t):
                pe.wait_ge(front_out, done(7, g, 3 + t))
                for k in range(KP):
                    ins = mm3(front_ps[0:R, 0:D], (xt[:, t, 0, k, :], xt[:, t, 1, k, :]),
                              (wtok[:, 0, k, :], wtok[:, 1, k, :]), k == 0, k == KP - 1)
                ins.then_inc(front_ready, 1)

            def turn_rows(g):
                pe.wait_ge(xn_done, done(2, g, 1))
                pe.wait_ge(front_out, done(7, g, 5))
                for k in range(KD):
                    for t in range(2):
                        ins = pe.transpose(front_ps[:, k * N2 + t * R:k * N2 + (t + 1) * R],
                                           xn[0:R, t, k * P:(k + 1) * P], ident[0:R, 0:R])
                ins.then_inc(front_ready, 1)

            def out_proj(g, t):
                pe.wait_ge(ot_lo, done(4, g, 2 * t + 1))
                if not (isinstance(g, int) and g == 0 and t == 0):
                    pe.wait_ge(back_out, done(5, g, t - 1))
                ts = slice(t * R, (t + 1) * R)
                for k in range(KI):
                    ins = mm3(back_ps[0:R, 0:D], (ot[:, 0, k, ts], ot[:, 1, k, ts]),
                              (wout[:, 0, k, :], wout[:, 1, k, :]), k == 0, k == KI - 1)
                ins.then_inc(back_ready, 1)

            def turn_xf(g):
                pe.wait_ge(xf_done, done(2, g, 1))
                pe.wait_ge(back_out, done(5, g, 1))
                for k in range(KD):
                    for t in range(2):
                        ins = pe.transpose(back_ps[:, k * N2 + t * R:k * N2 + (t + 1) * R],
                                           xf[0:R, t, k * P:(k + 1) * P], ident[0:R, 0:R])
                ins.then_inc(back_ready, 1)

            def gate(g):
                pe.wait_ge(back_out, done(5, g, 2))
                for t in range(2):
                    for k in range(KD):
                        cs = slice(t * R, (t + 1) * R)
                        ins = mm3(back_ps[0:R, t * E:(t + 1) * E], (xft[:, 0, k, cs], xft[:, 1, k, cs]),
                                  (wgate[:, 0, k, :], wgate[:, 1, k, :]), k == 0, k == KD - 1)
                ins.then_inc(back_ready, 1)

            def front(g):
                for t in range(2):
                    turn_pixels(g, t, 0)
                    turn_pixels(g, t, 1)
                embed(g, 0)
                embed(g, 1)
                turn_rows(g)

            def shared_hidden(g, j):
                if j == 0:
                    pe.wait_ge(back_out, done(5, g, 2))
                for n in range(2):
                    ws = slice(n * INTER, (n + 1) * INTER)
                    for k in range(KD):
                        ins = mm3(proj_ps[j][:, n * N2:(n + 1) * N2], (w13[:, 0, E + j, k, ws], w13[:, 1, E + j, k, ws]),
                                  (xft[:, 0, k, :], xft[:, 1, k, :]), k == 0, k == KD - 1)
                ins.then_inc(sh_ready, 1)

            def shared_down(g):
                pe.wait_ge(sh_lo, done(2, g, 1))
                pe.wait_ge(back_out, done(5, g, 3))
                for t in range(2):
                    ts = slice(t * R, (t + 1) * R)
                    for j in range(2):
                        ins = mm3(back_ps[0:R, t * D:(t + 1) * D], (sh_gp[:, j, 0, ts], sh_gp[:, j, 1, ts]),
                                  (w2[:, 0, E + j, :], w2[:, 1, E + j, :]), j == 0, j == 1)
                ins.then_inc(back_ready, 1)

            def body(g, first, last):
                if not first:
                    turn_probs(g - 1, 6)
                    attend(g - 1, 5)
                project(g, 0)
                if not first:
                    turn_probs(g - 1, 7)
                    attend(g - 1, 6)
                project(g, 1)
                project(g, 2)
                if not first:
                    attend(g - 1, 7)
                for s in range(3, 6):
                    project(g, s)
                if not first:
                    out_proj(g - 1, 0)
                if not last:
                    turn_pixels(g + 1, 0, 0)
                project(g, 6)
                if not last:
                    turn_pixels(g + 1, 0, 1)
                if not first:
                    out_proj(g - 1, 1)
                if not last:
                    turn_pixels(g + 1, 1, 0)
                project(g, 7)
                if not last:
                    turn_pixels(g + 1, 1, 1)
                project(g, 8)
                if not last:
                    embed(g + 1, 0)
                scores(g, 0)
                project(g, 9)
                if not first:
                    turn_xf(g - 1)
                scores(g, 1)
                if not last:
                    embed(g + 1, 1)
                for s in range(2, UNITS):
                    scores(g, s)
                    turn_probs(g, s - 2)
                    if s >= 3:
                        attend(g, s - 3)
                    if s == 2 and not first:
                        gate(g - 1)
                    if s in (2, 3) and not first:
                        pe.wait_ge(proj_lo, done(12, g, 6 + s))
                        shared_hidden(g - 1, s - 2)
                    if s in (4, 5):
                        project(g, 6 + s)
                    if s == 6 and not last:
                        turn_rows(g + 1)
                    if s == 7 and not first:
                        shared_down(g - 1)

            pe.wait_ge(prep, PREP)
            pe.wait_ge(w_lo, 1)
            front(0)
            pe.wait_ge(w_lo, len(pieces))
            pe.wait_ge(prep, PREP + 1)
            body(0, True, False)
            with pe.Fori(1, G - 2) as g:
                body(g, False, False)
            body(G - 2, False, False)
            body(G - 1, False, True)
            turn_probs(G - 1, 6)
            attend(G - 1, 5)
            turn_probs(G - 1, 7)
            attend(G - 1, 6)
            attend(G - 1, 7)
            out_proj(G - 1, 0)
            out_proj(G - 1, 1)
            turn_xf(G - 1)
            gate(G - 1)

            shared_hidden(G - 1, 0)
            shared_hidden(G - 1, 1)

            pe.wait_ge(route, CHOSEN)
            pe.matmul(score_ps[0][0:R, 0:TE], tri[0:R, 0, :], chosen[0:R, :], start=True, stop=False)
            for t in range(TILES - 1):
                later = TILES - 1 - t
                pe.matmul(score_ps[0][0:R, (t + 1) * E:TE], tri[0:R, 1, :],
                          chosen[0:R, t * E:(t + 1) * E].unsqueeze(1).to_broadcast([R, later, E]),
                          start=False, stop=t == TILES - 2)
            for t in range(TILES):
                ins = pe.matmul(score_ps[1][0:R, 0:E], tri[0:R, 1, :], chosen[0:R, t * E:(t + 1) * E],
                                start=t == 0, stop=t == TILES - 1)
            ins.then_inc(rank_ready, 1)
            shared_down(G - 1)
            pe.wait_ge(route, PLACED)
            for j in range(T2):
                ins = pe.matmul(pt_ps[:, 0:NB], hot_s[:, j, :], hot_b[:, j, :], start=j == 0, stop=j == T2 - 1)
            ins.then_inc(ids_ready, 1)

            def turn_block(b, i):
                pe.wait_ge(row_in[i % STEPS], 16 * (b + 1))
                if not (isinstance(b, int) and b == 0 and i < 2):
                    pe.wait_ge(row_lo, STEPS * b + i - 1)
                for k in range(KD):
                    ins = pe.transpose(score_ps[i % 2][:, k * P:(k + 1) * P], xrow[:, i, k * P:(k + 1) * P], ident[:, :])
                ins.then_inc(row_turned, 1)

            def hidden(b, i, ex):
                pe.wait_ge(row_lo, STEPS * b + i + 1)
                if not (isinstance(b, int) and b == 0 and i < 2):
                    pe.wait_ge(gated_done, STEPS * b + i - 1)
                for j in range(2):
                    for k in range(KD):
                        ws = slice(j * INTER, (j + 1) * INTER)
                        wide = lambda n: w13[:, n, bass.ds(ex, 1), k, ws].rearrange("p a n -> p (a n)")
                        xs = slice(k * P, (k + 1) * P)
                        ins = mm3(proj_ps[i % 2][:, j * P:(j + 1) * P], (wide(0), wide(1)),
                                  (xrt[:, i % 2, 0, xs], xrt[:, i % 2, 1, xs]), k == 0, k == KD - 1)
                ins.then_inc(hid_ready, 1)

            def down(b, i, ex):
                pe.wait_ge(g_lo, STEPS * b + i + 1)
                if not (isinstance(b, int) and b == 0 and i < 2):
                    pe.wait_ge(y_out, STEPS * b + i - 1)
                wide = lambda n: w2[:, n, bass.ds(ex, 1), :].rearrange("p a n -> p (a n)")
                ins = mm3((front_ps, back_ps)[i % 2][:, 0:D], (bgp[:, i % 3, 0, :], bgp[:, i % 3, 1, :]),
                          (wide(0), wide(1)), True, True)
                ins.then_inc(y_ready, 1)

            def blocks(b, first):
                ex = experts_of(b, mybir.EngineType.PE, 0, 3 + STEPS)
                for i in range(STEPS):
                    turn_block(b, i)
                    if i >= 1:
                        hidden(b, i - 1, ex[3 + i - 1])
                    elif not first:
                        hidden(b - 1, STEPS - 1, ex[2])
                    if i >= 3:
                        down(b, i - 3, ex[i])
                    elif not first:
                        down(b - 1, STEPS - 3 + i, ex[i])

            pe.wait_ge(route, ROUTED)
            blocks(0, True)
            with pe.Fori(1, NB // STEPS) as b:
                blocks(b, False)
            last = NB // STEPS - 1
            ex = experts_of(last, mybir.EngineType.PE, STEPS, 3)
            down(last, STEPS - 3, ex[0])
            hidden(last, STEPS - 1, ex[2])
            down(last, STEPS - 2, ex[1])
            down(last, STEPS - 1, ex[2])

            def last_bias(g, first):
                pe.wait_ge(comb_now_in, g + 1)
                if not first:
                    pe.wait_ge(be2_added, g)
                for t in range(2):
                    ins = pe.transpose(pt_ps[0:NE, t * R:(t + 1) * R], comb_now[0:R, t, :], ident[0:R, 0:R])
                ins.then_inc(combt_ready, 1)
                pe.wait_ge(combt_out, g + 1)
                for t in range(2):
                    ins = pe.matmul(o_ps[0:R, t * D:(t + 1) * D], combt[:, t * R:(t + 1) * R], be2row[:, :],
                                    start=True, stop=True)
                ins.then_inc(be2_ready, 1)

            last_bias(0, True)
            with pe.Fori(1, G) as g:
                last_bias(g, False)

        @block.scalar
        def _(act):
            def weights_hi(k):
                act.wait_ge(*landed(k))
                if k == 0:
                    act.wait_ge(prep, 3)
                for st, hi, _lo, scale in pieces[k][1]:
                    s = WS if scale is None else {"g1": g1col, "gam": gamcol}[scale[0]][:, scale[1]:scale[1] + 1]
                    ins = nc.scalar.activation(hi, st, ACT.Copy, scale=s)
                ins.then_inc(w_hi, 1)

            def pair_load(p):
                if not (isinstance(p, int) and p == 0):
                    act.wait_ge(pair_lo, p)
                es = bass.ds(2 * p, 2)
                for j in range(2):
                    for n, name in enumerate(("We1", "We3")):
                        src = a["L0_ffn_" + name][bass.ds(2 * p + j, 1), :, :].rearrange("e (c p) i -> p (e c) i", p=P)
                        act.dma_start(pair13[:, j, :, n * INTER:(n + 1) * INTER], src).then_inc(pair_in, 16)
                act.dma_start(pair2, a["L0_ffn_We2"][es].rearrange("e i d -> i e d")).then_inc(pair_in, 16)

            def pair_high(p):
                act.wait_ge(pair_in, 80 * (p + 1))
                es = bass.ds(2 * p, 2)
                nc.scalar.activation(w13[:, 0, es], pair13, ACT.Copy, scale=WS)
                nc.scalar.activation(w2[:, 0, es, :], pair2, ACT.Copy, scale=WS).then_inc(pair_hi, 1)

            def project_hi(g, s):
                act.wait_ge(proj_ready, done(12, g, s))
                if s < 8:
                    nc.scalar.activation(qk[:, 0, 2 * s:2 * s + 2, :],
                                         proj_ps[s % 2][:, 0:2 * N2].rearrange("p (a n) -> p a n", a=2),
                                         ACT.Copy, scale=QS if s < 4 else KS).then_inc(proj_hi, 1)
                else:
                    t, half = (s - 8) // 2, s % 2
                    nc.scalar.activation(vv[0:R, 0, t, half * 512:(half + 1) * 512], proj_ps[s % 2][0:R, :],
                                         ACT.Copy).then_inc(proj_hi, 1)

            def exps(g, u):
                act.wait_ge(max_done, done(8, g, u))
                for j in range(HU):
                    ins = nc.scalar.activation(probs[0:R, u % 3, j, :], score_ps[u % 2][0:R, j * R:(j + 1) * R], ACT.Exp,
                                               bias=negmax[0:R, u, j:j + 1],
                                               accum_out=rowsum[0:R, u, j:j + 1])
                ins.then_inc(exp_done, 1)

            def probs_hi(g, u):
                act.wait_ge(pt_ready, done(8, g, u))
                nc.scalar.activation(pt[0:R, u % 2, 0], pt_ps[0:R, 0:HU * R].rearrange("p (h r) -> p h r", h=HU),
                                     ACT.Copy, scale=PS).then_inc(pt_hi, 1)

            def attend_hi(g, w):
                t, half = w // 2, w % 2
                act.wait_ge(pv_ready, done(8, g, 2 * w + 1))
                nc.scalar.activation(ot[:, 0, 4 * half:4 * half + 4, t * R:(t + 1) * R],
                                     o_ps[:, 0:HU * R].rearrange("p (h r) -> p h r", h=HU),
                                     ACT.Copy, scale=1.0 / PS).then_inc(ot_hi, 1)

            def pixels_hi(g, t, part):
                act.wait_ge(front_ready, done(7, g, 2 * t + part))
                nc.scalar.activation(xt[:, t, 0, 3 * part:3 * part + 3, 0:PR],
                                     front_ps[:, 0:3 * PR].rearrange("p (k r) -> p k r", k=3),
                                     ACT.Copy).then_inc(front_hi, 1)

            def rows_hi(g):
                act.wait_ge(front_ready, done(7, g, 6))
                nc.scalar.activation(xnt[:, 0], front_ps[:, 0:KD * N2].rearrange("p (k n) -> p k n", k=KD),
                                     ACT.Copy).then_inc(front_hi, 1)

            def xf_hi(g):
                act.wait_ge(back_ready, done(5, g, 2))
                nc.scalar.activation(xft[:, 0],
                                     back_ps[:, 0:KD * N2].rearrange("p (k n) -> p k n", k=KD),
                                     ACT.Copy).then_inc(back_hi, 1)
                rows = xf_dram[bass.ds(g * N2, N2), :].rearrange("(t r) d -> r t d", t=2)
                act.dma_start(rows, xf[0:R, :, :]).then_inc(xf_stored, 16)

            def shared_tanh(g, j):
                act.wait_ge(sh_ready, done(2, g, j))
                nc.scalar.activation(sh_silu[:, j, :], proj_ps[j][:, 0:N2], ACT.Tanh, bias=shcol[:, 0, j:j + 1],
                                     scale=0.5 / WS).then_inc(sh_tanh, 1)

            def shared_hi(g, j):
                act.wait_ge(sh_gate_done, done(2, g, j))
                nc.scalar.activation(sh_gp[:, j, 0, :], sh_gated[:, j, :], ACT.Copy, scale=0.5 / WS).then_inc(sh_hi, 1)

            def body(g, first, last, pairs):
                if not first:
                    probs_hi(g - 1, 6)
                    attend_hi(g - 1, 2)
                project_hi(g, 0)
                if pairs:
                    pair_load(g - 1)
                if not first:
                    probs_hi(g - 1, 7)
                project_hi(g, 1)
                project_hi(g, 2)
                if not first:
                    attend_hi(g - 1, 3)
                for s in range(3, 6):
                    project_hi(g, s)
                if not last:
                    pixels_hi(g + 1, 0, 0)
                project_hi(g, 6)
                if not last:
                    pixels_hi(g + 1, 0, 1)
                    pixels_hi(g + 1, 1, 0)
                project_hi(g, 7)
                if not last:
                    pixels_hi(g + 1, 1, 1)
                project_hi(g, 8)
                exps(g, 0)
                project_hi(g, 9)
                if not first:
                    xf_hi(g - 1)
                exps(g, 1)
                if pairs:
                    pair_high(g - 1)
                for s in range(2, UNITS):
                    probs_hi(g, s - 2)
                    exps(g, s)
                    if s in (4, 6):
                        attend_hi(g, s // 2 - 2)
                    if s in (2, 3) and not first:
                        shared_tanh(g - 1, s - 2)
                    if s in (4, 5) and not first:
                        shared_hi(g - 1, s - 4)
                    if s in (5, 6):
                        project_hi(g, 5 + s)
                    if s == 6 and not last:
                        rows_hi(g + 1)

            weights_hi(0)
            for t in range(2):
                for part in range(2):
                    pixels_hi(0, t, part)
            for k in range(1, 5):
                weights_hi(k)
            rows_hi(0)
            for k in range(5, len(pieces)):
                weights_hi(k)
            act.wait_ge(prep, 5)
            nc.scalar.activation(wgate[:, 0], gatest[:, :, :], ACT.Copy, scale=WS).then_inc(w_hi, 1)
            body(0, True, False, False)
            with act.Fori(1, G - 2) as g:
                body(g, False, False, True)
            body(G - 2, False, False, False)
            body(G - 1, False, True, False)
            probs_hi(G - 1, 6)
            attend_hi(G - 1, 2)
            probs_hi(G - 1, 7)
            attend_hi(G - 1, 3)
            xf_hi(G - 1)
            for j in range(2):
                shared_tanh(G - 1, j)

            act.wait_ge(route_exp_in, 1)
            nc.scalar.activation(rt(1), rt(0), ACT.Exp).then_inc(route_exp, 1)
            for j in range(2):
                shared_hi(G - 1, j)

            def row_high(b, i):
                act.wait_ge(row_turned, STEPS * b + i + 1)
                nc.scalar.activation(xrt[:, i % 2, 0, :], score_ps[i % 2][:, 0:D], ACT.Copy).then_inc(row_hi, 1)

            def silus(b, i, ex):
                act.wait_ge(hid_ready, STEPS * b + i + 1)
                nc.scalar.activation(bsilu[:, i % 2, :], proj_ps[i % 2][:, 0:P], ACT.Silu,
                                     bias=b13col[:, 0, bass.ds(ex, 1)], scale=1.0 / WS).then_inc(silu_done, 1)

            def gated_hi(b, i):
                act.wait_ge(gated_done, STEPS * b + i + 1)
                if not (isinstance(b, int) and b == 0 and i < 3):
                    act.wait_ge(y_ready, STEPS * b + i - 2)
                nc.scalar.activation(bgp[:, i % 3, 0, :], bgated[:, i % 3, :], ACT.Copy).then_inc(g_hi, 1)

            def rows_out(b, i):
                act.wait_ge(y_ready, STEPS * b + i + 1)
                if not (isinstance(b, int) and b == 0):
                    act.wait_ge(y_stored[i], 16 * b)
                nc.scalar.activation(yrow[:, i, :], (front_ps, back_ps)[i % 2][:, 0:D], ACT.Copy,
                                     scale=1.0 / (WS * WS)).then_inc(y_out, 1)

            def store_rows(b, i):
                act.wait_ge(y_out, STEPS * b + i + 1)
                act.dma_start(y_dram[bass.ds((STEPS * b + i) * P, P), :], yrow[:, i, :]).then_inc(y_stored[i], 16)

            def blocks(b, first):
                ex = experts_of(b, mybir.EngineType.Activation, 2, STEPS)
                for i in range(STEPS):
                    row_high(b, i)
                    if i >= 1 or not first:
                        silus(*behind(b, i, 1), ex[i])
                    if i >= 2 or not first:
                        gated_hi(*behind(b, i, 2))
                    if i >= 3 or not first:
                        rows_out(*behind(b, i, 3))
                    if i >= 4 or not first:
                        store_rows(*behind(b, i, 4))

            act.wait_ge(route, ROUTED)
            blocks(0, True)
            with act.Fori(1, NB // STEPS) as b:
                blocks(b, False)
            end = NB // STEPS
            ex = experts_of(end, mybir.EngineType.Activation, 2, 1)
            gated_hi(*behind(end, 0, 2))
            rows_out(*behind(end, 0, 3))
            store_rows(*behind(end, 0, 4))
            silus(*behind(end, 0, 1), ex[0])
            gated_hi(*behind(end, 0, 1))
            store_rows(*behind(end, 0, 3))
            for back in (2, 1):
                rows_out(*behind(end, 0, back))
                store_rows(*behind(end, 0, back))

            def last_bias(g):
                act.wait_ge(combt_ready, g + 1)
                nc.scalar.activation(combt[:, :], pt_ps[0:NE, 0:N2], ACT.Copy).then_inc(combt_out, 1)

            last_bias(0)
            with act.Fori(1, G) as g:
                last_bias(g)

        @block.vector
        def _(dve):
            V = nc.vector
            V.memset(xt[:, :, :, :, PR:R], 0.0)
            V.memset(onerow[:, :], 1.0)
            V.memset(addrow3[:, :], 0.0)
            V.memset(power[:, 0:1], -0.5)
            V.memset(power[:, 1:2], 0.5)
            V.memset(power[:, 2:3], -1.0)
            V.memset(power[:, 3:4], EPS)
            V.memset(power[:, 4:5], float(D) ** 0.5)
            V.memset(blk_expert[:, 0:3], 0)
            V.memset(be2row[:, :], 0.0).then_inc(prep, 1)
            dve.wait_ge(const_in, 16 * NCONST)
            V.tensor_scalar(gamcol[:, :], gamcol[:, :], 1.0, WS, ALU.add, ALU.mult).then_inc(prep, 1)
            V.tensor_scalar(g1col[:, :], g1col[:, :], WS, None, ALU.mult).then_inc(prep, 1)
            V.tensor_copy(b1wide[:, :, :], b1col[:, :].unsqueeze(2).to_broadcast([P, KP, R])).then_inc(prep, 1)
            V.tensor_scalar(b13col[:, 1, :], b13col[:, 1, :], WS, None, ALU.mult).then_inc(prep, 1)
            V.tensor_tensor(addrow[0:R, :], addrow[0:R, :], addrow2[0:R, :], ALU.add).then_inc(prep, 1)
            dve.wait_ge(prep, 6)
            V.tensor_tensor(addrow[0:R, :], addrow[0:R, :], addrow3[0:R, :], ALU.add).then_inc(prep, 1)
            V.tensor_scalar(shcol[:, 0, :], b13col[:, 0, E:NE], 0.5, None, ALU.mult)
            V.tensor_scalar(shcol[:, 1, :], b13col[:, 0, E:NE], WS, None, ALU.mult).then_inc(prep, 1)
            dve.wait_ge(bias_mm, 1)
            V.tensor_copy(biasrow[0:R, :], back_ps[0:R, 0:D]).then_inc(prep, 1)

            def weights_lo(k):
                dve.wait_ge(w_hi, k + 1)
                for st, hi, lo, scale in pieces[k][1]:
                    s = WS if scale is None else {"g1": g1col, "gam": gamcol}[scale[0]][:, scale[1]:scale[1] + 1]
                    if len(st.shape) > 3:
                        merge = "p a b c -> p (a b c)"
                        st, hi, lo = st.rearrange(merge), hi.rearrange(merge), lo.rearrange(merge)
                    ins = V.scalar_tensor_tensor(lo, st, s, hi, ALU.mult, ALU.subtract)
                ins.then_inc(w_lo, 1)

            def pair_low(p):
                dve.wait_ge(pair_hi, p + 1)
                es = bass.ds(2 * p, 2)
                flat3 = lambda v: v.rearrange("p a b c -> p (a b c)")
                V.scalar_tensor_tensor(flat3(w13[:, 1, es]), flat3(pair13), WS, flat3(w13[:, 0, es]), ALU.mult, ALU.subtract)
                V.scalar_tensor_tensor(w2[:, 1, es, :], pair2, WS, w2[:, 0, es, :], ALU.mult, ALU.subtract).then_inc(pair_lo, 1)

            def project_lo(g, s):
                dve.wait_ge(proj_hi, done(12, g, s))
                if s < 8:
                    dst = lambda n: qk[:, n, 2 * s:2 * s + 2, :]
                    V.scalar_tensor_tensor(dst(1), proj_ps[s % 2][:, 0:2 * N2].rearrange("p (a n) -> p a n", a=2),
                                           QS if s < 4 else KS, dst(0), ALU.mult, ALU.subtract).then_inc(proj_lo, 1)
                else:
                    t, half = (s - 8) // 2, s % 2
                    cs = slice(half * 512, (half + 1) * 512)
                    V.tensor_tensor(vv[0:R, 1, t, cs], proj_ps[s % 2][0:R, :], vv[0:R, 0, t, cs],
                                    ALU.subtract).then_inc(proj_lo, 1)

            def row_max(g, u):
                dve.wait_ge(scores_ready, done(8, g, u))
                V.tensor_reduce(negmax[0:R, u, :], score_ps[u % 2][0:R, 0:HU * R].rearrange("p (h r) -> p h r", h=HU),
                                AX.X, ALU.max, negate=True).then_inc(max_done, 1)

            def row_inv(g, u):
                dve.wait_ge(exp_done, done(8, g, u))
                V.reciprocal(rinv[0:R, u, :], rowsum[0:R, u, :]).then_inc(rinv_done, 1)

            def probs_lo(g, u):
                dve.wait_ge(pt_hi, done(8, g, u))
                V.scalar_tensor_tensor(pt[0:R, u % 2, 1], pt_ps[0:R, 0:HU * R].rearrange("p (h r) -> p h r", h=HU), PS,
                                       pt[0:R, u % 2, 0], ALU.mult, ALU.subtract).then_inc(pt_lo, 1)

            def attend_lo(g, w):
                t, half = w // 2, w % 2
                dst = lambda n: ot[:, n, 4 * half:4 * half + 4, t * R:(t + 1) * R]
                dve.wait_ge(ot_hi, done(4, g, w))
                V.scalar_tensor_tensor(dst(1), o_ps[:, 0:HU * R].rearrange("p (h r) -> p h r", h=HU), 1.0 / PS,
                                       dst(0), ALU.mult, ALU.subtract).then_inc(ot_lo, 1)

            def pixel_stats(g, t):
                dve.wait_ge(x_in[t], 16 * g + 16)
                V.bn_stats(xst[0:PR, t, 0, :], xin[0:PR, t, 0:PD // 2])
                V.bn_stats(xst[0:PR, t, 1, :], xin[0:PR, t, PD // 2:PD]).then_inc(x_stats, 1)
                dve.wait_ge(x_stats, done(2, g, t))
                V.memset(scrap[:, 0 + t:1 + t], 0.0)
                V.bn_aggr(xmv[0:PR, t, :], xst[0:PR, t, :, :].rearrange("p a b -> p (a b)")).then_inc(x_moments, 1)

            def pixel_norm(g, t):
                dve.wait_ge(x_rstd, g + 1)
                V.tensor_scalar(xin[0:PR, t, :], xin[0:PR, t, :], xmv[0:PR, t, 0:1], xrs[0:PR, t, 1:2],
                                ALU.subtract, ALU.mult).then_inc(xhat_done, 1)

            def pixels_lo(g, t, part):
                dve.wait_ge(front_hi, done(5, g, 2 * t + part))
                dst = lambda n: xt[:, t, n, 3 * part:3 * part + 3, 0:PR]
                V.tensor_tensor(dst(1), front_ps[:, 0:3 * PR].rearrange("p (k r) -> p k r", k=3), dst(0),
                                ALU.subtract).then_inc(front_out, 1)

            def embed_out(g, t):
                dve.wait_ge(front_ready, done(7, g, 4 + t))
                V.scalar_tensor_tensor(ytok[0:R, t, :], front_ps[0:R, 0:D], 1.0 / WS, biasrow[0:R, :],
                                       ALU.mult, ALU.add).then_inc(front_out, 1)
                dve.wait_ge(front_out, done(7, g, 4 + t))
                V.memset(scrap[:, 2 + t:3 + t], 0.0)
                V.bn_stats(yst[0:R, t, :], ytok[0:R, t, :]).then_inc(y_stats, 1)

            def embed_moments(g, t):
                dve.wait_ge(y_stats, done(2, g, t))
                V.memset(scrap[:, 4 + t:5 + t], 0.0)
                V.bn_aggr(ymv[0:R, t, :], yst[0:R, t, :]).then_inc(y_moments, 1)

            def token_rows(g):
                dve.wait_ge(y_rstd, g + 1)
                for t in range(2):
                    V.scalar_tensor_tensor(ytok[0:R, t, :], ytok[0:R, t, :], ymv[0:R, t, 0:1], g2row[0:R, :],
                                           ALU.subtract, ALU.mult).then_inc(y_gain, 1)
                for t in range(2):
                    dve.wait_ge(y_gain, done(2, g, t))
                    V.scalar_tensor_tensor(hrows[0:R, 2 * g + t, :], ytok[0:R, t, :], yrs[0:R, t, 2:3], addrow[0:R, :],
                                           ALU.mult, ALU.add).then_inc(h_done, 1)

            def token_moments(g):
                for t in range(2):
                    dve.wait_ge(h_done, done(2, g, t))
                    V.memset(scrap[:, 6 + t:7 + t], 0.0)
                    V.bn_stats(hst[0:R, t, :], hrows[0:R, 2 * g + t, :]).then_inc(h_stats, 1)
                for t in range(2):
                    dve.wait_ge(h_stats, done(2, g, t))
                    V.memset(scrap[:, 8 + t:9 + t], 0.0)
                    V.bn_aggr(hmv[0:R, t, :], hst[0:R, t, :]).then_inc(h_moments, 1)

            def norm_rows(g, t):
                dve.wait_ge(h_scale, g + 1)
                V.tensor_scalar(xn[0:R, t, :], hrows[0:R, 2 * g + t, :], hmv[0:R, t, 0:1], hrs[0:R, t, 7:8],
                                ALU.subtract, ALU.mult).then_inc(xn_done, 1)

            def rows_lo(g):
                dve.wait_ge(front_hi, done(5, g, 4))
                V.tensor_tensor(xnt[:, 1], front_ps[:, 0:KD * N2].rearrange("p (k n) -> p k n", k=KD), xnt[:, 0],
                                ALU.subtract).then_inc(front_out, 1)

            def residual(g, t):
                h = hrows[0:R, 2 * g + t, :]
                dve.wait_ge(back_ready, done(5, g, t))
                V.scalar_tensor_tensor(h, back_ps[0:R, 0:D], 1.0 / (WS * WS), h, ALU.mult, ALU.add).then_inc(back_out, 1)
                dve.wait_ge(back_out, done(5, g, t))
                V.memset(scrap[:, 10 + t:11 + t], 0.0)
                V.bn_stats(fst[0:R, t, :], h).then_inc(f_stats, 1)
                dve.wait_ge(f_stats, done(2, g, t))
                V.memset(scrap[:, 12 + t:13 + t], 0.0)
                V.bn_aggr(fmv[0:R, t, :], fst[0:R, t, :]).then_inc(f_moments, 1)

            def norm_xf(g, t):
                dve.wait_ge(f_rstd, g + 1)
                if t == 0 and not (isinstance(g, int) and g == 0):
                    dve.wait_ge(xf_stored, 16 * g)
                V.tensor_scalar(xf[0:R, t, :], hrows[0:R, 2 * g + t, :], fmv[0:R, t, 0:1], frs[0:R, t, 1:2],
                                ALU.subtract, ALU.mult).then_inc(xf_done, 1)

            def xf_lo(g):
                dve.wait_ge(back_hi, g + 1)
                V.tensor_tensor(xft[:, 1], back_ps[:, 0:KD * N2].rearrange("p (k n) -> p k n", k=KD),
                                xft[:, 0], ALU.subtract).then_inc(back_out, 1)

            def gate_out(g):
                dve.wait_ge(back_ready, done(5, g, 3))
                V.tensor_scalar(logits[0:R, bass.ds(2 * g, 2), :], back_ps[0:R, 0:2 * E].rearrange("p (t e) -> p t e", t=2),
                                1.0 / WS, None, ALU.mult).then_inc(back_out, 1)

            def shared_gate(g, j):
                step = 2 * (done(2, g, j) - 1)
                dve.wait_ge(sh_tanh, done(2, g, j))
                V.tensor_scalar(sh_silu[:, j, :], sh_silu[:, j, :], 1.0, None, ALU.add).then_inc(sh_step, 1)
                dve.wait_ge(sh_step, step + 1)
                V.scalar_tensor_tensor(sh_silu[:, j, :], proj_ps[j][:, 0:N2], shcol[:, 1, j:j + 1], sh_silu[:, j, :],
                                       ALU.add, ALU.mult).then_inc(sh_step, 1)
                dve.wait_ge(sh_step, step + 2)
                V.scalar_tensor_tensor(sh_gated[:, j, :], proj_ps[j][:, N2:2 * N2], b13col[:, 1, E + j:E + j + 1],
                                       sh_silu[:, j, :], ALU.add, ALU.mult).then_inc(sh_gate_done, 1)

            def shared_lo(g, j):
                dve.wait_ge(sh_hi, done(2, g, j))
                V.scalar_tensor_tensor(sh_gp[:, j, 1, :], sh_gated[:, j, :], 0.5 / WS, sh_gp[:, j, 0, :],
                                       ALU.mult, ALU.subtract).then_inc(sh_lo, 1)

            def shared_add(g):
                rows = hrows[0:R, bass.ds(2 * g, 2), :]
                dve.wait_ge(back_ready, done(5, g, 4))
                V.scalar_tensor_tensor(rows, back_ps[0:R, 0:2 * D].rearrange("p (t d) -> p t d", t=2),
                                       1.0 / (WS * WS), rows, ALU.mult, ALU.add).then_inc(back_out, 1)

            def body(g, first, last, pairs):
                if not first:
                    row_inv(g - 1, 7)
                    probs_lo(g - 1, 6)
                    attend_lo(g - 1, 2)
                project_lo(g, 0)
                if not first:
                    probs_lo(g - 1, 7)
                project_lo(g, 1)
                if not last:
                    pixel_stats(g + 1, 0)
                project_lo(g, 2)
                if not first:
                    attend_lo(g - 1, 3)
                project_lo(g, 3)
                if not last:
                    pixel_stats(g + 1, 1)
                project_lo(g, 4)
                if not last:
                    pixel_norm(g + 1, 0)
                project_lo(g, 5)
                if not last:
                    pixel_norm(g + 1, 1)
                if not first:
                    residual(g - 1, 0)
                if not last:
                    pixels_lo(g + 1, 0, 0)
                project_lo(g, 6)
                if not last:
                    pixels_lo(g + 1, 0, 1)
                if not first:
                    residual(g - 1, 1)
                if not last:
                    pixels_lo(g + 1, 1, 0)
                project_lo(g, 7)
                if not last:
                    pixels_lo(g + 1, 1, 1)
                if not first:
                    norm_xf(g - 1, 0)
                    norm_xf(g - 1, 1)
                project_lo(g, 8)
                row_max(g, 0)
                if not last:
                    embed_out(g + 1, 0)
                    embed_moments(g + 1, 0)
                row_inv(g, 0)
                project_lo(g, 9)
                if not first:
                    xf_lo(g - 1)
                row_max(g, 1)
                if not last:
                    embed_out(g + 1, 1)
                    embed_moments(g + 1, 1)
                for s in range(2, UNITS):
                    row_inv(g, s - 1)
                    row_max(g, s)
                    probs_lo(g, s - 2)
                    if s in (4, 6):
                        attend_lo(g, s // 2 - 2)
                    if s == 2:
                        if not first:
                            gate_out(g - 1)
                        if not last:
                            token_rows(g + 1)
                    if s == 3:
                        if not last:
                            token_moments(g + 1)
                    if s in (3, 4) and not first:
                        shared_gate(g - 1, s - 3)
                    if s == 5:
                        project_lo(g, 10)
                        if not last:
                            for t in range(2):
                                norm_rows(g + 1, t)
                    if s in (5, 6) and not first:
                        shared_lo(g - 1, s - 5)
                    if s == 6:
                        project_lo(g, 11)
                        if not last:
                            rows_lo(g + 1)
                    if s == 7 and not first:
                        if pairs:
                            pair_low(g - 1)
                        shared_add(g - 1)

            weights_lo(0)
            for t in range(2):
                pixel_stats(0, t)
            for t in range(2):
                pixel_norm(0, t)
            for t in range(2):
                for part in range(2):
                    pixels_lo(0, t, part)
            weights_lo(1)
            for t in range(2):
                embed_out(0, t)
                embed_moments(0, t)
            weights_lo(2)
            token_rows(0)
            token_moments(0)
            weights_lo(3)
            for t in range(2):
                norm_rows(0, t)
            weights_lo(4)
            rows_lo(0)
            for k in range(5, len(pieces)):
                weights_lo(k)
            dve.wait_ge(w_hi, len(pieces) + 1)
            V.scalar_tensor_tensor(wgate[:, 1], gatest[:, :, :], WS, wgate[:, 0], ALU.mult, ALU.subtract).then_inc(prep, 1)
            dve.wait_ge(w_lo, len(pieces))
            body(0, True, False, False)
            with dve.Fori(1, G - 2) as g:
                body(g, False, False, True)
            body(G - 2, False, False, False)
            body(G - 1, False, True, False)
            row_inv(G - 1, 7)
            probs_lo(G - 1, 6)
            attend_lo(G - 1, 2)
            probs_lo(G - 1, 7)
            attend_lo(G - 1, 3)
            for t in range(2):
                residual(G - 1, t)
            for t in range(2):
                norm_xf(G - 1, t)
            xf_lo(G - 1)
            gate_out(G - 1)
            step = [0]

            def then(ins):
                step[0] += 1
                ins.then_inc(route, 1)
                dve.wait_ge(route, step[0])

            def wide(v, n=E):
                return v.unsqueeze(2).to_broadcast([R, TILES, n])

            lg = logits[0:R, :, :]
            mx, tot, inv, m1, i1, m2, i2 = (sc8[0:R, k, :] for k in range(7))
            dve.wait_ge(back_out, 5 * G - 1)
            dve.wait_ge(scores_ready, 8 * G)
            then(V.tensor_reduce(mx, lg, AX.X, ALU.max))
            V.tensor_tensor(rt(0), lg, wide(mx), ALU.subtract).then_inc(route_exp_in, 1)
            dve.wait_ge(route_exp, 1)
            then(V.tensor_reduce(tot, rt(1), AX.X, ALU.add))
            then(V.reciprocal(inv, tot))
            then(V.tensor_tensor(rt(1), rt(1), wide(inv), ALU.mult))
            gb = gbrow[0:R, :].unsqueeze(1).to_broadcast([R, TILES, E])
            then(V.tensor_tensor(rt(2), rt(1), gb, ALU.add))
            sg = rt(2).rearrange("p t (g e) -> p t g e", g=4)
            V.tensor_tensor(rg(0), sg[:, :, :, 0], sg[:, :, :, 1], ALU.max)
            V.tensor_tensor(rg(1), sg[:, :, :, 0], sg[:, :, :, 1], ALU.min)
            V.tensor_tensor(rg(2), sg[:, :, :, 2], sg[:, :, :, 3], ALU.max)
            then(V.tensor_tensor(rg(3), sg[:, :, :, 2], sg[:, :, :, 3], ALU.min))
            V.tensor_tensor(rg(4), rg(0), rg(2), ALU.max)
            V.tensor_tensor(rg(5), rg(0), rg(2), ALU.min)
            then(V.tensor_tensor(rg(6), rg(1), rg(3), ALU.max))
            then(V.tensor_tensor(rg(5), rg(5), rg(6), ALU.max))
            then(V.tensor_tensor(rg(0), rg(4), rg(5), ALU.add))
            then(V.tensor_copy(rg(1), small[0:R, 17:21].unsqueeze(1).to_broadcast([R, TILES, 4])))
            for d in range(1, 4):
                won = rg(2)[:, :, 0:4 - d]
                then(V.tensor_tensor(won, rg(0)[:, :, 0:4 - d], rg(0)[:, :, d:4], ALU.is_ge))
                then(V.tensor_tensor(rg(1)[:, :, d:4], rg(1)[:, :, d:4], won, ALU.add))
                then(V.tensor_tensor(rg(1)[:, :, 0:4 - d], rg(1)[:, :, 0:4 - d], won, ALU.subtract))
            then(V.tensor_scalar(rg(3), rg(1), 2.0, None, ALU.is_lt))
            then(V.tensor_scalar(rg(4), rg(3), 1.0, OUT, ALU.subtract, ALU.mult))
            keep, pen = (rg(k).unsqueeze(3).to_broadcast([R, TILES, 4, 4]) for k in (3, 4))
            s3 = rt(3).rearrange("p t (g e) -> p t g e", g=4)
            then(V.tensor_tensor(s3, sg, keep, ALU.mult))
            then(V.tensor_tensor(s3, s3, pen, ALU.add))
            iota = small[0:R, 1:17].unsqueeze(1).to_broadcast([R, TILES, E])
            for m, i, pick in ((m1, i1, rt(6)), (m2, i2, rt(7))):
                then(V.tensor_reduce(m, rt(3), AX.X, ALU.max))
                then(V.tensor_tensor(rt(4), rt(3), wide(m), ALU.is_equal))
                then(V.scalar_tensor_tensor(rt(5), rt(4), -float(E), iota, ALU.mult, ALU.add))
                then(V.tensor_reduce(i, rt(5), AX.X, ALU.min))
                then(V.tensor_tensor(pick, rt(5), wide(i), ALU.is_equal))
                then(V.scalar_tensor_tensor(rt(3), pick, -3.0 * OUT, rt(3), ALU.mult, ALU.add))
            then(V.tensor_tensor(rt(4), rt(6), rt(7), ALU.add))
            V.memset(comb[:, :, E:NE], 1.0)
            then(V.tensor_tensor(comb[0:R, :, 0:E], rt(4), rt(1), ALU.mult))
            then(V.tensor_copy(chosen[0:R, :], qkf[0:R, 4 * TE:5 * TE]))
            assert step[0] == CHOSEN, step[0]
            for j in range(2):
                shared_gate(G - 1, j)

            def over(v, n):
                return v.unsqueeze(2).to_broadcast([R, T2, n])

            def both(v):
                return v.unsqueeze(1).to_broadcast([R, 2, TILES, E])

            picks4 = picks.rearrange("p (c t) e -> p c t e", c=2)
            prod4 = prod.rearrange("p (c t) e -> p c t e", c=2)
            then(V.tensor_tensor(prod4, picks4, both(rt(1)), ALU.mult))
            then(V.tensor_reduce(weights[0:R, :, :].rearrange("p c t -> p (c t)"), prod, AX.X, ALU.add))
            for j in range(2):
                shared_lo(G - 1, j)
            blocks_e, first_e, end_e = (per_e[0:R, k, :] for k in range(3))
            dve.wait_ge(rank_ready, 1)
            rank_all = score_ps[0][0:R, 0:TE].rearrange("p (t e) -> p t e", t=TILES)
            cmp = prod.rearrange("p j e -> p (j e)")
            cmp_k = cmp[:, 0:E * KMAX].rearrange("p (e k) -> p e k", e=E)
            then(V.tensor_tensor(cmp_k, score_ps[1][0:R, 0:E].unsqueeze(2).to_broadcast([R, E, KMAX]),
                                 full.unsqueeze(1).to_broadcast([R, E, KMAX]), ALU.is_gt))
            then(V.tensor_reduce(blocks_e, cmp_k, AX.X, ALU.add))
            cmp_e = cmp[:, 0:E * E].rearrange("p (e k) -> p e k", e=E)
            then(V.tensor_tensor(cmp_e, before, blocks_e.unsqueeze(1).to_broadcast([R, E, E]), ALU.mult))
            then(V.tensor_reduce(first_e, cmp_e, AX.X, ALU.add))
            then(V.tensor_tensor(end_e, first_e, blocks_e, ALU.add))
            first_of, rank_of, full_of, block_of, place_of, slot_of = (place[0:R, k, :] for k in range(6))
            then(V.tensor_tensor(prod, picks, first_e.unsqueeze(1).to_broadcast([R, T2, E]), ALU.mult))
            then(V.tensor_reduce(first_of, prod, AX.X, ALU.add))
            then(V.tensor_tensor(prod4, picks4, both(rank_all), ALU.mult))
            then(V.tensor_reduce(rank_of, prod, AX.X, ALU.add))
            then(V.tensor_tensor(past, over(rank_of, KMAX - 1), full[:, 1:KMAX].unsqueeze(1).to_broadcast([R, T2, KMAX - 1]),
                                 ALU.is_ge))
            then(V.tensor_reduce(full_of, past, AX.X, ALU.add))
            V.tensor_tensor(block_of, first_of, full_of, ALU.add)
            then(V.scalar_tensor_tensor(place_of, full_of, -float(P), rank_of, ALU.mult, ALU.add))
            then(V.scalar_tensor_tensor(slot_of, block_of, float(P), place_of, ALU.mult, ALU.add))
            V.tensor_copy(slots[0:R, :, :], slot_of.rearrange("p (c t) -> p t c", c=2))
            V.tensor_tensor(hot_s, over(place_of, P), iota_s.unsqueeze(1).to_broadcast([R, T2, P]), ALU.is_equal)
            then(V.tensor_tensor(hot_b, over(block_of, NB), iota_b.unsqueeze(1).to_broadcast([R, T2, NB]), ALU.is_equal))
            shared_add(G - 1)
            hot_b4 = hot_b.rearrange("p (c t) b -> p c t b", c=2)
            for c in range(2):
                ins = V.tensor_tensor(hot_b4[:, c], hot_b4[:, c], rowid.unsqueeze(2).to_broadcast([R, TILES, NB]), ALU.mult)
            then(ins)
            assert step[0] == PLACED, step[0]
            cmp_b = qkf[0:R, 0:NB * E].rearrange("p (b e) -> p b e", b=NB)
            then(V.tensor_tensor(cmp_b, iota_b.unsqueeze(2).to_broadcast([R, NB, E]),
                                 end_e.unsqueeze(1).to_broadcast([R, NB, E]), ALU.is_ge))
            then(V.tensor_reduce(qkf[0:R, NB * E:NB * E + NB], cmp_b, AX.X, ALU.add))
            then(V.tensor_scalar(blk_expert[0:1, 3:3 + NB], qkf[0:1, NB * E:NB * E + NB], float(E - 1), None, ALU.min))
            dve.wait_ge(ids_ready, 1)
            then(V.tensor_scalar(ids[:, :], pt_ps[:, 0:NB], float(MID), None, ALU.add))
            assert step[0] == ROUTED, step[0]

            def row_low(b, i):
                dve.wait_ge(row_hi, STEPS * b + i + 1)
                V.tensor_tensor(xrt[:, i % 2, 1, :], score_ps[i % 2][:, 0:D], xrt[:, i % 2, 0, :],
                                ALU.subtract).then_inc(row_lo, 1)

            def gate_up(b, i, ex):
                dve.wait_ge(silu_done, STEPS * b + i + 1)
                if not (isinstance(b, int) and b == 0 and i < 3):
                    dve.wait_ge(g_lo, STEPS * b + i - 2)
                V.scalar_tensor_tensor(bgated[:, i % 3, :], proj_ps[i % 2][:, P:2 * P], b13col[:, 1, bass.ds(ex, 1)],
                                       bsilu[:, i % 2, :], ALU.add, ALU.mult).then_inc(gated_done, 1)

            def gated_lo(b, i):
                dve.wait_ge(g_hi, STEPS * b + i + 1)
                V.tensor_tensor(bgp[:, i % 3, 1, :], bgated[:, i % 3, :], bgp[:, i % 3, 0, :],
                                ALU.subtract).then_inc(g_lo, 1)

            def blocks(b, first):
                ex = experts_of(b, mybir.EngineType.DVE, 2, STEPS)
                for i in range(STEPS):
                    row_low(b, i)
                    if i >= 1 or not first:
                        gate_up(*behind(b, i, 1), ex[i])
                    if i >= 2 or not first:
                        gated_lo(*behind(b, i, 2))

            blocks(0, True)
            with dve.Fori(1, NB // STEPS) as b:
                blocks(b, False)
            end = NB // STEPS
            ex = experts_of(end, mybir.EngineType.DVE, 2, 1)
            gated_lo(*behind(end, 0, 2))
            gate_up(*behind(end, 0, 1), ex[0])
            gated_lo(*behind(end, 0, 1))

            def combine(g, half):
                V.tensor_copy(comb_now[0:R, :, :], comb[0:R, bass.ds(2 * g, 2), :]).then_inc(comb_now_in, 1)
                dve.wait_ge(be2_ready, g + 1)
                rows = hrows[0:R, bass.ds(2 * g, 2), :]
                V.tensor_tensor(rows, o_ps[0:R, 0:2 * D].rearrange("p (t d) -> p t d", t=2), rows,
                                ALU.add).then_inc(be2_added, 1)
                for c in range(2):
                    if c == 0:
                        dve.wait_ge(be2_added, g + 1)
                    else:
                        dve.wait_ge(summed, 2 * g + 1)
                    for t in range(2):
                        k = 4 * half + 2 * t + c
                        dve.wait_ge(pick_in[k], 8 * (g + 2 - half))
                        h = hrows[0:R, 2 * g + t, :]
                        ins = V.scalar_tensor_tensor(h, ypick[0:R, k, :], weights[0:R, c, bass.ds(2 * g + t, 1)], h,
                                                     ALU.mult, ALU.add)
                    ins.then_inc(summed, 1)
                dve.wait_ge(summed, 2 * g + 2)
                V.memset(scrap[:, 14:15], 0.0).then_inc(rows_final, 1)

            combine(0, 0)
            with dve.Fori(0, G // 2) as n:
                combine(2 * n + 1, 1)
                combine(2 * n + 2, 0)

        @block.gpsimd
        def _(pool):
            Q = nc.gpsimd

            def normalise(g, u):
                pool.wait_ge(rinv_done, done(8, g, u))
                Q.tensor_tensor(probs[0:R, u % 3], probs[0:R, u % 3], rinv[0:R, u, :].unsqueeze(2).to_broadcast([R, HU, R]),
                                ALU.mult).then_inc(probs_ready, 1)

            def pw(n, k):
                return power[0:n, k:k + 1].to_broadcast([n, 2])


            def pixel_rstd(g):
                pool.wait_ge(x_moments, done(2, g, 1))
                Q.tensor_tensor(xrs[0:PR, :, 0], xmv[0:PR, :, 1], pw(PR, 3), ALU.add).then_inc(px, 1)
                pool.wait_ge(px, g + 1)
                Q.tensor_tensor(xrs[0:PR, :, 1], xrs[0:PR, :, 0], pw(PR, 0), ALU.pow).then_inc(x_rstd, 1)

            def token_rstd(g):
                pool.wait_ge(y_moments, done(2, g, 1))
                Q.tensor_tensor(yrs[0:R, :, 0], ymv[0:R, :, 1], pw(R, 3), ALU.add).then_inc(py, 1)
                pool.wait_ge(py, 2 * g + 1)
                Q.tensor_tensor(yrs[0:R, :, 1], yrs[0:R, :, 0], pw(R, 0), ALU.pow).then_inc(py, 1)
                pool.wait_ge(py, 2 * g + 2)
                Q.tensor_tensor(yrs[0:R, :, 2], yrs[0:R, :, 1], small[0:R, 0:1].to_broadcast([R, 2]), ALU.mult).then_inc(y_rstd, 1)

            def row_scale(g):
                pool.wait_ge(h_moments, done(2, g, 1))
                s = [hrs[0:R, :, k] for k in range(8)]
                var = hmv[0:R, :, 1]
                Q.tensor_tensor(s[0], var, pw(R, 3), ALU.add)
                Q.tensor_tensor(s[2], var, pw(R, 1), ALU.pow).then_inc(ph, 1)
                pool.wait_ge(ph, 5 * g + 1)
                Q.tensor_tensor(s[1], s[0], pw(R, 0), ALU.pow).then_inc(ph, 1)
                pool.wait_ge(ph, 5 * g + 2)
                Q.tensor_tensor(s[3], s[2], s[1], ALU.mult).then_inc(ph, 1)
                pool.wait_ge(ph, 5 * g + 3)
                Q.tensor_tensor(s[6], s[1], pw(R, 4), ALU.mult)
                Q.tensor_scalar(s[4], s[3], float(D) ** 0.5, 1e-12, ALU.mult, ALU.max).then_inc(ph, 1)
                pool.wait_ge(ph, 5 * g + 4)
                Q.tensor_tensor(s[5], s[4], pw(R, 2), ALU.pow).then_inc(ph, 1)
                pool.wait_ge(ph, 5 * g + 5)
                Q.tensor_tensor(s[7], s[6], s[5], ALU.mult).then_inc(h_scale, 1)

            def last_rstd(g):
                pool.wait_ge(f_moments, done(2, g, 1))
                Q.tensor_tensor(frs[0:R, :, 0], fmv[0:R, :, 1], pw(R, 3), ALU.add).then_inc(pf, 1)
                pool.wait_ge(pf, g + 1)
                Q.tensor_tensor(frs[0:R, :, 1], frs[0:R, :, 0], pw(R, 0), ALU.pow).then_inc(f_rstd, 1)

            def body(g, first, last):
                if not first:
                    normalise(g - 1, 7)
                if not last:
                    pixel_rstd(g + 1)
                if not first:
                    last_rstd(g - 1)
                for u in range(UNITS - 1):
                    normalise(g, u)
                    if not last:
                        if u == 0:
                            token_rstd(g + 1)
                        if u == 2:
                            row_scale(g + 1)

            pool.wait_ge(prep, 7)
            pixel_rstd(0)
            token_rstd(0)
            row_scale(0)
            body(0, True, False)
            with pool.Fori(1, G - 1) as g:
                body(g, False, False)
            body(G - 1, False, True)
            normalise(G - 1, 7)
            last_rstd(G - 1)

            def hold(n):
                Q.tensor_tensor(held[:, n:n + 1], power[:, 3:4], power[:, 3:4], ALU.mult)

            def fetch(b, half, first):
                if not first:
                    pool.wait_ge(row_turned, STEPS * (b - 1) + 1)
                    hold(0)
                now = ids_now[:, half * STEPS:(half + 1) * STEPS]
                Q.tensor_copy(now, ids[:, bass.ds(STEPS * b, STEPS)]).then_inc(ids_copied, 1)
                pool.wait_ge(ids_copied, b + 1)
                hold(1)
                for i in range(STEPS):
                    if i > 0 and not first:
                        pool.wait_ge(row_turned, STEPS * (b - 1) + i + 1)
                        hold(3 + i)
                    Q.indirect_dma_start(xrow[:, i, :], None, xf_dram,
                                         bass.IndirectOffsetOnAxis(now[:, i:i + 1], 0)).then_inc(row_in[i], 16)

            pool.wait_ge(xf_stored, 16 * G)
            pool.wait_ge(route, ROUTED)
            fetch(0, 0, True)
            with pool.Fori(0, NB // STEPS // 2) as n:
                fetch(2 * n + 1, 1, False)
                fetch(2 * n + 2, 0, False)

            def pick(g, half, first):
                if not first:
                    pool.wait_ge(summed, 2 * g - 2)
                    hold(2)
                Q.tensor_copy(slots_now[0:R, 4 * half:4 * half + 4],
                              slots[0:R, bass.ds(2 * g, 2), :].rearrange("p t c -> p (t c)")).then_inc(slots_copied, 1)
                pool.wait_ge(slots_copied, g + 1)
                hold(0)
                for c in range(2):
                    for t in range(2):
                        k = 4 * half + 2 * t + c
                        Q.indirect_dma_start(ypick[0:R, k, :], None, y_dram,
                                             bass.IndirectOffsetOnAxis(slots_now[0:R, k:k + 1], 0)).then_inc(pick_in[k], 16)

            for k in range(STEPS):
                pool.wait_ge(y_stored[k], 16 * (NB // STEPS))
            pick(0, 0, True)
            pick(1, 1, True)
            pick(2, 0, False)
            with pool.Fori(1, G // 2) as n:
                pick(2 * n + 1, 1, False)
                pick(2 * n + 2, 0, False)


_INS = ['x', 'L0_tok_cls_token', 'L0_tok_cls_pos_embedding', 'L0_tok_ln1_g', 'L0_tok_ln1_b', 'L0_tok_W', 'L0_tok_bias',
        'L0_tok_ln2_g', 'L0_tok_ln2_b', 'L0_attn_gamma', 'L0_attn_w_qkv', 'L0_attn_w_out', 'L0_ffn_gate_w', 'L0_ffn_gate_b',
        'L0_ffn_We1', 'L0_ffn_be1', 'L0_ffn_We2', 'L0_ffn_be2', 'L0_ffn_We3', 'L0_ffn_be3', 'L0_ffn_ws1', 'L0_ffn_bs1',
        'L0_ffn_ws2', 'L0_ffn_bs2', 'L0_ffn_ws3', 'L0_ffn_bs3']


def kernel(**inputs):
    import numpy as _np
    import concourse.bacc as _bacc
    from concourse import mybir as _mybir
    from concourse.bass_utils import run_bass_kernel_spmd as _run

    nc = _bacc.Bacc("TRN2", target_bir_lowering=False, num_devices=1)
    arrays, args = {}, {}
    for name, value in [(n, inputs[n]) for n in _INS] + list(constants().items()):
        v = lay_out(name, _np.asarray(value))
        arrays[f"in_{name}_dram"] = v
        args[name] = nc.dram_tensor(f"in_{name}_dram", v.shape, _mybir.dt.from_np(v.dtype), kind="ExternalInput").ap()
    out = nc.dram_tensor("out_0_dram", (B, SEQ, D), _mybir.dt.float32, kind="ExternalOutput").ap()
    build(nc, args, out)
    r = _run(nc, [arrays], core_ids=[0])
    return r.results[0]["out_0_dram"]
```

```python
from contextlib import ExitStack

import numpy as np

import concourse.bass as bass
from concourse import mybir

F32 = mybir.dt.float32
F16 = mybir.dt.float16
ALU = mybir.AluOpType
ACT = mybir.ActivationFunctionType
AX = mybir.AxisListType

B, C, IMG, PATCH = 64, 3, 96, 16
HP = IMG // PATCH
NPATCH = HP * HP
SEQ = NPATCH + 1
D = 256
PD = C * PATCH * PATCH
HEADS, DH = 16, 64
DI = HEADS * DH
E, INTER = 16, 128
NE = E + 2
P = 128
KD = D // P
KP = PD // P
KI = DI // P
GI = 3
PR = GI * NPATCH
R = GI * SEQ
TILES = -(-B // GI)
LAST_B0 = B - GI
G = TILES // 2
N2 = 2 * R
UNITS = 8
HU = HEADS // 4
assert TILES == 2 * G and 3 * (TILES - 1) > LAST_B0

EPS = 1e-5
WS = 64.0
PS = 256.0
QS, KS = 2.0 ** -7, 2.0 ** -8
assert QS * KS * WS * WS == DH ** -0.5
OUT = 1e30
MOST = TILES * R
NB = (2 * MOST + E * (P - 1)) // P
STEPS = 6
KMAX = -(-MOST // P)
MID = MOST // 2
assert NB % STEPS == 0 and MID < 2048
BIG = 32768.0


def constants():
    om = np.arange(D // 4, dtype=np.float32) / np.float32(D // 4 - 1)
    om = (np.float32(1.0) / np.power(np.float32(10000.0), om)).astype(np.float32)
    y, x = np.meshgrid(np.arange(HP), np.arange(HP), indexing="ij")
    y = (y.reshape(-1)[:, None] * om[None, :]).astype(np.float32)
    x = (x.reshape(-1)[:, None] * om[None, :]).astype(np.float32)
    pe = np.concatenate((np.sin(x), np.cos(x), np.sin(y), np.cos(y)), axis=1).astype(np.float32)
    rows = np.zeros((P, D), np.float32)
    rows[:PR] = np.tile(pe, (GI, 1))
    img = np.array([r // NPATCH if r < PR else r - PR for r in range(R)])
    own = (img[None, :] == np.arange(GI)[:, None]).astype(np.float32)
    ml = np.zeros((P, R), np.float16)
    mr = np.zeros((P, HU * R), np.float16)
    for base in (0, 64):
        ml[base:base + GI] = own * BIG
        mr[base:base + GI] = np.tile(-(1 - own) * BIG, (1, HU))
    small = np.zeros((P, 24), np.float32)
    small[:, 0] = np.arange(P) < PR
    small[:, 1:17] = np.arange(E) + E
    small[:, 17:21] = np.arange(3, -1, -1)
    route = np.zeros((P, 256 + KMAX + NB + P + TILES), np.float32)
    e = np.arange(E)
    route[:, 0:256] = (e[None, :] < e[:, None]).astype(np.float32).reshape(1, -1)
    route[:, 256:256 + KMAX] = np.arange(KMAX) * P
    route[:, 256 + KMAX:256 + KMAX + NB] = np.arange(NB)
    route[:, 256 + KMAX + NB:256 + KMAX + NB + P] = np.arange(P)
    route[:, 256 + KMAX + NB + P:] = np.arange(TILES)[None, :] * R + np.arange(P)[:, None] - MID
    tri = np.zeros((P, 2, R), np.float16)
    tri[:, 0] = np.arange(P)[:, None] < np.arange(R)[None, :]
    tri[:, 1] = 1
    return {"c_tables": np.concatenate([np.eye(P, dtype=np.float32), small, route, rows], axis=1),
            "c_halves": np.concatenate([ml, mr, tri.reshape(P, -1)], axis=1)}


COLUMNS = ("L0_tok_ln1_g", "L0_tok_ln1_b", "L0_attn_gamma", "L0_ffn_be1", "L0_ffn_bs1", "L0_ffn_be3", "L0_ffn_bs3",
           "L0_ffn_gate_w")


def lay_out(name, v):
    if name == "x":
        v = v.reshape(B, C, HP, PATCH, HP, PATCH).transpose(0, 2, 4, 3, 5, 1).reshape(B * NPATCH, PD)
    elif name in ("L0_tok_ln1_g", "L0_tok_ln1_b", "L0_attn_gamma", "L0_ffn_bs1", "L0_ffn_bs3"):
        v = v.reshape(-1, P).T
    elif name in ("L0_ffn_be1", "L0_ffn_be3"):
        v = v.T
    elif name == "L0_ffn_gate_w":
        v = v.reshape(E, KD, P).transpose(2, 1, 0).reshape(P, KD * E)
    return np.ascontiguousarray(v)


def done(per, g, k):
    return per * g + (k + 1)


def build(nc, a, out):
    x = a["x"]
    ctx = ExitStack()
    with ctx:
        def sb(name, shape, dt=F32):
            return ctx.enter_context(nc.sbuf_tensor(name, shape, dt))

        def bank(name, shape, dt=F32):
            return ctx.enter_context(nc.psum_tensor(name, shape, dt))

        def sem(name):
            return ctx.enter_context(nc.semaphore(name))

        wtok = sb("wtok", [P, 2, KP, D], F16)
        wqkv = sb("wqkv", [P, 2, KD, 3 * DI], F16)
        wout = sb("wout", [P, 2, KI, D], F16)
        w13 = sb("w13", [P, 2, NE, KD, 2 * INTER], F16)
        w2 = sb("w2", [P, 2, NE, D], F16)
        wgate = sb("wgate", [P, 2, KD, E], F16)

        NR = 256 + KMAX + NB + P + TILES
        tables = sb("tables", [P, P + 24 + NR + D])
        ident = tables[:, 0:P]
        halves = sb("halves", [P, (3 + HU) * R], F16)
        maskl = halves[:, 0:R]
        maskr = halves[:, R:(1 + HU) * R]
        tri = halves[:, (1 + HU) * R:(3 + HU) * R].rearrange("p (a r) -> p a r", a=2)
        small = tables[:, P:P + 24]
        addrow = tables[:, P + 24 + NR:P + 24 + NR + D]
        g2row = sb("g2row", [P, D])
        biasrow = sb("biasrow", [P, D])
        cols = sb("cols", [P, 2 * KP + KD + 2 * NE + KD * E])
        c0, c1, c2, c3, c4 = (int(n) for n in np.cumsum([KP, KP, KD, 2 * NE, KD * E]))
        g1col, b1col, gamcol = cols[:, 0:c0], cols[:, c0:c1], cols[:, c1:c2]
        b13col = cols[:, c2:c3].rearrange("p (a e) -> p a e", a=2)
        gatest = cols[:, c3:c4].rearrange("p (k e) -> p k e", k=KD)
        gbrow = sb("gbrow", [P, E])
        bs2row = sb("bs2row", [P, D])
        shcol = sb("shcol", [P, 2, 2])
        rtab = tables[:, P + 24:P + 24 + NR]
        before = rtab[0:R, 0:256].rearrange("p (a b) -> p a b", a=E)
        full = rtab[0:R, 256:256 + KMAX]
        iota_b = rtab[0:R, 256 + KMAX:256 + KMAX + NB]
        iota_s = rtab[0:R, 256 + KMAX + NB:256 + KMAX + NB + P]
        rowid = rtab[0:R, 256 + KMAX + NB + P:256 + KMAX + NB + P + TILES]
        power = sb("power", [P, 5])
        scrap = sb("scrap", [P, 15])

        hrows = sb("hrows", [P, TILES, D])
        xft = sb("xft", [P, 2, KD, N2], F16)
        logits = sb("logits", [P, TILES, E])
        stage = hrows[:, 4:TILES, :].rearrange("p t d -> p (t d)")
        pair = sb("pair", [P, 1536])
        pair13 = pair[:, 0:1024].rearrange("p (e c n) -> p e c n", e=2, c=KD)
        pair2 = pair[:, 1024:1536].rearrange("p (e d) -> p e d", e=2)

        xin = sb("xin", [P, 2, PD])
        xt = sb("xt", [P, 2, 2, KP, R], F16)
        ytok = sb("ytok", [P, 2, D])
        xn = sb("xn", [P, 2, D])
        xf = sb("xf", [P, 2, D])
        xnt = sb("xnt", [P, 2, KD, N2], F16)
        qk = sb("qk", [P, 2, 2 * KI, N2], F16)
        arena = sb("arena", [P, 4 * DI + 6 * HU * R + 4 * HU * R + 2 * KI * N2], F16)
        a0, a1, a2, a3 = 4 * DI, 4 * DI + 6 * HU * R, 4 * DI + 10 * HU * R, 4 * DI + 10 * HU * R + 2 * KI * N2
        vv = arena[:, 0:a0].rearrange("p (a t n) -> p a t n", a=2, t=2)
        probs = arena[:, a0:a1].bitcast(F32).rearrange("p (s h r) -> p s h r", s=3, h=HU)
        pt = arena[:, a1:a2].rearrange("p (s a h r) -> p s a h r", s=2, a=2, h=HU)
        ot = arena[:, a2:a3].rearrange("p (a k n) -> p a k n", a=2, k=KI)
        sh_silu = sb("sh_silu", [P, 2, N2])
        sh_gated = sb("sh_gated", [P, 2, N2])
        sh_gp = sb("sh_gp", [P, 2, 2, N2], F16)
        early = arena[:, a2:a3].bitcast(F32)
        addrow2, addrow3 = early[:, 0:D], early[:, D:2 * D]
        brow, onerow = early[0:1, 2 * D:3 * D], early[0:1, 3 * D:3 * D + R]
        b1wide = early[:, 4 * D:4 * D + KP * R].rearrange("p (k r) -> p k r", k=KP)
        negmax = sb("negmax", [P, UNITS, HU])
        rowsum = sb("rowsum", [P, UNITS, HU])
        rinv = sb("rinv", [P, UNITS, HU])
        xst = sb("xst", [P, 2, 2, 6])
        xmv = sb("xmv", [P, 2, 2])
        yst = sb("yst", [P, 2, 6])
        ymv = sb("ymv", [P, 2, 2])
        hst = sb("hst", [P, 2, 6])
        hmv = sb("hmv", [P, 2, 2])
        fst = sb("fst", [P, 2, 6])
        fmv = sb("fmv", [P, 2, 2])
        xrs = sb("xrs", [P, 2, 2])
        yrs = sb("yrs", [P, 2, 3])
        hrs = sb("hrs", [P, 2, 8])
        frs = sb("frs", [P, 2, 2])

        qkf = qk[:, :, :, :].rearrange("p a c n -> p (a c n)").bitcast(F32)
        TE = TILES * E
        EARLY = 2 * (G - 1)

        def rt(k, t0=0, n=TILES):
            home = (xin[:, :, :].rearrange("p t n -> p (t n)"), pair[:, :])[k // 4]
            return home[0:R, k % 4 * TE:(k % 4 + 1) * TE].rearrange("p (t e) -> p t e", t=TILES)[:, t0:t0 + n]

        groups_home = wtok[:, :, :, :].rearrange("p a k d -> p (a k d)").bitcast(F32)

        def rg(k, t0=0, n=TILES):
            return groups_home[0:R, k * TILES * 4:(k + 1) * TILES * 4].rearrange("p (t g) -> p t g", t=TILES)[:, t0:t0 + n]

        sc8 = sb("sc8", [P, 8, TILES])
        T2 = 2 * TILES
        picks = pair[0:R, 2 * TE:4 * TE].rearrange("p (j e) -> p j e", j=T2)
        weights = sb("weights", [P, 2, TILES])
        slots = sb("slots", [P, TILES, 2], mybir.dt.int32)
        ids = sb("ids", [P, NB], mybir.dt.int32)
        blk_expert = sb("blk_expert", [1, 3 + NB], mybir.dt.int32)
        ids_now = sb("ids_now", [P, 2 * STEPS], mybir.dt.int32)
        slots_now = sb("slots_now", [P, 8], mybir.dt.int32)
        hot_b = arena[0:R, 0:T2 * NB].rearrange("p (j b) -> p j b", j=T2)
        hot_s = arena[0:R, T2 * NB:T2 * (NB + P)].rearrange("p (j s) -> p j s", j=T2)
        free = arena[0:R, T2 * (NB + P):].bitcast(F32)
        prod = free[:, 0:2 * TE].rearrange("p (j e) -> p j e", j=T2)
        past = free[:, 2 * TE:2 * TE + T2 * (KMAX - 1)].rearrange("p (j k) -> p j k", j=T2)
        held = sb("held", [P, 13])
        chosen = sb("chosen", [P, TE], F16)
        per_e = sb("per_e", [P, 3, E])
        place = sb("place", [P, 6, T2])
        xrow = xin[:, :, :].rearrange("p t n -> p (t n)").rearrange("p (s d) -> p s d", s=STEPS)
        yrow = qkf[:, 0:STEPS * D].rearrange("p (s d) -> p s d", s=STEPS)
        bsilu = qkf[:, 1536:1792].rearrange("p (s n) -> p s n", s=2)
        bgated = qkf[:, 1792:2176].rearrange("p (s n) -> p s n", s=3)
        bgp = qkf[:, 2176:2560].bitcast(F16).rearrange("p (s a n) -> p s a n", s=3, a=2)
        xrt = qkf[:, 2560:3072].bitcast(F16).rearrange("p (s a n) -> p s a n", s=2, a=2)
        ypick = qkf[:, 0:8 * D].rearrange("p (s d) -> p s d", s=8)

        be2 = wqkv[:, :, :, :].rearrange("p a k n -> p (a k n)")[:, 0:2 * E * D].bitcast(F32).rearrange("p (e d) -> p e d", e=E)

        xf_dram = nc.dram_tensor("xf_rows", (MOST, D), F32, kind="Internal").ap()
        y_dram = nc.dram_tensor("y_rows", (NB * P, D), F32, kind="Internal").ap()

        proj_ps = [bank(f"proj{k}", [P, 512]) for k in range(2)]
        front_ps = bank("front", [P, 512])
        back_ps = bank("back", [P, 512])
        score_ps = [bank(f"score{k}", [P, 512]) for k in range(2)]
        pt_ps = bank("ptps", [P, 512])
        o_ps = bank("ops", [P, 512])

        const_in = sem("const_in")
        stage_in = [sem(f"stage_in{k}") for k in range(3)]
        w_hi, w_lo = sem("w_hi"), sem("w_lo")
        prep = sem("prep")
        bias_mm = sem("bias_mm")
        x_in = [sem(f"x_in{k}") for k in range(2)]
        proj_ready, proj_hi, proj_lo = sem("proj_ready"), sem("proj_hi"), sem("proj_lo")
        front_ready, front_hi, front_out = sem("front_ready"), sem("front_hi"), sem("front_out")
        back_ready, back_hi, back_out = sem("back_ready"), sem("back_hi"), sem("back_out")
        scores_ready, max_done, exp_done = sem("scores_ready"), sem("max_done"), sem("exp_done")
        rinv_done, probs_ready = sem("rinv_done"), sem("probs_ready")
        pt_ready, pt_hi, pt_lo = sem("pt_ready"), sem("pt_hi"), sem("pt_lo")
        pv_ready, ot_hi, ot_lo = sem("pv_ready"), sem("ot_hi"), sem("ot_lo")
        x_stats, x_moments, x_rstd, xhat_done = sem("x_stats"), sem("x_moments"), sem("x_rstd"), sem("xhat_done")
        y_stats, y_moments, y_rstd = sem("y_stats"), sem("y_moments"), sem("y_rstd")
        y_gain, h_done = sem("y_gain"), sem("h_done")
        h_stats, h_moments, h_scale, xn_done = sem("h_stats"), sem("h_moments"), sem("h_scale"), sem("xn_done")
        f_stats, f_moments, f_rstd, xf_done = sem("f_stats"), sem("f_moments"), sem("f_rstd"), sem("xf_done")
        px, py, ph, pf = sem("px_step"), sem("py_step"), sem("ph_step"), sem("pf_step")
        route, route_exp_in, route_exp = sem("route"), sem("route_exp_in"), sem("route_exp")
        bs2_added, be2_in = sem("bs2_added"), sem("be2_in")
        pair_in, pair_scaled, pair_hi, pair_lo = sem("pair_in"), sem("pair_scaled"), sem("pair_hi"), sem("pair_lo")
        sh_ready, sh_tanh, sh_step, sh_gate_done, sh_hi, sh_lo = (sem("sh_" + n) for n in ("ready", "tanh", "step", "gate", "hi", "lo"))
        xf_stored = sem("xf_stored")
        rank_ready, ids_ready = sem("rank_ready"), sem("ids_ready")
        ids_copied, slots_copied = sem("ids_copied"), sem("slots_copied")
        row_in = [sem(f"row_in{k}") for k in range(STEPS)]
        row_turned, row_hi, row_lo = sem("row_turned"), sem("row_hi"), sem("row_lo")
        hid_ready, silu_done, gated_done, g_hi, g_lo = (sem(n) for n in ("hid_ready", "silu_done", "gated_done", "g_hi", "g_lo"))
        y_ready, y_out = sem("y_ready"), sem("y_out")
        y_stored = [sem(f"y_stored{k}") for k in range(STEPS)]
        pick_in = [sem(f"pick_in{k}") for k in range(8)]
        picked, summed = sem("picked"), sem("summed")
        rows_final = sem("rows_final")
        stored = sem("stored")

        def stage_at(slot, *shape):
            n = int(np.prod(shape))
            v = stage[:, slot * 1536:slot * 1536 + n]
            names = "abc"[:len(shape)]
            return v.rearrange(f"p ({' '.join(names)}) -> p {' '.join(names)}", **dict(zip(names, shape)))

        pieces = []

        def piece(loads, parts):
            pieces.append((loads, parts))

        def slot():
            return len(pieces) % 3

        v = stage_at(slot(), KP, D)
        piece([(v, a["L0_tok_W"].rearrange("(k p) d -> p k d", p=P))],
              [(v[:, k, :], wtok[:, 0, k, :], wtok[:, 1, k, :], ("g1", k)) for k in range(KP)])
        for k in range(KD):
            for half in range(2):
                v = stage_at(slot(), 1536)
                sl = slice(half * 1536, (half + 1) * 1536)
                piece([(v, a["L0_attn_w_qkv"][k * P:(k + 1) * P, sl])],
                      [(v, wqkv[:, 0, k, sl], wqkv[:, 1, k, sl], ("gam", k))])
        for half in range(2):
            v = stage_at(slot(), 4, D)
            sl = slice(4 * half, 4 * half + 4)
            piece([(v, a["L0_attn_w_out"].rearrange("(c p) d -> p c d", p=P)[:, sl, :])],
                  [(v, wout[:, 0, sl, :], wout[:, 1, sl, :], None)])
        v = stage_at(slot(), 1536)
        v13 = v[:, 0:1024].rearrange("p (e c n) -> p e c n", e=2, c=KD)
        v2 = v[:, 1024:1536].rearrange("p (e d) -> p e d", e=2)
        loads = [(v2, a["L0_ffn_ws2"].rearrange("(m i) d -> i m d", m=2))]
        for j in range(2):
            for n, name in enumerate(("ws1", "ws3")):
                loads.append((v13[:, j, :, n * INTER:(n + 1) * INTER],
                              a["L0_ffn_" + name][:, j * INTER:(j + 1) * INTER].rearrange("(c p) i -> p c i", p=P)))
        piece(loads, [(v13, w13[:, 0, E:NE], w13[:, 1, E:NE], None), (v2, w2[:, 0, E:NE, :], w2[:, 1, E:NE, :], None)])

        def landed(k):
            return stage_in[k % 3], 16 * sum(len(pieces[j][0]) for j in range(k % 3, k + 1, 3))

        block = ctx.enter_context(nc.Block())

        def experts_of(turn, engine, first, n):
            _, regs = nc.values_load_multi_w_load_instructions(
                blk_expert[0:1, bass.ds(STEPS * turn + first, n)], engines=[engine], min_val=0, max_val=E - 1,
                skip_runtime_bounds_check_because="the routing takes the minimum with E - 1")
            return regs

        def behind(turn, i, back):
            return (turn, i - back) if i >= back else (turn - 1, STEPS + i - back)

        CHOSEN_EARLY, CHOSEN, PLACED, ROUTED = 36, 72, 89, 93
        PREP = 9

        NCONST = 10

        @block.sync
        def _(sp):
            n = [0]

            def const(dst, src):
                n[0] += 1
                sp.dma_start(dst, src, allow_slow_non_contiguous=True).then_inc(const_in, 16)

            def load_x(b0, t):
                sp.dma_start(xin[0:PR, t, :], x[bass.ds(b0 * NPATCH, PR), :]).then_inc(x_in[t], 16)

            load_x(0, 0)
            load_x(GI, 1)
            const(cols[:, :], a["columns"])
            const(tables[:, :], a["c_tables"])
            const(halves[:, :], a["c_halves"])
            sp.wait_ge(prep, 1)
            const(addrow2[0:PR, :], a["L0_tok_ln2_b"].rearrange("(o d) -> o d", o=1).to_broadcast([PR, D]))
            const(addrow2[PR:R, :], a["L0_tok_cls_token"].rearrange("a b d -> (a b) d").to_broadcast([GI, D]))
            const(addrow3[PR:R, :], a["L0_tok_cls_pos_embedding"].rearrange("a b d -> (a b) d").to_broadcast([GI, D]))
            const(g2row[0:R, :], a["L0_tok_ln2_g"].rearrange("(o d) -> o d", o=1).to_broadcast([R, D]))
            const(brow[:, :], a["L0_tok_bias"].rearrange("(o d) -> o d", o=1))
            const(gbrow[0:R, :], a["L0_ffn_gate_b"].rearrange("(o e) -> o e", o=1).to_broadcast([R, E]))
            const(bs2row[0:R, :], a["L0_ffn_bs2"].rearrange("(o d) -> o d", o=1).to_broadcast([R, D]))

            for k in range(1, len(pieces)):
                if k < 3:
                    for dst, src in pieces[k][0]:
                        sp.dma_start(dst, src).then_inc(stage_in[k], 16)
                    continue
                if k == 3:
                    sp.wait_ge(bias_mm, 1)
                sp.wait_ge(w_lo, k - 2)
                sp.wait_ge(w_hi, k - 2)
                for dst, src in pieces[k][0]:
                    sp.dma_start(dst, src).then_inc(stage_in[k % 3], 16)

            with sp.Fori(4, 4 + 7 * (G - 2), 7) as turned:
                sp.wait_ge(const_in, 16)
                sp.wait_ge(front_ready, turned)
                g = (turned - 4) // 7 + 1
                load_x(2 * GI * g, 0)
                load_x(2 * GI * g + GI, 1)
            sp.wait_ge(front_ready, done(7, G - 2, 3))
            load_x(2 * GI * (G - 1), 0)
            load_x(LAST_B0, 1)

            sp.wait_ge(route, CHOSEN)
            sp.dma_start(be2, a["L0_ffn_be2"].unsqueeze(0).to_broadcast([P, E, D])).then_inc(be2_in, 16)

            flat = out.rearrange("b s d -> (b s) d")
            cls = out[:, 0, :]

            def store(tile, b0, first=0):
                for im in range(first, GI):
                    sp.dma_start(flat[bass.ds((b0 + im) * SEQ + 1, NPATCH), :],
                                 hrows[im * NPATCH:(im + 1) * NPATCH, tile, :]).then_inc(stored, 16)
                sp.dma_start(cls[bass.ds(b0 + first, GI - first), :], hrows[PR + first:R, tile, :]).then_inc(stored, 16)

            with sp.Fori(1, G) as ready:
                sp.wait_ge(const_in, 16)
                sp.wait_ge(rows_final, ready)
                g = ready - 1
                both = out[bass.ds(2 * GI * g, 2 * GI), :, :].rearrange("(t i) s d -> i s t d", t=2)
                for im in range(GI):
                    sp.dma_start(both[im, 1:SEQ], hrows[im * NPATCH:(im + 1) * NPATCH, bass.ds(2 * g, 2), :]).then_inc(stored, 16)
                sp.dma_start(both[:, 0], hrows[PR:R, bass.ds(2 * g, 2), :]).then_inc(stored, 16)
            sp.wait_ge(rows_final, G)
            store(TILES - 2, 2 * GI * (G - 1))
            store(TILES - 1, LAST_B0, first=GI * (TILES - 1) - LAST_B0)
            sp.wait_ge(stored, 16 * ((1 + GI) * (G + 1) - (GI * (TILES - 1) - LAST_B0)))
            assert n[0] == NCONST, n[0]

        @block.tensor
        def _(pe):
            def mm3(dst, lh, rh, first, last, **kw):
                pe.matmul(dst, lh[0], rh[0], start=first, stop=False, **kw)
                pe.matmul(dst, lh[0], rh[1], start=False, stop=False, **kw)
                return pe.matmul(dst, lh[1], rh[0], start=False, stop=last, **kw)

            def bias_row():
                pe.wait_ge(*landed(0))
                v0 = stage_at(0, KP, D)
                for k in range(KP):
                    pe.matmul(back_ps[0:R, 0:D], b1wide[:, k, :], v0[:, k, :], start=k == 0, stop=False)
                pe.matmul(back_ps[0:R, 0:D], onerow[:, :], brow[:, :], start=False, stop=True).then_inc(bias_mm, 1)

            def project(g, s):
                if s == 0:
                    pe.wait_ge(front_out, done(7, g, 6))
                if not (isinstance(g, int) and g == 0 and s < 2):
                    pe.wait_ge(proj_lo, done(12, g, s - 2))
                if s >= 10 and not (isinstance(g, int) and g == 0):
                    pe.wait_ge(sh_gate_done, done(2, g - 1, s - 10))
                bk = proj_ps[s % 2]
                if s < 8:
                    for j in range(2):
                        cs = slice((2 * s + j) * P, (2 * s + j + 1) * P)
                        for k in range(KD):
                            ins = mm3(bk[:, j * N2:(j + 1) * N2], (wqkv[:, 0, k, cs], wqkv[:, 1, k, cs]),
                                      (xnt[:, 0, k, :], xnt[:, 1, k, :]), k == 0, k == KD - 1)
                else:
                    t, half = (s - 8) // 2, s % 2
                    cs = slice(2 * DI + half * 512, 2 * DI + (half + 1) * 512)
                    ts = slice(t * R, (t + 1) * R)
                    for k in range(KD):
                        ins = mm3(bk[0:R, :], (xnt[:, 0, k, ts], xnt[:, 1, k, ts]),
                                  (wqkv[:, 0, k, cs], wqkv[:, 1, k, cs]), k == 0, k == KD - 1)
                ins.then_inc(proj_ready, 1)

            def scores(g, u):
                t, half, par = u // 4, u // 2 % 2, u % 2
                if u == 0:
                    pe.wait_ge(proj_lo, done(12, g, 7))
                if not (isinstance(g, int) and g == 0 and u < 2):
                    pe.wait_ge(exp_done, done(8, g, u - 2))
                bk = score_ps[u % 2]
                rows = slice(64 * par, 64 * par + 64)
                pe.matmul(bk[0:R, 0:HU * R], maskl[rows, :], maskr[rows, :], start=True, stop=False)
                for j in range(HU):
                    ch = 4 * half + j
                    ts = slice(t * R, (t + 1) * R)
                    ins = mm3(bk[0:R, j * R:(j + 1) * R],
                              (qk[rows, 0, ch, ts], qk[rows, 1, ch, ts]),
                              (qk[rows, 0, KI + ch, ts], qk[rows, 1, KI + ch, ts]), False, j == HU - 1)
                ins.then_inc(scores_ready, 1)

            def turn_probs(g, u):
                pe.wait_ge(probs_ready, done(8, g, u))
                if not (isinstance(g, int) and g == 0 and u == 0):
                    pe.wait_ge(pt_lo, done(8, g, u - 1))
                for j in range(HU):
                    ins = pe.transpose(pt_ps[0:R, j * R:(j + 1) * R], probs[0:R, u % 3, j, :], ident[0:R, 0:R])
                ins.then_inc(pt_ready, 1)

            def attend(g, u):
                t, half, par = u // 4, u // 2 % 2, u % 2
                if u in (0, 4):
                    pe.wait_ge(proj_lo, done(12, g, 9 + u // 2))
                pe.wait_ge(pt_lo, done(8, g, u))
                if par == 0 and not (isinstance(g, int) and g == 0 and u == 0):
                    pe.wait_ge(ot_lo, done(4, g, u // 2 - 1))
                for j in range(HU):
                    h = 2 * (4 * half + j) + par
                    hs = slice(h * DH, (h + 1) * DH)
                    ins = mm3(o_ps[64 * par:64 * par + 64, j * R:(j + 1) * R],
                              (vv[0:R, 0, t, hs], vv[0:R, 1, t, hs]),
                              (pt[0:R, u % 2, 0, j, :], pt[0:R, u % 2, 1, j, :]), True, True)
                ins.then_inc(pv_ready, 1)

            def turn_pixels(g, t, part):
                pe.wait_ge(xhat_done, done(2, g, t))
                if not (isinstance(g, int) and g == 0 and t == 0 and part == 0):
                    pe.wait_ge(front_out, done(7, g, 2 * t + part - 1))
                for j in range(3):
                    k = 3 * part + j
                    ins = pe.transpose(front_ps[:, j * PR:(j + 1) * PR], xin[0:PR, t, k * P:(k + 1) * P], ident[0:PR, 0:PR])
                ins.then_inc(front_ready, 1)

            def embed(g, t):
                pe.wait_ge(front_out, done(7, g, 3 + t))
                for k in range(KP):
                    ins = mm3(front_ps[0:R, 0:D], (xt[:, t, 0, k, :], xt[:, t, 1, k, :]),
                              (wtok[:, 0, k, :], wtok[:, 1, k, :]), k == 0, k == KP - 1)
                ins.then_inc(front_ready, 1)

            def turn_rows(g):
                pe.wait_ge(xn_done, done(2, g, 1))
                pe.wait_ge(front_out, done(7, g, 5))
                for k in range(KD):
                    for t in range(2):
                        ins = pe.transpose(front_ps[:, k * N2 + t * R:k * N2 + (t + 1) * R],
                                           xn[0:R, t, k * P:(k + 1) * P], ident[0:R, 0:R])
                ins.then_inc(front_ready, 1)

            def out_proj(g, t):
                pe.wait_ge(ot_lo, done(4, g, 2 * t + 1))
                if not (isinstance(g, int) and g == 0 and t == 0):
                    pe.wait_ge(back_out, done(5, g, t - 1))
                ts = slice(t * R, (t + 1) * R)
                for k in range(KI):
                    ins = mm3(back_ps[0:R, 0:D], (ot[:, 0, k, ts], ot[:, 1, k, ts]),
                              (wout[:, 0, k, :], wout[:, 1, k, :]), k == 0, k == KI - 1)
                ins.then_inc(back_ready, 1)

            def turn_xf(g):
                pe.wait_ge(xf_done, done(2, g, 1))
                pe.wait_ge(back_out, done(5, g, 1))
                for k in range(KD):
                    for t in range(2):
                        ins = pe.transpose(back_ps[:, k * N2 + t * R:k * N2 + (t + 1) * R],
                                           xf[0:R, t, k * P:(k + 1) * P], ident[0:R, 0:R])
                ins.then_inc(back_ready, 1)

            def gate(g):
                pe.wait_ge(back_out, done(5, g, 2))
                for t in range(2):
                    for k in range(KD):
                        cs = slice(t * R, (t + 1) * R)
                        ins = mm3(back_ps[0:R, t * E:(t + 1) * E], (xft[:, 0, k, cs], xft[:, 1, k, cs]),
                                  (wgate[:, 0, k, :], wgate[:, 1, k, :]), k == 0, k == KD - 1)
                ins.then_inc(back_ready, 1)

            def shared_hidden(g, j):
                if j == 0:
                    pe.wait_ge(back_out, done(5, g, 2))
                for n in range(2):
                    ws = slice(n * INTER, (n + 1) * INTER)
                    for k in range(KD):
                        ins = mm3(proj_ps[j][:, n * N2:(n + 1) * N2], (w13[:, 0, E + j, k, ws], w13[:, 1, E + j, k, ws]),
                                  (xft[:, 0, k, :], xft[:, 1, k, :]), k == 0, k == KD - 1)
                ins.then_inc(sh_ready, 1)

            def shared_down(g):
                pe.wait_ge(sh_lo, done(2, g, 1))
                pe.wait_ge(back_out, done(5, g, 3))
                for t in range(2):
                    ts = slice(t * R, (t + 1) * R)
                    for j in range(2):
                        ins = mm3(back_ps[0:R, t * D:(t + 1) * D], (sh_gp[:, j, 0, ts], sh_gp[:, j, 1, ts]),
                                  (w2[:, 0, E + j, :], w2[:, 1, E + j, :]), j == 0, j == 1)
                ins.then_inc(back_ready, 1)

            def body(g, first, last):
                if not first:
                    turn_probs(g - 1, 6)
                    attend(g - 1, 5)
                project(g, 0)
                project(g, 1)
                if not first:
                    turn_probs(g - 1, 7)
                    attend(g - 1, 6)
                project(g, 2)
                project(g, 3)
                if not first:
                    attend(g - 1, 7)
                for s in range(4, 6):
                    project(g, s)
                if not first:
                    out_proj(g - 1, 0)
                if not last:
                    turn_pixels(g + 1, 0, 0)
                project(g, 6)
                if not last:
                    turn_pixels(g + 1, 0, 1)
                if not first:
                    out_proj(g - 1, 1)
                if not last:
                    turn_pixels(g + 1, 1, 0)
                project(g, 7)
                if not last:
                    turn_pixels(g + 1, 1, 1)
                project(g, 8)
                if not last:
                    embed(g + 1, 0)
                scores(g, 0)
                project(g, 9)
                if not first:
                    turn_xf(g - 1)
                scores(g, 1)
                if not last:
                    embed(g + 1, 1)
                for s in range(2, UNITS):
                    scores(g, s)
                    turn_probs(g, s - 2)
                    if s >= 3:
                        attend(g, s - 3)
                    if s == 2 and not first:
                        gate(g - 1)
                    if s in (2, 3) and not first:
                        pe.wait_ge(proj_lo, done(12, g, 6 + s))
                        shared_hidden(g - 1, s - 2)
                    if s in (4, 5):
                        project(g, 6 + s)
                    if s == 6 and not last:
                        turn_rows(g + 1)
                    if s == 7 and not first:
                        shared_down(g - 1)

            pe.wait_ge(prep, PREP - 1)
            turn_pixels(0, 0, 0)
            bias_row()
            turn_pixels(0, 0, 1)
            turn_pixels(0, 1, 0)
            turn_pixels(0, 1, 1)
            pe.wait_ge(w_lo, 1)
            embed(0, 0)
            embed(0, 1)
            turn_rows(0)
            pe.wait_ge(w_lo, 5)
            body(0, True, False)
            pe.wait_ge(w_lo, len(pieces))
            pe.wait_ge(prep, PREP + 1)
            with pe.Fori(1, G - 2) as g:
                body(g, False, False)
            body(G - 2, False, False)
            body(G - 1, False, True)
            turn_probs(G - 1, 6)
            attend(G - 1, 5)
            turn_probs(G - 1, 7)
            attend(G - 1, 6)
            attend(G - 1, 7)
            out_proj(G - 1, 0)
            out_proj(G - 1, 1)
            turn_xf(G - 1)
            gate(G - 1)

            shared_hidden(G - 1, 0)
            shared_hidden(G - 1, 1)

            rank, total = score_ps[0][0:R, :], score_ps[1][0:R, :]

            def count(t0, n):
                if t0 == 0:
                    pe.matmul(rank[:, 0:E], tri[0:R, 0, :], chosen[0:R, 0:E], start=True, stop=False)
                    pe.matmul(rank[:, E:TE], tri[0:R, 1, :],
                              chosen[0:R, 0:E].unsqueeze(1).to_broadcast([R, TILES - 1, E]), start=False, stop=False)
                first = max(t0, 1)
                pe.matmul(rank[:, first * E:(t0 + n) * E], tri[0:R, 0, :], chosen[0:R, first * E:(t0 + n) * E],
                          start=False, stop=False)
                for t in range(first, min(t0 + n, TILES - 1)):
                    pe.matmul(rank[:, (t + 1) * E:TE], tri[0:R, 1, :],
                              chosen[0:R, t * E:(t + 1) * E].unsqueeze(1).to_broadcast([R, TILES - 1 - t, E]),
                              start=False, stop=t == TILES - 2)
                for t in range(t0, t0 + n):
                    ins = pe.matmul(total[:, 0:E], tri[0:R, 1, :], chosen[0:R, t * E:(t + 1) * E],
                                    start=t == 0, stop=t == TILES - 1)
                return ins

            pe.wait_ge(route, CHOSEN_EARLY)
            count(0, EARLY)
            pe.wait_ge(route, CHOSEN)
            count(EARLY, TILES - EARLY).then_inc(rank_ready, 1)
            shared_down(G - 1)
            pe.wait_ge(route, PLACED)
            for j in range(T2):
                ins = pe.matmul(pt_ps[:, 0:NB], hot_s[:, j, :], hot_b[:, j, :], start=j == 0, stop=j == T2 - 1)
            ins.then_inc(ids_ready, 1)

            def turn_block(b, i):
                pe.wait_ge(row_in[i % STEPS], 16 * (b + 1))
                if not (isinstance(b, int) and b == 0 and i < 2):
                    pe.wait_ge(row_lo, STEPS * b + i - 1)
                for k in range(KD):
                    ins = pe.transpose(score_ps[i % 2][:, k * P:(k + 1) * P], xrow[:, i, k * P:(k + 1) * P], ident[:, :])
                ins.then_inc(row_turned, 1)

            def hidden(b, i, ex):
                pe.wait_ge(row_lo, STEPS * b + i + 1)
                if not (isinstance(b, int) and b == 0 and i < 2):
                    pe.wait_ge(gated_done, STEPS * b + i - 1)
                for j in range(2):
                    for k in range(KD):
                        ws = slice(j * INTER, (j + 1) * INTER)
                        wide = lambda n: w13[:, n, bass.ds(ex, 1), k, ws].rearrange("p a n -> p (a n)")
                        xs = slice(k * P, (k + 1) * P)
                        ins = mm3(proj_ps[i % 2][:, j * P:(j + 1) * P], (wide(0), wide(1)),
                                  (xrt[:, i % 2, 0, xs], xrt[:, i % 2, 1, xs]), k == 0, k == KD - 1)
                ins.then_inc(hid_ready, 1)

            def down(b, i, ex):
                pe.wait_ge(g_lo, STEPS * b + i + 1)
                if not (isinstance(b, int) and b == 0 and i < 2):
                    pe.wait_ge(y_out, STEPS * b + i - 1)
                wide = lambda n: w2[:, n, bass.ds(ex, 1), :].rearrange("p a n -> p (a n)")
                ins = mm3((front_ps, back_ps)[i % 2][:, 0:D], (bgp[:, i % 3, 0, :], bgp[:, i % 3, 1, :]),
                          (wide(0), wide(1)), True, True)
                ins.then_inc(y_ready, 1)

            def blocks(b, first):
                ex = experts_of(b, mybir.EngineType.PE, 0, 3 + STEPS)
                for i in range(STEPS):
                    turn_block(b, i)
                    if i >= 1:
                        hidden(b, i - 1, ex[3 + i - 1])
                    elif not first:
                        hidden(b - 1, STEPS - 1, ex[2])
                    if i >= 3:
                        down(b, i - 3, ex[i])
                    elif not first:
                        down(b - 1, STEPS - 3 + i, ex[i])

            pe.wait_ge(route, ROUTED)
            blocks(0, True)
            with pe.Fori(1, NB // STEPS) as b:
                blocks(b, False)
            last = NB // STEPS - 1
            ex = experts_of(last, mybir.EngineType.PE, STEPS, 3)
            down(last, STEPS - 3, ex[0])
            hidden(last, STEPS - 1, ex[2])
            down(last, STEPS - 2, ex[1])
            down(last, STEPS - 1, ex[2])

        @block.scalar
        def _(act):
            for dst, src in pieces[0][0]:
                act.dma_start(dst, src).then_inc(stage_in[0], 16)

            def weights_hi(k):
                act.wait_ge(*landed(k))
                if k == 0:
                    act.wait_ge(prep, 3)
                for st, hi, _lo, scale in pieces[k][1]:
                    s = WS if scale is None else {"g1": g1col, "gam": gamcol}[scale[0]][:, scale[1]:scale[1] + 1]
                    ins = nc.scalar.activation(hi, st, ACT.Copy, scale=s)
                ins.then_inc(w_hi, 1)

            def pair_load(p):
                if not (isinstance(p, int) and p == 0):
                    act.wait_ge(pair_lo, p)
                es = bass.ds(2 * p, 2)
                for n, name in enumerate(("We1", "We3")):
                    chunks = pair[:, 0:1024].rearrange("p (c n) -> p c n", c=2 * KD)
                    act.dma_start(chunks[:, :, n * INTER:(n + 1) * INTER],
                                  a["L0_ffn_" + name][es].rearrange("e (c p) i -> p (e c) i", p=P)).then_inc(pair_in, 16)
                act.dma_start(pair2, a["L0_ffn_We2"][es].rearrange("e i d -> i e d")).then_inc(pair_in, 16)

            def pair_high(p):
                act.wait_ge(pair_scaled, p + 1)
                es = bass.ds(2 * p, 2)
                nc.scalar.activation(w13[:, 0, es], pair13, ACT.Copy)
                nc.scalar.activation(w2[:, 0, es, :], pair2, ACT.Copy).then_inc(pair_hi, 1)

            def project_hi(g, s):
                act.wait_ge(proj_ready, done(12, g, s))
                if s < 8:
                    nc.scalar.activation(qk[:, 0, 2 * s:2 * s + 2, :],
                                         proj_ps[s % 2][:, 0:2 * N2].rearrange("p (a n) -> p a n", a=2),
                                         ACT.Copy, scale=QS if s < 4 else KS).then_inc(proj_hi, 1)
                else:
                    t, half = (s - 8) // 2, s % 2
                    nc.scalar.activation(vv[0:R, 0, t, half * 512:(half + 1) * 512], proj_ps[s % 2][0:R, :],
                                         ACT.Copy).then_inc(proj_hi, 1)

            def exps(g, u):
                act.wait_ge(max_done, done(8, g, u))
                for j in range(HU):
                    ins = nc.scalar.activation(probs[0:R, u % 3, j, :], score_ps[u % 2][0:R, j * R:(j + 1) * R], ACT.Exp,
                                               bias=negmax[0:R, u, j:j + 1],
                                               accum_out=rowsum[0:R, u, j:j + 1])
                ins.then_inc(exp_done, 1)

            def probs_hi(g, u):
                act.wait_ge(pt_ready, done(8, g, u))
                nc.scalar.activation(pt[0:R, u % 2, 0], pt_ps[0:R, 0:HU * R].rearrange("p (h r) -> p h r", h=HU),
                                     ACT.Copy, scale=PS).then_inc(pt_hi, 1)

            def attend_hi(g, w):
                t, half = w // 2, w % 2
                act.wait_ge(pv_ready, done(8, g, 2 * w + 1))
                nc.scalar.activation(ot[:, 0, 4 * half:4 * half + 4, t * R:(t + 1) * R],
                                     o_ps[:, 0:HU * R].rearrange("p (h r) -> p h r", h=HU),
                                     ACT.Copy, scale=1.0 / PS).then_inc(ot_hi, 1)

            def pixels_hi(g, t, part):
                act.wait_ge(front_ready, done(7, g, 2 * t + part))
                nc.scalar.activation(xt[:, t, 0, 3 * part:3 * part + 3, 0:PR],
                                     front_ps[:, 0:3 * PR].rearrange("p (k r) -> p k r", k=3),
                                     ACT.Copy).then_inc(front_hi, 1)

            def rows_hi(g):
                act.wait_ge(front_ready, done(7, g, 6))
                nc.scalar.activation(xnt[:, 0], front_ps[:, 0:KD * N2].rearrange("p (k n) -> p k n", k=KD),
                                     ACT.Copy).then_inc(front_hi, 1)

            def xf_hi(g):
                act.wait_ge(back_ready, done(5, g, 2))
                nc.scalar.activation(xft[:, 0],
                                     back_ps[:, 0:KD * N2].rearrange("p (k n) -> p k n", k=KD),
                                     ACT.Copy).then_inc(back_hi, 1)
                rows = xf_dram[bass.ds(g * N2, N2), :].rearrange("(t r) d -> r t d", t=2)
                act.dma_start(rows, xf[0:R, :, :]).then_inc(xf_stored, 16)

            def shared_tanh(g, j):
                act.wait_ge(sh_ready, done(2, g, j))
                nc.scalar.activation(sh_silu[:, j, :], proj_ps[j][:, 0:N2], ACT.Tanh, bias=shcol[:, 0, j:j + 1],
                                     scale=0.5 / WS).then_inc(sh_tanh, 1)

            def shared_hi(g, j):
                act.wait_ge(sh_gate_done, done(2, g, j))
                nc.scalar.activation(sh_gp[:, j, 0, :], sh_gated[:, j, :], ACT.Copy, scale=0.5 / WS).then_inc(sh_hi, 1)

            def route_exps(turn, t0, n):
                act.wait_ge(route_exp_in, turn)
                nc.scalar.activation(rt(1, t0, n), rt(0, t0, n), ACT.Exp).then_inc(route_exp, 1)

            def body(g, first, last, pairs):
                if not first:
                    probs_hi(g - 1, 6)
                    attend_hi(g - 1, 2)
                project_hi(g, 0)
                project_hi(g, 1)
                if not first:
                    probs_hi(g - 1, 7)
                if pairs:
                    pair_load(g - 1)
                project_hi(g, 2)
                for s in range(3, 6):
                    project_hi(g, s)
                    if s == 3 and not first:
                        attend_hi(g - 1, 3)
                    if first:
                        weights_hi(s + 2)
                if first:
                    nc.scalar.activation(wgate[:, 0], gatest[:, :, :], ACT.Copy, scale=WS).then_inc(w_hi, 1)
                if not last:
                    pixels_hi(g + 1, 0, 0)
                project_hi(g, 6)
                if not last:
                    pixels_hi(g + 1, 0, 1)
                    pixels_hi(g + 1, 1, 0)
                project_hi(g, 7)
                if not last:
                    pixels_hi(g + 1, 1, 1)
                project_hi(g, 8)
                if pairs:
                    pair_high(g - 1)
                exps(g, 0)
                project_hi(g, 9)
                if not first:
                    xf_hi(g - 1)
                exps(g, 1)
                for s in range(2, UNITS):
                    probs_hi(g, s - 2)
                    if s in (5, 6):
                        project_hi(g, 5 + s)
                    if s in (4, 6):
                        attend_hi(g, s // 2 - 2)
                    exps(g, s)
                    if s in (2, 3) and not first:
                        shared_tanh(g - 1, s - 2)
                    if s in (4, 5) and not first:
                        shared_hi(g - 1, s - 4)
                    if s == 6 and not last:
                        rows_hi(g + 1)

            pixels_hi(0, 0, 0)
            weights_hi(0)
            pixels_hi(0, 0, 1)
            pixels_hi(0, 1, 0)
            pixels_hi(0, 1, 1)
            for k in range(1, 5):
                weights_hi(k)
            rows_hi(0)
            body(0, True, False, False)
            with act.Fori(1, G - 2) as g:
                body(g, False, False, True)
            body(G - 2, False, False, False)
            body(G - 1, False, True, False)
            probs_hi(G - 1, 6)
            attend_hi(G - 1, 2)
            probs_hi(G - 1, 7)
            attend_hi(G - 1, 3)
            route_exps(1, 0, EARLY)
            xf_hi(G - 1)
            for j in range(2):
                shared_tanh(G - 1, j)

            route_exps(2, EARLY, TILES - EARLY)
            for j in range(2):
                shared_hi(G - 1, j)

            def row_high(b, i):
                act.wait_ge(row_turned, STEPS * b + i + 1)
                nc.scalar.activation(xrt[:, i % 2, 0, :], score_ps[i % 2][:, 0:D], ACT.Copy).then_inc(row_hi, 1)

            def silus(b, i, ex):
                act.wait_ge(hid_ready, STEPS * b + i + 1)
                nc.scalar.activation(bsilu[:, i % 2, :], proj_ps[i % 2][:, 0:P], ACT.Silu,
                                     bias=b13col[:, 0, bass.ds(ex, 1)], scale=1.0 / WS).then_inc(silu_done, 1)

            def gated_hi(b, i):
                act.wait_ge(gated_done, STEPS * b + i + 1)
                if not (isinstance(b, int) and b == 0 and i < 3):
                    act.wait_ge(y_ready, STEPS * b + i - 2)
                nc.scalar.activation(bgp[:, i % 3, 0, :], bgated[:, i % 3, :], ACT.Copy).then_inc(g_hi, 1)

            def store_rows(b, i):
                act.wait_ge(y_out, STEPS * b + i + 1)
                act.dma_start(y_dram[bass.ds((STEPS * b + i) * P, P), :], yrow[:, i, :]).then_inc(y_stored[i], 16)

            def blocks(b, first):
                ex = experts_of(b, mybir.EngineType.Activation, 2, STEPS)
                for i in range(STEPS):
                    row_high(b, i)
                    if i >= 1 or not first:
                        silus(*behind(b, i, 1), ex[i])
                    if i >= 2 or not first:
                        gated_hi(*behind(b, i, 2))
                    if i >= 4 or not first:
                        store_rows(*behind(b, i, 4))

            act.wait_ge(route, ROUTED)
            blocks(0, True)
            with act.Fori(1, NB // STEPS) as b:
                blocks(b, False)
            end = NB // STEPS
            ex = experts_of(end, mybir.EngineType.Activation, 2, 1)
            gated_hi(*behind(end, 0, 2))
            store_rows(*behind(end, 0, 4))
            silus(*behind(end, 0, 1), ex[0])
            gated_hi(*behind(end, 0, 1))
            for back in (3, 2, 1):
                store_rows(*behind(end, 0, back))

        @block.vector
        def _(dve):
            V = nc.vector
            V.memset(xt[:, :, :, :, PR:R], 0.0)
            V.memset(onerow[:, :], 1.0)
            V.memset(addrow3[:, :], 0.0)
            V.memset(power[:, 0:1], -0.5)
            V.memset(power[:, 1:2], 0.5)
            V.memset(power[:, 2:3], -1.0)
            V.memset(power[:, 3:4], EPS)
            V.memset(power[:, 4:5], float(D) ** 0.5)
            V.memset(blk_expert[:, 0:3], 0)
            V.memset(scrap[:, :], 0.0).then_inc(prep, 1)
            def weights_lo(k):
                dve.wait_ge(w_hi, k + 1)
                for st, hi, lo, scale in pieces[k][1]:
                    s = WS if scale is None else {"g1": g1col, "gam": gamcol}[scale[0]][:, scale[1]:scale[1] + 1]
                    if len(st.shape) > 3:
                        merge = "p a b c -> p (a b c)"
                        st, hi, lo = st.rearrange(merge), hi.rearrange(merge), lo.rearrange(merge)
                    ins = V.scalar_tensor_tensor(lo, st, s, hi, ALU.mult, ALU.subtract)
                ins.then_inc(w_lo, 1)

            def project_lo(g, s):
                dve.wait_ge(proj_hi, done(12, g, s))
                if s < 8:
                    dst = lambda n: qk[:, n, 2 * s:2 * s + 2, :]
                    V.scalar_tensor_tensor(dst(1), proj_ps[s % 2][:, 0:2 * N2].rearrange("p (a n) -> p a n", a=2),
                                           QS if s < 4 else KS, dst(0), ALU.mult, ALU.subtract).then_inc(proj_lo, 1)
                else:
                    t, half = (s - 8) // 2, s % 2
                    cs = slice(half * 512, (half + 1) * 512)
                    V.tensor_tensor(vv[0:R, 1, t, cs], proj_ps[s % 2][0:R, :], vv[0:R, 0, t, cs],
                                    ALU.subtract).then_inc(proj_lo, 1)

            def row_max(g, u):
                dve.wait_ge(scores_ready, done(8, g, u))
                V.tensor_reduce(negmax[0:R, u, :], score_ps[u % 2][0:R, 0:HU * R].rearrange("p (h r) -> p h r", h=HU),
                                AX.X, ALU.max, negate=True).then_inc(max_done, 1)

            def row_inv(g, u):
                dve.wait_ge(exp_done, done(8, g, u))
                V.reciprocal(rinv[0:R, u, :], rowsum[0:R, u, :]).then_inc(rinv_done, 1)

            def probs_lo(g, u):
                dve.wait_ge(pt_hi, done(8, g, u))
                V.scalar_tensor_tensor(pt[0:R, u % 2, 1], pt_ps[0:R, 0:HU * R].rearrange("p (h r) -> p h r", h=HU), PS,
                                       pt[0:R, u % 2, 0], ALU.mult, ALU.subtract).then_inc(pt_lo, 1)

            def attend_lo(g, w):
                t, half = w // 2, w % 2
                dst = lambda n: ot[:, n, 4 * half:4 * half + 4, t * R:(t + 1) * R]
                dve.wait_ge(ot_hi, done(4, g, w))
                V.scalar_tensor_tensor(dst(1), o_ps[:, 0:HU * R].rearrange("p (h r) -> p h r", h=HU), 1.0 / PS,
                                       dst(0), ALU.mult, ALU.subtract).then_inc(ot_lo, 1)

            def pixel_stats(g, t):
                dve.wait_ge(x_in[t], 16 * g + 16)
                V.bn_stats(xst[0:PR, t, 0, :], xin[0:PR, t, 0:PD // 2])
                V.bn_stats(xst[0:PR, t, 1, :], xin[0:PR, t, PD // 2:PD]).then_inc(x_stats, 1)
                dve.wait_ge(x_stats, done(2, g, t))
                V.memset(scrap[:, 0 + t:1 + t], 0.0)
                V.bn_aggr(xmv[0:PR, t, :], xst[0:PR, t, :, :].rearrange("p a b -> p (a b)")).then_inc(x_moments, 1)

            def pixel_norm(g, t):
                dve.wait_ge(x_rstd, g + 1)
                V.tensor_scalar(xin[0:PR, t, :], xin[0:PR, t, :], xmv[0:PR, t, 0:1], xrs[0:PR, t, 1:2],
                                ALU.subtract, ALU.mult).then_inc(xhat_done, 1)

            def pixels_lo(g, t, part):
                dve.wait_ge(front_hi, done(5, g, 2 * t + part))
                dst = lambda n: xt[:, t, n, 3 * part:3 * part + 3, 0:PR]
                V.tensor_tensor(dst(1), front_ps[:, 0:3 * PR].rearrange("p (k r) -> p k r", k=3), dst(0),
                                ALU.subtract).then_inc(front_out, 1)

            def embed_out(g, t):
                dve.wait_ge(front_ready, done(7, g, 4 + t))
                V.scalar_tensor_tensor(ytok[0:R, t, :], front_ps[0:R, 0:D], 1.0 / WS, biasrow[0:R, :],
                                       ALU.mult, ALU.add).then_inc(front_out, 1)
                dve.wait_ge(front_out, done(7, g, 4 + t))
                V.memset(scrap[:, 2 + t:3 + t], 0.0)
                V.bn_stats(yst[0:R, t, :], ytok[0:R, t, :]).then_inc(y_stats, 1)

            def embed_moments(g, t):
                dve.wait_ge(y_stats, done(2, g, t))
                V.memset(scrap[:, 4 + t:5 + t], 0.0)
                V.bn_aggr(ymv[0:R, t, :], yst[0:R, t, :]).then_inc(y_moments, 1)

            def token_rows(g):
                dve.wait_ge(y_rstd, g + 1)
                for t in range(2):
                    V.scalar_tensor_tensor(ytok[0:R, t, :], ytok[0:R, t, :], ymv[0:R, t, 0:1], g2row[0:R, :],
                                           ALU.subtract, ALU.mult).then_inc(y_gain, 1)
                for t in range(2):
                    dve.wait_ge(y_gain, done(2, g, t))
                    V.scalar_tensor_tensor(hrows[0:R, 2 * g + t, :], ytok[0:R, t, :], yrs[0:R, t, 2:3], addrow[0:R, :],
                                           ALU.mult, ALU.add).then_inc(h_done, 1)

            def token_moments(g):
                for t in range(2):
                    dve.wait_ge(h_done, done(2, g, t))
                    V.memset(scrap[:, 6 + t:7 + t], 0.0)
                    V.bn_stats(hst[0:R, t, :], hrows[0:R, 2 * g + t, :]).then_inc(h_stats, 1)
                for t in range(2):
                    dve.wait_ge(h_stats, done(2, g, t))
                    V.memset(scrap[:, 8 + t:9 + t], 0.0)
                    V.bn_aggr(hmv[0:R, t, :], hst[0:R, t, :]).then_inc(h_moments, 1)

            def norm_rows(g, t):
                dve.wait_ge(h_scale, g + 1)
                V.tensor_scalar(xn[0:R, t, :], hrows[0:R, 2 * g + t, :], hmv[0:R, t, 0:1], hrs[0:R, t, 7:8],
                                ALU.subtract, ALU.mult).then_inc(xn_done, 1)

            def rows_lo(g):
                dve.wait_ge(front_hi, done(5, g, 4))
                V.tensor_tensor(xnt[:, 1], front_ps[:, 0:KD * N2].rearrange("p (k n) -> p k n", k=KD), xnt[:, 0],
                                ALU.subtract).then_inc(front_out, 1)

            def residual(g, t):
                h = hrows[0:R, 2 * g + t, :]
                dve.wait_ge(back_ready, done(5, g, t))
                V.scalar_tensor_tensor(h, back_ps[0:R, 0:D], 1.0 / (WS * WS), h, ALU.mult, ALU.add).then_inc(back_out, 1)
                dve.wait_ge(back_out, done(5, g, t))
                V.memset(scrap[:, 10 + t:11 + t], 0.0)
                V.bn_stats(fst[0:R, t, :], h).then_inc(f_stats, 1)
                dve.wait_ge(f_stats, done(2, g, t))
                V.memset(scrap[:, 12 + t:13 + t], 0.0)
                V.bn_aggr(fmv[0:R, t, :], fst[0:R, t, :]).then_inc(f_moments, 1)

            def norm_xf(g, t):
                dve.wait_ge(f_rstd, g + 1)
                if t == 0 and not (isinstance(g, int) and g == 0):
                    dve.wait_ge(xf_stored, 16 * g)
                V.tensor_scalar(xf[0:R, t, :], hrows[0:R, 2 * g + t, :], fmv[0:R, t, 0:1], frs[0:R, t, 1:2],
                                ALU.subtract, ALU.mult).then_inc(xf_done, 1)

            def xf_lo(g):
                dve.wait_ge(back_hi, g + 1)
                V.tensor_tensor(xft[:, 1], back_ps[:, 0:KD * N2].rearrange("p (k n) -> p k n", k=KD),
                                xft[:, 0], ALU.subtract).then_inc(back_out, 1)

            def gate_out(g):
                dve.wait_ge(back_ready, done(5, g, 3))
                V.tensor_scalar(logits[0:R, bass.ds(2 * g, 2), :], back_ps[0:R, 0:2 * E].rearrange("p (t e) -> p t e", t=2),
                                1.0 / WS, None, ALU.mult).then_inc(back_out, 1)

            def shared_gate(g, j):
                step = 2 * (done(2, g, j) - 1)
                dve.wait_ge(sh_tanh, done(2, g, j))
                V.tensor_scalar(sh_silu[:, j, :], sh_silu[:, j, :], 1.0, None, ALU.add).then_inc(sh_step, 1)
                dve.wait_ge(sh_step, step + 1)
                V.scalar_tensor_tensor(sh_silu[:, j, :], proj_ps[j][:, 0:N2], shcol[:, 1, j:j + 1], sh_silu[:, j, :],
                                       ALU.add, ALU.mult).then_inc(sh_step, 1)
                dve.wait_ge(sh_step, step + 2)
                V.scalar_tensor_tensor(sh_gated[:, j, :], proj_ps[j][:, N2:2 * N2], b13col[:, 1, E + j:E + j + 1],
                                       sh_silu[:, j, :], ALU.add, ALU.mult).then_inc(sh_gate_done, 1)

            def shared_lo(g, j):
                dve.wait_ge(sh_hi, done(2, g, j))
                V.scalar_tensor_tensor(sh_gp[:, j, 1, :], sh_gated[:, j, :], 0.5 / WS, sh_gp[:, j, 0, :],
                                       ALU.mult, ALU.subtract).then_inc(sh_lo, 1)

            def shared_add(g):
                rows = hrows[0:R, bass.ds(2 * g, 2), :]
                dve.wait_ge(bs2_added, g + 1)
                dve.wait_ge(back_ready, done(5, g, 4))
                V.scalar_tensor_tensor(rows, back_ps[0:R, 0:2 * D].rearrange("p (t d) -> p t d", t=2),
                                       1.0 / (WS * WS), rows, ALU.mult, ALU.add).then_inc(back_out, 1)

            step = [0]

            def then(ins):
                step[0] += 1
                ins.then_inc(route, 1)
                dve.wait_ge(route, step[0])

            def wide(v, n):
                return v.unsqueeze(2).to_broadcast([R, n, E])

            def per_row(k, t0, n):
                return sc8[0:R, k, t0:t0 + n]

            def route_softmax_in(t0, n):
                lg = logits[0:R, t0:t0 + n, :]
                then(V.tensor_reduce(per_row(0, t0, n), lg, AX.X, ALU.max))
                V.tensor_tensor(rt(0, t0, n), lg, wide(per_row(0, t0, n), n), ALU.subtract).then_inc(route_exp_in, 1)

            def route_softmax_out(turn, t0, n):
                dve.wait_ge(route_exp, turn)
                then(V.tensor_reduce(per_row(1, t0, n), rt(1, t0, n), AX.X, ALU.add))
                then(V.reciprocal(per_row(2, t0, n), per_row(1, t0, n)))
                then(V.tensor_tensor(rt(1, t0, n), rt(1, t0, n), wide(per_row(2, t0, n), n), ALU.mult))
                gb = gbrow[0:R, :].unsqueeze(1).to_broadcast([R, n, E])
                then(V.tensor_tensor(rt(2, t0, n), rt(1, t0, n), gb, ALU.add))

            def route_group_scores(t0, n):
                sg = rt(2, t0, n).rearrange("p t (g e) -> p t g e", g=4)
                r = [rg(k, t0, n) for k in range(7)]
                V.tensor_tensor(r[0], sg[:, :, :, 0], sg[:, :, :, 1], ALU.max)
                V.tensor_tensor(r[1], sg[:, :, :, 0], sg[:, :, :, 1], ALU.min)
                V.tensor_tensor(r[2], sg[:, :, :, 2], sg[:, :, :, 3], ALU.max)
                then(V.tensor_tensor(r[3], sg[:, :, :, 2], sg[:, :, :, 3], ALU.min))
                V.tensor_tensor(r[4], r[0], r[2], ALU.max)
                V.tensor_tensor(r[5], r[0], r[2], ALU.min)
                then(V.tensor_tensor(r[6], r[1], r[3], ALU.max))
                then(V.tensor_tensor(r[5], r[5], r[6], ALU.max))
                then(V.tensor_tensor(r[0], r[4], r[5], ALU.add))

            def route_group_ranks(t0, n):
                r = [rg(k, t0, n) for k in range(3)]
                then(V.tensor_copy(r[1], small[0:R, 17:21].unsqueeze(1).to_broadcast([R, n, 4])))
                for d in range(1, 4):
                    won = r[2][:, :, 0:4 - d]
                    then(V.tensor_tensor(won, r[0][:, :, 0:4 - d], r[0][:, :, d:4], ALU.is_ge))
                    then(V.tensor_tensor(r[1][:, :, d:4], r[1][:, :, d:4], won, ALU.add))
                    then(V.tensor_tensor(r[1][:, :, 0:4 - d], r[1][:, :, 0:4 - d], won, ALU.subtract))

            def route_keep(t0, n):
                then(V.tensor_scalar(rg(3, t0, n), rg(1, t0, n), 2.0, None, ALU.is_lt))
                then(V.tensor_scalar(rg(4, t0, n), rg(3, t0, n), 1.0, OUT, ALU.subtract, ALU.mult))
                keep, pen = (rg(k, t0, n).unsqueeze(3).to_broadcast([R, n, 4, 4]) for k in (3, 4))
                s2, s3 = (rt(k, t0, n).rearrange("p t (g e) -> p t g e", g=4) for k in (2, 3))
                then(V.tensor_tensor(s3, s2, keep, ALU.mult))
                then(V.tensor_tensor(s3, s3, pen, ALU.add))

            def route_choose(c, t0, n):
                iota = small[0:R, 1:17].unsqueeze(1).to_broadcast([R, n, E])
                best, number = per_row(3 + 2 * c, t0, n), per_row(4 + 2 * c, t0, n)
                r3, r4, r5, pick = (rt(k, t0, n) for k in (3, 4, 5, 6 + c))
                then(V.tensor_reduce(best, r3, AX.X, ALU.max))
                then(V.tensor_tensor(r4, r3, wide(best, n), ALU.is_equal))
                then(V.scalar_tensor_tensor(r5, r4, -float(E), iota, ALU.mult, ALU.add))
                then(V.tensor_reduce(number, r5, AX.X, ALU.min))
                then(V.tensor_tensor(pick, r5, wide(number, n), ALU.is_equal))
                then(V.scalar_tensor_tensor(r3, pick, -3.0 * OUT, r3, ALU.mult, ALU.add))

            def route_chosen(t0, n):
                then(V.tensor_tensor(chosen[0:R, t0 * E:(t0 + n) * E].rearrange("p (t e) -> p t e", t=n),
                                     rt(6, t0, n), rt(7, t0, n), ALU.add))

            def body(g, first, last, pairs):
                if not first:
                    row_inv(g - 1, 7)
                    probs_lo(g - 1, 6)
                    attend_lo(g - 1, 2)
                project_lo(g, 0)
                project_lo(g, 1)
                if not first:
                    probs_lo(g - 1, 7)
                if not last:
                    pixel_stats(g + 1, 0)
                project_lo(g, 2)
                project_lo(g, 3)
                if not first:
                    attend_lo(g - 1, 3)
                if first:
                    weights_lo(5)
                if not last:
                    pixel_stats(g + 1, 1)
                project_lo(g, 4)
                if first:
                    weights_lo(6)
                if not last:
                    pixel_norm(g + 1, 0)
                project_lo(g, 5)
                if first:
                    weights_lo(7)
                    dve.wait_ge(w_hi, len(pieces) + 1)
                    V.scalar_tensor_tensor(wgate[:, 1], gatest[:, :, :], WS, wgate[:, 0], ALU.mult,
                                           ALU.subtract).then_inc(prep, 1)
                if not last:
                    pixel_norm(g + 1, 1)
                if not last:
                    pixels_lo(g + 1, 0, 0)
                if not first:
                    residual(g - 1, 0)
                project_lo(g, 6)
                if not last:
                    pixels_lo(g + 1, 0, 1)
                if not last:
                    pixels_lo(g + 1, 1, 0)
                if not first:
                    residual(g - 1, 1)
                project_lo(g, 7)
                if not last:
                    pixels_lo(g + 1, 1, 1)
                if not first:
                    norm_xf(g - 1, 0)
                    norm_xf(g - 1, 1)
                project_lo(g, 8)
                row_max(g, 0)
                if not last:
                    embed_out(g + 1, 0)
                    embed_moments(g + 1, 0)
                row_inv(g, 0)
                project_lo(g, 9)
                if not first:
                    xf_lo(g - 1)
                row_max(g, 1)
                if not last:
                    embed_out(g + 1, 1)
                    embed_moments(g + 1, 1)
                for s in range(2, UNITS):
                    row_inv(g, s - 1)
                    row_max(g, s)
                    probs_lo(g, s - 2)
                    if s in (4, 6):
                        attend_lo(g, s // 2 - 2)
                    if s == 6:
                        project_lo(g, 11)
                    if s == 2:
                        if not first:
                            gate_out(g - 1)
                        if not last:
                            token_rows(g + 1)
                    if s in (3, 4) and not first:
                        shared_gate(g - 1, s - 3)
                    if s == 3 and not last:
                        token_moments(g + 1)
                    if s == 5:
                        project_lo(g, 10)
                        if not last:
                            for t in range(2):
                                norm_rows(g + 1, t)
                    if s in (5, 6) and not first:
                        shared_lo(g - 1, s - 5)
                    if s == 6 and not last:
                        rows_lo(g + 1)
                    if s == 7 and not first:
                        shared_add(g - 1)

            for t in range(2):
                pixel_stats(0, t)
            for t in range(2):
                pixel_norm(0, t)
            dve.wait_ge(const_in, 16 * NCONST)
            V.tensor_scalar(gamcol[:, :], gamcol[:, :], 1.0, WS, ALU.add, ALU.mult).then_inc(prep, 1)
            V.tensor_scalar(g1col[:, :], g1col[:, :], WS, None, ALU.mult).then_inc(prep, 1)
            V.tensor_copy(b1wide[:, :, :], b1col[:, :].unsqueeze(2).to_broadcast([P, KP, R])).then_inc(prep, 1)
            V.tensor_scalar(b13col[:, 1, :], b13col[:, 1, :], WS, None, ALU.mult).then_inc(prep, 1)
            V.tensor_tensor(addrow[0:R, :], addrow[0:R, :], addrow2[0:R, :], ALU.add).then_inc(prep, 1)
            dve.wait_ge(prep, 6)
            V.tensor_tensor(addrow[0:R, :], addrow[0:R, :], addrow3[0:R, :], ALU.add).then_inc(prep, 1)
            V.tensor_scalar(shcol[:, 0, :], b13col[:, 0, E:NE], 0.5, None, ALU.mult)
            V.tensor_scalar(shcol[:, 1, :], b13col[:, 0, E:NE], WS, None, ALU.mult).then_inc(prep, 1)
            pixels_lo(0, 0, 0)
            pixels_lo(0, 0, 1)
            weights_lo(0)
            pixels_lo(0, 1, 0)
            pixels_lo(0, 1, 1)
            weights_lo(1)
            dve.wait_ge(bias_mm, 1)
            V.tensor_copy(biasrow[0:R, :], back_ps[0:R, 0:D]).then_inc(prep, 1)
            dve.wait_ge(prep, PREP)
            for t in range(2):
                embed_out(0, t)
                embed_moments(0, t)
            weights_lo(2)
            token_rows(0)
            token_moments(0)
            weights_lo(3)
            for t in range(2):
                norm_rows(0, t)
            weights_lo(4)
            rows_lo(0)
            body(0, True, False, False)
            dve.wait_ge(w_lo, len(pieces))
            with dve.Fori(1, G - 2) as g:
                body(g, False, False, True)
            body(G - 2, False, False, False)
            body(G - 1, False, True, False)
            row_inv(G - 1, 7)
            probs_lo(G - 1, 6)
            attend_lo(G - 1, 2)
            probs_lo(G - 1, 7)
            attend_lo(G - 1, 3)
            early = (0, EARLY)
            dve.wait_ge(back_out, 5 * (G - 1))
            dve.wait_ge(pair_lo, E // 2)
            route_softmax_in(*early)
            residual(G - 1, 0)
            route_softmax_out(1, *early)
            route_group_scores(*early)
            residual(G - 1, 1)
            route_group_ranks(*early)
            for t in range(2):
                norm_xf(G - 1, t)
            route_keep(*early)
            xf_lo(G - 1)
            route_choose(0, *early)
            gate_out(G - 1)
            route_choose(1, *early)
            route_chosen(*early)
            assert step[0] == CHOSEN_EARLY, step[0]
            dve.wait_ge(back_out, 5 * G - 1)
            late = (EARLY, TILES - EARLY)
            route_softmax_in(*late)
            route_softmax_out(2, *late)
            route_group_scores(*late)
            route_group_ranks(*late)
            route_keep(*late)
            route_choose(0, *late)
            route_choose(1, *late)
            route_chosen(*late)
            assert step[0] == CHOSEN, step[0]
            for j in range(2):
                shared_gate(G - 1, j)

            def over(v, n):
                return v.unsqueeze(2).to_broadcast([R, T2, n])

            def both(v):
                return v.unsqueeze(1).to_broadcast([R, 2, TILES, E])

            picks4 = picks.rearrange("p (c t) e -> p c t e", c=2)
            prod4 = prod.rearrange("p (c t) e -> p c t e", c=2)
            then(V.tensor_tensor(prod4, picks4, both(rt(1)), ALU.mult))
            then(V.tensor_reduce(weights[0:R, :, :].rearrange("p c t -> p (c t)"), prod, AX.X, ALU.add))
            for j in range(2):
                shared_lo(G - 1, j)
            blocks_e, first_e, end_e = (per_e[0:R, k, :] for k in range(3))
            dve.wait_ge(rank_ready, 1)
            rank_all = score_ps[0][0:R, 0:TE].rearrange("p (t e) -> p t e", t=TILES)
            cmp = prod.rearrange("p j e -> p (j e)")
            cmp_k = cmp[:, 0:E * KMAX].rearrange("p (e k) -> p e k", e=E)
            then(V.tensor_tensor(cmp_k, score_ps[1][0:R, 0:E].unsqueeze(2).to_broadcast([R, E, KMAX]),
                                 full.unsqueeze(1).to_broadcast([R, E, KMAX]), ALU.is_gt))
            then(V.tensor_reduce(blocks_e, cmp_k, AX.X, ALU.add))
            cmp_e = cmp[:, 0:E * E].rearrange("p (e k) -> p e k", e=E)
            then(V.tensor_tensor(cmp_e, before, blocks_e.unsqueeze(1).to_broadcast([R, E, E]), ALU.mult))
            then(V.tensor_reduce(first_e, cmp_e, AX.X, ALU.add))
            then(V.tensor_tensor(end_e, first_e, blocks_e, ALU.add))
            first_of, rank_of, full_of, block_of, place_of, slot_of = (place[0:R, k, :] for k in range(6))
            then(V.tensor_tensor(prod, picks, first_e.unsqueeze(1).to_broadcast([R, T2, E]), ALU.mult))
            then(V.tensor_reduce(first_of, prod, AX.X, ALU.add))
            then(V.tensor_tensor(prod4, picks4, both(rank_all), ALU.mult))
            then(V.tensor_reduce(rank_of, prod, AX.X, ALU.add))
            then(V.tensor_tensor(past, over(rank_of, KMAX - 1), full[:, 1:KMAX].unsqueeze(1).to_broadcast([R, T2, KMAX - 1]),
                                 ALU.is_ge))
            then(V.tensor_reduce(full_of, past, AX.X, ALU.add))
            V.tensor_tensor(block_of, first_of, full_of, ALU.add)
            then(V.scalar_tensor_tensor(place_of, full_of, -float(P), rank_of, ALU.mult, ALU.add))
            then(V.scalar_tensor_tensor(slot_of, block_of, float(P), place_of, ALU.mult, ALU.add))
            V.tensor_copy(slots[0:R, :, :], slot_of.rearrange("p (c t) -> p t c", c=2))
            V.tensor_tensor(hot_s, over(place_of, P), iota_s.unsqueeze(1).to_broadcast([R, T2, P]), ALU.is_equal)
            then(V.tensor_tensor(hot_b, over(block_of, NB), iota_b.unsqueeze(1).to_broadcast([R, T2, NB]), ALU.is_equal))
            shared_add(G - 1)
            hot_b4 = hot_b.rearrange("p (c t) b -> p c t b", c=2)
            for c in range(2):
                ins = V.tensor_tensor(hot_b4[:, c], hot_b4[:, c], rowid.unsqueeze(2).to_broadcast([R, TILES, NB]), ALU.mult)
            then(ins)
            assert step[0] == PLACED, step[0]
            cmp_b = qkf[0:R, 0:NB * E].rearrange("p (b e) -> p b e", b=NB)
            then(V.tensor_tensor(cmp_b, iota_b.unsqueeze(2).to_broadcast([R, NB, E]),
                                 end_e.unsqueeze(1).to_broadcast([R, NB, E]), ALU.is_ge))
            then(V.tensor_reduce(qkf[0:R, NB * E:NB * E + NB], cmp_b, AX.X, ALU.add))
            then(V.tensor_scalar(blk_expert[0:1, 3:3 + NB], qkf[0:1, NB * E:NB * E + NB], float(E - 1), None, ALU.min))
            dve.wait_ge(ids_ready, 1)
            then(V.tensor_scalar(ids[:, :], pt_ps[:, 0:NB], float(MID), None, ALU.add))
            assert step[0] == ROUTED, step[0]

            def row_low(b, i):
                dve.wait_ge(row_hi, STEPS * b + i + 1)
                V.tensor_tensor(xrt[:, i % 2, 1, :], score_ps[i % 2][:, 0:D], xrt[:, i % 2, 0, :],
                                ALU.subtract).then_inc(row_lo, 1)

            def gate_up(b, i, ex):
                dve.wait_ge(silu_done, STEPS * b + i + 1)
                if not (isinstance(b, int) and b == 0 and i < 3):
                    dve.wait_ge(g_lo, STEPS * b + i - 2)
                V.scalar_tensor_tensor(bgated[:, i % 3, :], proj_ps[i % 2][:, P:2 * P], b13col[:, 1, bass.ds(ex, 1)],
                                       bsilu[:, i % 2, :], ALU.add, ALU.mult).then_inc(gated_done, 1)

            def gated_lo(b, i):
                dve.wait_ge(g_hi, STEPS * b + i + 1)
                V.tensor_tensor(bgp[:, i % 3, 1, :], bgated[:, i % 3, :], bgp[:, i % 3, 0, :],
                                ALU.subtract).then_inc(g_lo, 1)

            def rows_out(b, i, ex):
                dve.wait_ge(y_ready, STEPS * b + i + 1)
                if not (isinstance(b, int) and b == 0):
                    dve.wait_ge(y_stored[i], 16 * b)
                V.scalar_tensor_tensor(yrow[:, i, :], (front_ps, back_ps)[i % 2][:, 0:D], 1.0 / (WS * WS),
                                       be2[:, bass.ds(ex, 1), :].rearrange("p a d -> p (a d)"),
                                       ALU.mult, ALU.add).then_inc(y_out, 1)

            def blocks(b, first):
                ex = experts_of(b, mybir.EngineType.DVE, 0, STEPS + 2)
                for i in range(STEPS):
                    row_low(b, i)
                    if i >= 1 or not first:
                        gate_up(*behind(b, i, 1), ex[i + 2])
                    if i >= 2 or not first:
                        gated_lo(*behind(b, i, 2))
                    if i >= 3 or not first:
                        rows_out(*behind(b, i, 3), ex[i])

            dve.wait_ge(be2_in, 16)
            blocks(0, True)
            with dve.Fori(1, NB // STEPS) as b:
                blocks(b, False)
            end = NB // STEPS
            ex = experts_of(end, mybir.EngineType.DVE, 0, 3)
            gated_lo(*behind(end, 0, 2))
            rows_out(*behind(end, 0, 3), ex[0])
            gate_up(*behind(end, 0, 1), ex[2])
            gated_lo(*behind(end, 0, 1))
            for back in (2, 1):
                rows_out(*behind(end, 0, back), ex[3 - back])

            def combine(g, half):
                for c in range(2):
                    if c == 1:
                        dve.wait_ge(summed, 2 * g + 1)
                    for t in range(2):
                        k = 4 * half + 2 * t + c
                        dve.wait_ge(pick_in[k], 8 * (g + 2 - half))
                        h = hrows[0:R, 2 * g + t, :]
                        ins = V.scalar_tensor_tensor(h, ypick[0:R, k, :], weights[0:R, c, bass.ds(2 * g + t, 1)], h,
                                                     ALU.mult, ALU.add)
                    ins.then_inc(summed, 1)
                dve.wait_ge(summed, 2 * g + 2)
                V.memset(scrap[:, 14:15], 0.0).then_inc(rows_final, 1)

            combine(0, 0)
            with dve.Fori(0, G // 2) as n:
                combine(2 * n + 1, 1)
                combine(2 * n + 2, 0)

        @block.gpsimd
        def _(pool):
            Q = nc.gpsimd

            def hold(n):
                Q.tensor_tensor(held[:, n:n + 1], power[:, 3:4], power[:, 3:4], ALU.mult)

            def normalise(g, u):
                pool.wait_ge(rinv_done, done(8, g, u))
                Q.tensor_tensor(probs[0:R, u % 3], probs[0:R, u % 3], rinv[0:R, u, :].unsqueeze(2).to_broadcast([R, HU, R]),
                                ALU.mult).then_inc(probs_ready, 1)

            def pw(n, k):
                return power[0:n, k:k + 1].to_broadcast([n, 2])


            def pixel_rstd(g):
                pool.wait_ge(x_moments, done(2, g, 1))
                Q.tensor_tensor(xrs[0:PR, :, 0], xmv[0:PR, :, 1], pw(PR, 3), ALU.add).then_inc(px, 1)
                pool.wait_ge(px, g + 1)
                Q.tensor_tensor(xrs[0:PR, :, 1], xrs[0:PR, :, 0], pw(PR, 0), ALU.pow).then_inc(x_rstd, 1)

            def token_rstd(g):
                pool.wait_ge(y_moments, done(2, g, 1))
                Q.tensor_tensor(yrs[0:R, :, 0], ymv[0:R, :, 1], pw(R, 3), ALU.add).then_inc(py, 1)
                pool.wait_ge(py, 2 * g + 1)
                Q.tensor_tensor(yrs[0:R, :, 1], yrs[0:R, :, 0], pw(R, 0), ALU.pow).then_inc(py, 1)
                pool.wait_ge(py, 2 * g + 2)
                Q.tensor_tensor(yrs[0:R, :, 2], yrs[0:R, :, 1], small[0:R, 0:1].to_broadcast([R, 2]), ALU.mult).then_inc(y_rstd, 1)

            def row_scale(g):
                pool.wait_ge(h_moments, done(2, g, 1))
                s = [hrs[0:R, :, k] for k in range(8)]
                var = hmv[0:R, :, 1]
                Q.tensor_tensor(s[0], var, pw(R, 3), ALU.add)
                Q.tensor_tensor(s[2], var, pw(R, 1), ALU.pow).then_inc(ph, 1)
                pool.wait_ge(ph, 5 * g + 1)
                Q.tensor_tensor(s[1], s[0], pw(R, 0), ALU.pow).then_inc(ph, 1)
                pool.wait_ge(ph, 5 * g + 2)
                Q.tensor_tensor(s[3], s[2], s[1], ALU.mult).then_inc(ph, 1)
                pool.wait_ge(ph, 5 * g + 3)
                Q.tensor_tensor(s[6], s[1], pw(R, 4), ALU.mult)
                Q.tensor_scalar(s[4], s[3], float(D) ** 0.5, 1e-12, ALU.mult, ALU.max).then_inc(ph, 1)
                pool.wait_ge(ph, 5 * g + 4)
                Q.tensor_tensor(s[5], s[4], pw(R, 2), ALU.pow).then_inc(ph, 1)
                pool.wait_ge(ph, 5 * g + 5)
                Q.tensor_tensor(s[7], s[6], s[5], ALU.mult).then_inc(h_scale, 1)

            def last_rstd(g):
                pool.wait_ge(f_moments, done(2, g, 1))
                Q.tensor_tensor(frs[0:R, :, 0], fmv[0:R, :, 1], pw(R, 3), ALU.add).then_inc(pf, 1)
                pool.wait_ge(pf, g + 1)
                Q.tensor_tensor(frs[0:R, :, 1], frs[0:R, :, 0], pw(R, 0), ALU.pow).then_inc(f_rstd, 1)

            def add_bs2(g):
                pool.wait_ge(xf_done, done(2, g, 1))
                hold(12)
                rows = hrows[0:R, bass.ds(2 * g, 2), :]
                Q.tensor_tensor(rows, rows, bs2row[0:R, :].unsqueeze(1).to_broadcast([R, 2, D]), ALU.add).then_inc(bs2_added, 1)

            def pair_scale(p):
                pool.wait_ge(pair_in, 48 * (p + 1))
                hold(11)
                Q.tensor_scalar(pair[:, :], pair[:, :], WS, None, ALU.mult).then_inc(pair_scaled, 1)

            def pair_low(p):
                pool.wait_ge(pair_hi, p + 1)
                hold(10)
                es = bass.ds(2 * p, 2)
                flat3 = lambda v: v.rearrange("p a b c -> p (a b c)")
                Q.tensor_tensor(flat3(w13[:, 1, es]), flat3(pair13), flat3(w13[:, 0, es]), ALU.subtract)
                Q.tensor_tensor(w2[:, 1, es, :], pair2, w2[:, 0, es, :], ALU.subtract).then_inc(pair_lo, 1)

            def body(g, first, last, pairs):
                if not first:
                    normalise(g - 1, 7)
                if not last:
                    pixel_rstd(g + 1)
                if pairs:
                    pair_scale(g - 1)
                if not first:
                    last_rstd(g - 1)
                if pairs:
                    pair_low(g - 1)
                for u in range(UNITS - 1):
                    normalise(g, u)
                    if u == 0:
                        if not first:
                            add_bs2(g - 1)
                        if not last:
                            token_rstd(g + 1)
                    if u == 3 and not last:
                        row_scale(g + 1)

            pool.wait_ge(prep, 1)
            pixel_rstd(0)
            pool.wait_ge(prep, 7)
            token_rstd(0)
            row_scale(0)
            body(0, True, False, False)
            with pool.Fori(1, G - 2) as g:
                body(g, False, False, True)
            body(G - 2, False, False, False)
            body(G - 1, False, True, False)
            normalise(G - 1, 7)
            last_rstd(G - 1)
            add_bs2(G - 1)

            def fetch(b, half, first):
                if not first:
                    pool.wait_ge(row_turned, STEPS * (b - 1) + 1)
                    hold(0)
                now = ids_now[:, half * STEPS:(half + 1) * STEPS]
                Q.tensor_copy(now, ids[:, bass.ds(STEPS * b, STEPS)]).then_inc(ids_copied, 1)
                pool.wait_ge(ids_copied, b + 1)
                hold(1)
                for i in range(STEPS):
                    if i > 0 and not first:
                        pool.wait_ge(row_turned, STEPS * (b - 1) + i + 1)
                        hold(3 + i)
                    Q.indirect_dma_start(xrow[:, i, :], None, xf_dram,
                                         bass.IndirectOffsetOnAxis(now[:, i:i + 1], 0)).then_inc(row_in[i], 16)

            pool.wait_ge(xf_stored, 16 * G)
            pool.wait_ge(route, ROUTED)
            fetch(0, 0, True)
            with pool.Fori(0, NB // STEPS // 2) as n:
                fetch(2 * n + 1, 1, False)
                fetch(2 * n + 2, 0, False)

            def pick(g, half, first):
                if not first:
                    pool.wait_ge(summed, 2 * g - 2)
                    hold(2)
                Q.tensor_copy(slots_now[0:R, 4 * half:4 * half + 4],
                              slots[0:R, bass.ds(2 * g, 2), :].rearrange("p t c -> p (t c)")).then_inc(slots_copied, 1)
                pool.wait_ge(slots_copied, g + 1)
                hold(0)
                for c in range(2):
                    for t in range(2):
                        k = 4 * half + 2 * t + c
                        Q.indirect_dma_start(ypick[0:R, k, :], None, y_dram,
                                             bass.IndirectOffsetOnAxis(slots_now[0:R, k:k + 1], 0)).then_inc(pick_in[k], 16)

            for k in range(STEPS):
                pool.wait_ge(y_stored[k], 16 * (NB // STEPS))
            pick(0, 0, True)
            pick(1, 1, True)
            pick(2, 0, False)
            with pool.Fori(1, G // 2) as n:
                pick(2 * n + 1, 1, False)
                pick(2 * n + 2, 0, False)


_INS = ['x', 'L0_tok_cls_token', 'L0_tok_cls_pos_embedding', 'L0_tok_ln1_g', 'L0_tok_ln1_b', 'L0_tok_W', 'L0_tok_bias',
        'L0_tok_ln2_g', 'L0_tok_ln2_b', 'L0_attn_gamma', 'L0_attn_w_qkv', 'L0_attn_w_out', 'L0_ffn_gate_w', 'L0_ffn_gate_b',
        'L0_ffn_We1', 'L0_ffn_be1', 'L0_ffn_We2', 'L0_ffn_be2', 'L0_ffn_We3', 'L0_ffn_be3', 'L0_ffn_ws1', 'L0_ffn_bs1',
        'L0_ffn_ws2', 'L0_ffn_bs2', 'L0_ffn_ws3', 'L0_ffn_bs3']


def kernel(**inputs):
    import numpy as _np
    import concourse.bacc as _bacc
    from concourse import mybir as _mybir
    from concourse.bass_utils import run_bass_kernel_spmd as _run

    nc = _bacc.Bacc("TRN2", target_bir_lowering=False, num_devices=1)
    arrays, args = {}, {}
    laid = {n: lay_out(n, _np.asarray(inputs[n])) for n in _INS}
    columns = _np.concatenate([laid.pop(n) for n in COLUMNS], axis=1)
    for name, v in list(laid.items()) + [("columns", columns)] + list(constants().items()):
        arrays[f"in_{name}_dram"] = v
        args[name] = nc.dram_tensor(f"in_{name}_dram", v.shape, _mybir.dt.from_np(v.dtype), kind="ExternalInput").ap()
    out = nc.dram_tensor("out_0_dram", (B, SEQ, D), _mybir.dt.float32, kind="ExternalOutput").ap()
    build(nc, args, out)
    r = _run(nc, [arrays], core_ids=[0])
    return r.results[0]["out_0_dram"]
```
